# Optimizing a Trainium2 kernel written in Bass

```python
import numpy as np
import jax
import jax.numpy as jnp

def _softmax(x, axis=-1):
    return jax.nn.softmax(x, axis=axis)

def _gelu(x):
    return jax.nn.gelu(x, approximate=True)

def _silu(x):
    return jax.nn.silu(x)

def _sigmoid(x):
    return jax.nn.sigmoid(x)

def _layernorm(x, axis=-1, eps=1e-05):
    m = jnp.mean(x, axis=axis, keepdims=True)
    v = jnp.var(x, axis=axis, keepdims=True)
    return (x - m) / jnp.sqrt(v + eps)

def _scatter_add(tgt, idx, src, axis=0):
    return tgt.at[idx].add(src)

def _segment_sum(src, seg, n):
    return jax.ops.segment_sum(src, seg, n)
kernel_name = 'mk_hybrid_d1_jaxref_r8_42939f'

def setup_inputs(seed: int=0):
    np.random.seed(seed)
    _w = jnp.asarray

    def _L0_attn_a_setup():
        import jax, jax.numpy as jnp
        import numpy as np
        import math
        B, T, D_IN, D_OUT = (2, 256, 512, 512)
        N_HEADS, N_KV = (32, 8)
        HEAD_DIM = D_OUT // N_HEADS
        GROUP_SIZE = N_HEADS // N_KV
        ROPE_BASE = 500000.0
        CTX = 256

        def _rope_tables(head_dim, base, seq_len):
            inv_freq = 1.0 / base ** (jnp.arange(0, head_dim, 2, dtype=jnp.float32) / head_dim)
            t = jnp.arange(seq_len, dtype=jnp.float32)
            freqs = jnp.einsum('i,j->ij', t, inv_freq)
            return (jnp.cos(freqs), jnp.sin(freqs))

        def _apply_rope(x, cos, sin):
            x1, x2 = jnp.split(x, 2, axis=-1)
            c = cos[None, None]
            s = sin[None, None]
            return jnp.concatenate([x1 * c - x2 * s, x1 * s + x2 * c], axis=-1)
        key = jax.random.key(seed)
        ks = jax.random.split(key, 5)
        scale = 0.02
        return {'x': jax.random.normal(ks[0], (B, T, D_IN), dtype=jnp.float32), 'Wq': jax.random.normal(ks[1], (D_IN, D_OUT), dtype=jnp.float32) * scale, 'Wk': jax.random.normal(ks[2], (D_IN, N_KV * HEAD_DIM), dtype=jnp.float32) * scale, 'Wv': jax.random.normal(ks[3], (D_IN, N_KV * HEAD_DIM), dtype=jnp.float32) * scale, 'Wo': jax.random.normal(ks[4], (D_OUT, D_OUT), dtype=jnp.float32) * scale}
    _L0_attn_a_in = _L0_attn_a_setup()

    def _L0_attn_b_setup():
        import jax, jax.numpy as jnp
        import numpy as np
        import math
        B, L, D, H = (32, 64, 512, 32)
        HD = D // H
        key = jax.random.key(seed)
        ks = jax.random.split(key, 9)
        s = 1.0 / math.sqrt(D)
        return {'x': jax.random.normal(ks[0], (B, L, D), jnp.float32), 'Wq': jax.random.normal(ks[1], (D, D), jnp.float32) * s, 'bq': jax.random.normal(ks[2], (D,), jnp.float32) * s, 'Wk': jax.random.normal(ks[3], (D, D), jnp.float32) * s, 'bk': jax.random.normal(ks[4], (D,), jnp.float32) * s, 'Wv': jax.random.normal(ks[5], (D, D), jnp.float32) * s, 'bv': jax.random.normal(ks[6], (D,), jnp.float32) * s, 'Wo': jax.random.normal(ks[7], (D, D), jnp.float32) * s, 'bo': jax.random.normal(ks[8], (D,), jnp.float32) * s}
    _L0_attn_b_in = _L0_attn_b_setup()

    def _L0_ffn_setup():
        import jax, jax.numpy as jnp
        import numpy as np
        H = 512
        I = 1376
        R = 32
        NLEV = 16
        Q_ZERO = 7.5
        Q_STEP = 0.005
        LR_SCALE = 0.02

        def _qlinear(x, q, scale, A, Bm):
            w = (q.astype(jnp.float32) - Q_ZERO) * (scale * Q_STEP)[:, None]
            y = jnp.einsum('bsh,oh->bso', x, w)
            return y + LR_SCALE * (x @ A @ Bm)
        key = jax.random.key(seed)
        ks = jax.random.split(key, 13)
        B, S = (2, 256)
        inp = {'x': jax.random.normal(ks[0], (B, S, H), jnp.float32), 'gate_q': jax.random.randint(ks[1], (I, H), 0, NLEV, jnp.int32), 'gate_scale': jax.random.uniform(ks[2], (I,), jnp.float32), 'gate_A': jax.random.normal(ks[3], (H, R), jnp.float32), 'gate_B': jax.random.normal(ks[4], (R, I), jnp.float32), 'up_q': jax.random.randint(ks[5], (I, H), 0, NLEV, jnp.int32), 'up_scale': jax.random.uniform(ks[6], (I,), jnp.float32), 'up_A': jax.random.normal(ks[7], (H, R), jnp.float32), 'up_B': jax.random.normal(ks[8], (R, I), jnp.float32), 'down_q': jax.random.randint(ks[9], (H, I), 0, NLEV, jnp.int32), 'down_scale': jax.random.uniform(ks[10], (H,), jnp.float32), 'down_A': jax.random.normal(ks[11], (I, R), jnp.float32), 'down_B': jax.random.normal(ks[12], (R, H), jnp.float32)}
        return inp
    _L0_ffn_in = _L0_ffn_setup()
    _d = {'L0_attn_a_x': _L0_attn_a_in['x'], 'L0_attn_a_Wq': _L0_attn_a_in['Wq'], 'L0_attn_a_Wk': _L0_attn_a_in['Wk'], 'L0_attn_a_Wv': _L0_attn_a_in['Wv'], 'L0_attn_a_Wo': _L0_attn_a_in['Wo'], 'L0_attn_b_Wq': _L0_attn_b_in['Wq'], 'L0_attn_b_bq': _L0_attn_b_in['bq'], 'L0_attn_b_Wk': _L0_attn_b_in['Wk'], 'L0_attn_b_bk': _L0_attn_b_in['bk'], 'L0_attn_b_Wv': _L0_attn_b_in['Wv'], 'L0_attn_b_bv': _L0_attn_b_in['bv'], 'L0_attn_b_Wo': _L0_attn_b_in['Wo'], 'L0_attn_b_bo': _L0_attn_b_in['bo'], 'L0_ffn_gate_q': _L0_ffn_in['gate_q'], 'L0_ffn_gate_scale': _L0_ffn_in['gate_scale'], 'L0_ffn_gate_A': _L0_ffn_in['gate_A'], 'L0_ffn_gate_B': _L0_ffn_in['gate_B'], 'L0_ffn_up_q': _L0_ffn_in['up_q'], 'L0_ffn_up_scale': _L0_ffn_in['up_scale'], 'L0_ffn_up_A': _L0_ffn_in['up_A'], 'L0_ffn_up_B': _L0_ffn_in['up_B'], 'L0_ffn_down_q': _L0_ffn_in['down_q'], 'L0_ffn_down_scale': _L0_ffn_in['down_scale'], 'L0_ffn_down_A': _L0_ffn_in['down_A'], 'L0_ffn_down_B': _L0_ffn_in['down_B']}
    _x0 = _d['L0_attn_a_x']
    _d['L0_attn_a_x'] = jax.random.normal(jax.random.fold_in(jax.random.key(seed), 1), (4, 512, 512), dtype=_x0.dtype)
    del _x0
    return _d

def reference(L0_attn_a_x, L0_attn_a_Wq, L0_attn_a_Wk, L0_attn_a_Wv, L0_attn_a_Wo, L0_attn_b_Wq, L0_attn_b_bq, L0_attn_b_Wk, L0_attn_b_bk, L0_attn_b_Wv, L0_attn_b_bv, L0_attn_b_Wo, L0_attn_b_bo, L0_ffn_gate_q, L0_ffn_gate_scale, L0_ffn_gate_A, L0_ffn_gate_B, L0_ffn_up_q, L0_ffn_up_scale, L0_ffn_up_A, L0_ffn_up_B, L0_ffn_down_q, L0_ffn_down_scale, L0_ffn_down_A, L0_ffn_down_B):

    def _L0_attn_a_ref(x, Wq, Wk, Wv, Wo):
        import jax, jax.numpy as jnp
        import numpy as np
        import math
        B, T, D_IN, D_OUT = (2, 256, 512, 512)
        N_HEADS, N_KV = (32, 8)
        HEAD_DIM = D_OUT // N_HEADS
        GROUP_SIZE = N_HEADS // N_KV
        ROPE_BASE = 500000.0
        CTX = 256

        def _rope_tables(head_dim, base, seq_len):
            inv_freq = 1.0 / base ** (jnp.arange(0, head_dim, 2, dtype=jnp.float32) / head_dim)
            t = jnp.arange(seq_len, dtype=jnp.float32)
            freqs = jnp.einsum('i,j->ij', t, inv_freq)
            return (jnp.cos(freqs), jnp.sin(freqs))

        def _apply_rope(x, cos, sin):
            x1, x2 = jnp.split(x, 2, axis=-1)
            c = cos[None, None]
            s = sin[None, None]
            return jnp.concatenate([x1 * c - x2 * s, x1 * s + x2 * c], axis=-1)
        b, t, _ = x.shape
        cos, sin = _rope_tables(HEAD_DIM, ROPE_BASE, t)
        q = (x @ Wq).reshape(b, t, N_HEADS, HEAD_DIM).transpose(0, 2, 1, 3)
        k = (x @ Wk).reshape(b, t, N_KV, HEAD_DIM).transpose(0, 2, 1, 3)
        v = (x @ Wv).reshape(b, t, N_KV, HEAD_DIM).transpose(0, 2, 1, 3)
        q = _apply_rope(q, cos, sin)
        k = _apply_rope(k, cos, sin)
        k_h = jnp.repeat(k, GROUP_SIZE, axis=1)
        v_h = jnp.repeat(v, GROUP_SIZE, axis=1)
        scores = jnp.einsum('bhqd,bhkd->bhqk', q, k_h) / math.sqrt(HEAD_DIM)
        causal = jnp.triu(jnp.ones((t, t), dtype=bool), k=1)
        scores = jnp.where(causal[None, None], jnp.finfo(scores.dtype).min, scores)
        attn = jax.nn.softmax(scores, axis=-1)
        ctx = jnp.einsum('bhqk,bhkd->bhqd', attn, v_h)
        ctx = ctx.transpose(0, 2, 1, 3).reshape(b, t, D_OUT)
        return ctx @ Wo

    def _L0_attn_b_ref(x, Wq, bq, Wk, bk, Wv, bv, Wo, bo):
        import jax, jax.numpy as jnp
        import numpy as np
        import math
        B, L, D, H = (32, 64, 512, 32)
        HD = D // H
        b, l, d = x.shape
        h, hd = (H, HD)
        q = (x @ Wq.T + bq).reshape(b, l, h, hd).transpose(0, 2, 1, 3)
        k = (x @ Wk.T + bk).reshape(b, l, h, hd).transpose(0, 2, 1, 3)
        v = (x @ Wv.T + bv).reshape(b, l, h, hd).transpose(0, 2, 1, 3)
        scores = jnp.einsum('bhqd,bhkd->bhqk', q, k) / math.sqrt(hd)
        causal = jnp.tril(jnp.ones((l, l), bool))
        scores = jnp.where(causal, scores, -jnp.inf)
        att = jax.nn.softmax(scores, axis=-1)
        out = jnp.einsum('bhqk,bhkd->bhqd', att, v)
        out = out.transpose(0, 2, 1, 3).reshape(b, l, d)
        return out @ Wo.T + bo

    def _L0_ffn_ref(x, gate_q, gate_scale, gate_A, gate_B, up_q, up_scale, up_A, up_B, down_q, down_scale, down_A, down_B):
        import jax, jax.numpy as jnp
        import numpy as np
        H = 512
        I = 1376
        R = 32
        NLEV = 16
        Q_ZERO = 7.5
        Q_STEP = 0.005
        LR_SCALE = 0.02

        def _qlinear(x, q, scale, A, Bm):
            w = (q.astype(jnp.float32) - Q_ZERO) * (scale * Q_STEP)[:, None]
            y = jnp.einsum('bsh,oh->bso', x, w)
            return y + LR_SCALE * (x @ A @ Bm)
        g = _qlinear(x, gate_q, gate_scale, gate_A, gate_B)
        u = _qlinear(x, up_q, up_scale, up_A, up_B)
        h = jax.nn.silu(g) * u
        return _qlinear(h, down_q, down_scale, down_A, down_B)
    x = L0_attn_a_x
    x = x + _L0_attn_a_ref(_layernorm(x, axis=-1), L0_attn_a_Wq, L0_attn_a_Wk, L0_attn_a_Wv, L0_attn_a_Wo)
    x = x + _L0_ffn_ref(_layernorm(x, axis=-1), L0_ffn_gate_q, L0_ffn_gate_scale, L0_ffn_gate_A, L0_ffn_gate_B, L0_ffn_up_q, L0_ffn_up_scale, L0_ffn_up_A, L0_ffn_up_B, L0_ffn_down_q, L0_ffn_down_scale, L0_ffn_down_A, L0_ffn_down_B)
    x = x + _L0_attn_b_ref(_layernorm(x, axis=-1), L0_attn_b_Wq, L0_attn_b_bq, L0_attn_b_Wk, L0_attn_b_bk, L0_attn_b_Wv, L0_attn_b_bv, L0_attn_b_Wo, L0_attn_b_bo)
    x = x + _L0_ffn_ref(_layernorm(x, axis=-1), L0_ffn_gate_q, L0_ffn_gate_scale, L0_ffn_gate_A, L0_ffn_gate_B, L0_ffn_up_q, L0_ffn_up_scale, L0_ffn_up_A, L0_ffn_up_B, L0_ffn_down_q, L0_ffn_down_scale, L0_ffn_down_A, L0_ffn_down_B)
    return x

_drawn_inputs = setup_inputs


def setup_inputs(seed=0):
    import zlib

    import numpy as np

    out = dict(_drawn_inputs(seed))
    spreads = {}
    factors = {'L0_attn_a_Wq': 6.932,
     'L0_attn_a_Wk': 6.897,
     'L0_attn_b_Wq': 3.859,
     'L0_attn_b_bq': 8.0,
     'L0_attn_b_Wk': 3.97,
     'L0_attn_b_bk': 64.0,
     'L0_attn_b_Wv': 3.346,
     'L0_attn_b_bv': 8.0,
     'L0_attn_b_Wo': 3.295,
     'L0_attn_b_bo': 23.005}
    for name, (base, spread) in spreads.items():
        noise = np.random.default_rng([zlib.crc32(name.encode()), seed]).standard_normal(out[name].shape)
        drawn = base * np.exp(spread * noise) if base else spread * noise
        out[name] = jnp.asarray(drawn.astype(out[name].dtype))
    for name, factor in factors.items():
        out[name] = (out[name] * factor).astype(out[name].dtype)
    return out
```

```python
from contextlib import ExitStack

import numpy as np

import concourse.bass as bass
from concourse import mybir

F32 = mybir.dt.float32
F32R = mybir.dt.float32r
BF16 = mybir.dt.bfloat16
F16 = mybir.dt.float16
I32 = mybir.dt.int32
ALU = mybir.AluOpType
ACT = mybir.ActivationFunctionType
AX_X = mybir.AxisListType.X

P = 128
BATCH, T, D = 4, 512, 512
NT = T // P
KD = D // P
HEADS, HD = 32, 16
KV_GQA = 8
ROPE_BASE = 500000.0
INTER, RANK = 1376, 32
NI = -(-INTER // P)
LAST = INTER - (NI - 1) * P
Q_ZERO, Q_STEP, LR_SCALE = 7.5, 0.005, 0.02
EPS = 1e-5

PARTS = 6
STK = PARTS * HD
MAXROW = STK
ROWS = STK + 4
SHIFT = 36.0
VW = 50
MASKED = -1.0e30
PAIRS = HEADS // 2
PCOLS = 2 * (512 + 384 + 256 + 128)



class Signal:

    def __init__(self, sem, per_batch, credit=0):
        self.sem, self.per_batch, self.credit = sem, per_batch, credit

    def at(self, b, k):
        return b * self.per_batch + (k + self.credit)


class Phase:

    def __init__(self, nc):
        self.nc, self.held, self.stack = nc, [], ExitStack()

    def semaphore(self, name):
        self.held.append(self.stack.enter_context(self.nc.semaphore(name)))
        return self.held[-1]

    def __enter__(self):
        return self

    def __exit__(self, *failed):
        if failed[0] is None:
            with self.nc.Block() as block:

                @block.sync
                def _(sp):
                    for s in self.held:
                        sp.sem_clear(s)

        self.stack.close()


class Ring:

    SLOTS = 3

    def __init__(self, ctx, phase, nc, name, uses):
        self.psum = ctx.enter_context(nc.psum_tensor(f"{name}_ring", [P, self.SLOTS, 1024], F32))
        self.place = {u: (i % self.SLOTS, i // self.SLOTS) for i, u in enumerate(uses)}
        count = [len(range(s, len(uses), self.SLOTS)) for s in range(self.SLOTS)]
        self.filled = [Signal(phase.semaphore(f"{name}_psum{s}_filled"), count[s])
                       for s in range(self.SLOTS)]
        self.freed = [Signal(phase.semaphore(f"{name}_psum{s}_freed"), count[s], 1)
                      for s in range(self.SLOTS)]

    def give_credits(self, eng):
        for s in range(self.SLOTS):
            eng.sem_inc(self.freed[s].sem, 1)

    def take(self, pe, b, use):
        s, n = self.place[use]
        pe.wait_ge(self.freed[s].sem, self.freed[s].at(b, n))
        return self.psum[:, s, :]

    def read(self, eng, b, use):
        s, n = self.place[use]
        eng.wait_ge(self.filled[s].sem, self.filled[s].at(b, n + 1))
        return self.psum[:, s, :]

    def emptied(self, eng, b, use):
        s, n = self.place[use]
        eng.wait_ge(self.freed[s].sem, self.freed[s].at(b, n + 1))

    def is_filled(self, use):
        return self.filled[self.place[use][0]].sem

    def is_free(self, use):
        return self.freed[self.place[use][0]].sem


def constants(ctx, nc):
    identf = ctx.enter_context(nc.sbuf_tensor("identf", [P, P], F32))
    identb = ctx.enter_context(nc.sbuf_tensor("identb", [P, P], BF16))
    mask_qk = ctx.enter_context(nc.sbuf_tensor("mask_qk", [P, P], BF16))
    mask_kq = ctx.enter_context(nc.sbuf_tensor("mask_kq", [P, P], BF16))
    made = ctx.enter_context(nc.semaphore("constants_cleared"))
    with nc.Block() as block:

        @block.gpsimd
        def _(pool):
            pool.memset(identf[:], 0.0)
            pool.memset(identb[:], 0.0)
            pool.memset(mask_qk[:], 0.0)
            pool.memset(mask_kq[:], 0.0).then_inc(made, 1)
            pool.wait_ge(made, 1)
            for m in (identf, identb):
                pool.affine_select(out=m[:], in_=m[:], compare_op=ALU.not_equal, fill=1.0, base=0,
                                   pattern=[[-1, P]], channel_multiplier=1)
            pool.affine_select(out=mask_qk[:], in_=mask_qk[:], compare_op=ALU.is_ge, fill=MASKED, base=0,
                               pattern=[[-1, P]], channel_multiplier=1)
            pool.affine_select(out=mask_kq[:], in_=mask_kq[:], compare_op=ALU.is_ge, fill=MASKED, base=0,
                               pattern=[[1, P]], channel_multiplier=-1)

    return identf, identb, mask_qk, mask_kq


class Norm:

    def __init__(self, ctx, phase, nc, name, ring, identf, x_dram, xn=None):
        sb = lambda n, s, d: ctx.enter_context(nc.sbuf_tensor(f"{name}_{n}", s, d))
        sem = lambda n: phase.semaphore(f"{name}_{n}")
        self.ring, self.identf, self.x_dram, self.nc = ring, identf, x_dram, nc
        self.x = sb("x", [P, NT, D], F32)
        self.xn = sb("xn", [P, 2, D], F32) if xn is None else xn
        self.xt = sb("xt", [P, 2, KD, T], F32R)
        self.stats = sb("stats", [P, NT, 6], F32)
        self.mv = sb("mv", [P, NT, 2], F32)
        self.rstd = sb("rstd", [P, NT], F32)
        self.var = sb("var", [P, NT], F32)
        self.power = sb("power", [P, 1], F32)
        self.loaded = [Signal(sem(f"x{t}_loaded"), 16) for t in range(NT)]
        self.stats_made = Signal(sem("stats_made"), NT)
        self.stats_seen = sem("stats_seen")
        self.aggregated = Signal(sem("aggregated"), NT)
        self.var_made = Signal(sem("var_made"), NT)
        self.rstd_made = Signal(sem("rstd_made"), NT)
        self.normed = Signal(sem("normed"), NT)
        self.hi_made = Signal(sem("hi_made"), NT)
        self.stored = [Signal(sem(f"y{t}_stored"), 16, 16) for t in range(NT)]

    def credits(self, sp):
        for t in range(NT):
            sp.sem_inc(self.stored[t].sem, 16)

    def load(self, sp, b, t):
        sp.wait_ge(self.stored[t].sem, self.stored[t].at(b, 0))
        sp.dma_start(self.x[:, t, :], self.x_dram[b, t]).then_inc(self.loaded[t].sem, 16)

    def store(self, sp, b, t, y_dram, use):
        self.ring.emptied(sp, b, use)
        sp.dma_start(y_dram[b, t], self.x[:, t, :]).then_inc(self.stored[t].sem, 16)

    def setup(self, dve):
        dve.memset(self.power[:], -0.5)

    def statistics(self, dve, b, t):
        dve.wait_ge(self.loaded[t].sem, self.loaded[t].at(b, 16))
        dve.bn_stats(self.stats[:, t, :], self.x[:, t, :]).then_inc(self.stats_made.sem, 1)
        dve.wait_ge(self.stats_made.sem, self.stats_made.at(b, t + 1))
        dve.sem_inc(self.stats_seen, 1)
        dve.bn_aggr(self.mv[:, t, :], self.stats[:, t, :]).then_inc(self.aggregated.sem, 1)
        dve.wait_ge(self.aggregated.sem, self.aggregated.at(b, t + 1))
        dve.tensor_scalar(self.var[:, t:t + 1], self.mv[:, t, 1:2], EPS, None, ALU.add)\
           .then_inc(self.var_made.sem, 1)

    def root(self, pool, b, t):
        pool.wait_ge(self.var_made.sem, self.var_made.at(b, t + 1))
        pool.tensor_tensor(self.rstd[:, t:t + 1], self.var[:, t:t + 1], self.power[:], ALU.pow)\
            .then_inc(self.rstd_made.sem, 1)

    def normalise(self, dve, b, t):
        dve.wait_ge(self.rstd_made.sem, self.rstd_made.at(b, t + 1))
        if t >= 2:
            self.ring.read(dve, b, f"X{t - 2}")
        dve.tensor_scalar(self.xn[:, t % 2, :], self.x[:, t, :], self.mv[:, t, 0:1],
                          self.rstd[:, t:t + 1], ALU.subtract, ALU.mult).then_inc(self.normed.sem, 1)

    def transpose(self, pe, b, t):
        out = self.ring.take(pe, b, f"X{t}")
        pe.wait_ge(self.normed.sem, self.normed.at(b, t + 1))
        for f in range(KD):
            mm = pe.transpose(out[:, f * P:(f + 1) * P], self.xn[:, t % 2, f * P:(f + 1) * P],
                              self.identf[:])
        mm.then_inc(self.ring.is_filled(f"X{t}"), 1)

    def split_hi(self, act, b, t, use="X", done=None):
        dst, done = self.xt, done or self.hi_made
        src = self.ring.read(act, b, f"{use}{t}")[:, 0:D].rearrange("p (f t) -> p f t", f=KD)
        act.copy(dst[:, 0, :, t * P:(t + 1) * P], src).then_inc(done.sem, 1)

    def split_lo(self, dve, b, t, use="X", hi=None):
        hi = hi or self.hi_made
        src = self.ring.read(dve, b, f"{use}{t}")[:, 0:D].rearrange("p (f t) -> p f t", f=KD)
        dve.wait_ge(hi.sem, hi.at(b, t + 1))
        tok = slice(t * P, (t + 1) * P)
        dve.tensor_tensor(self.xt[:, 1, :, tok], src, self.xt[:, 0, :, tok].bitcast(F32), ALU.subtract)\
           .then_inc(self.ring.is_free(f"{use}{t}"), 1)


def passes(pe, out, pairs, start=True, stop=True):
    for i, (w, x) in enumerate(pairs):
        mm = pe.matmul(out, w, x, start=start and i == 0, stop=stop and i == len(pairs) - 1)
    return mm


def attention(nc, phase, name, consts, x_dram, y_dram, w_dram, kv_heads, rope_dram=None, bias_dram=None,
              biassel_dram=None):
    identf, identb, mask_qk, mask_kq = consts
    rope, biased = rope_dram is not None, bias_dram is not None
    rep = HEADS // kv_heads
    KVD = kv_heads * HD
    OQ, OK, OV, OO = 0, D, D + KVD, D + 2 * KVD
    WN = OO + D
    split_v = KVD == D

    uses = [f"X{t}" for t in range(NT)]
    stacks = ["TQ0", "TQ1"] + (["TK0", "TK1"] if kv_heads > 16 else ["TK0"])
    for t in range(NT + 1):
        if t < NT:
            uses += [f"QK{t}"] + ([f"V{t}"] if split_v else [])
        if t >= 1:
            uses += [f"{s}_{t - 1}" for s in stacks]
    uses += ["M0_0", "M1_0", "M2_0", "N0", "M0_1", "M1_1", "M2_1"]
    for s in range(PAIRS):
        if s + 1 < PAIRS:
            uses.append(f"N{s + 1}")
        for u in range(3):
            uses.append(f"E{u}_{s}")
            if s + 2 < PAIRS:
                uses.append(f"M{u}_{s + 2}")
    uses += [f"C{t}" for t in range(NT)] + [f"O{t}" for t in range(NT)]

    with ExitStack() as ctx:
        sb = lambda n, s, d: ctx.enter_context(nc.sbuf_tensor(f"{name}_{n}", s, d))
        sem = lambda n: phase.semaphore(f"{name}_{n}")
        ring = Ring(ctx, phase, nc, name, uses)
        av = ctx.enter_context(nc.psum_tensor(f"{name}_av", [P, 2, 512], F32))
        region = sb("region", [P, 7 * 1024], F32)
        rest = region[:, 6144:7168].rearrange("p (i n) -> p i n", i=2)
        norm = Norm(ctx, phase, nc, name, ring, identf, x_dram, rest)
        xt = norm.xt
        w = sb("w", [P, 2, KD, WN], F32R)
        qs = sb("qs", [ROWS, HEADS, T], BF16)
        ks = sb("ks", [ROWS, kv_heads, T], BF16)
        v = sb("v", [P, NT, kv_heads, VW], BF16)
        cx = sb("ctx", [P, NT, D], F32)
        nmax = sb("nmax", [P, 2, NT, 2], F32)
        nrest = sb("nrest", [P, 2, NT, 2], F32)
        nparts = sb("nparts", [P, 2, NT, 2, 4], BF16)
        osum = sb("osum", [P, 2, 8, HD], F32)
        rden = sb("rden", [P, 2, 8], F32)
        wraw = region[:, 0:2 * WN].rearrange("p (i n) -> p i n", i=2)
        staged = region[:, 0:6144].bitcast(BF16).rearrange("p (i h s d) -> p i h s d", i=4, s=PARTS, d=HD)
        pf = region[:, 0:2048].rearrange("p (i n) -> p i n", i=2)
        ph = region[:, 2048:2048 + PCOLS].bitcast(F16).rearrange("p (i n) -> p i n", i=2)
        pl = region[:, 2048 + PCOLS:2048 + 2 * PCOLS].bitcast(F16).rearrange("p (i n) -> p i n", i=2)
        if rope:
            trig = sb("trig", [P, NT, 2, HD], F32)
            turned = sb("turned", [P, 2, 2, D], F32)
        if biased:
            biasraw, biashi = region[:, 2 * WN:2 * WN + D], region[:, 2 * WN + D:2 * WN + 2 * D]
            selraw = region[:, 2 * WN + 2 * D:2 * WN + 2 * D + NT * P + 1]
            bias = sb("bias", [P, D], F32R)
            sel = sb("sel", [P, NT * P], F32R)

        w_loaded = [sem(f"w{i}_loaded") for i in range(2)]
        w_hi_made, w_lo_made = sem("w_hi_made"), sem("w_lo_made")
        extra_loaded, extra_hi, extra_made = sem("extra_loaded"), sem("extra_hi"), sem("extra_made")
        rows_set, bias_cleared = sem("rows_set"), sem("bias_cleared")
        NITEM = 3 * NT
        part_hi = Signal(sem("part_hi"), NITEM)
        part_rest = Signal(sem("part_rest"), (1 if split_v else 2) * NT)
        part_mid = Signal(sem("part_mid"), NITEM)
        part_lo = Signal(sem("part_lo"), NITEM, 2)
        turn_a = Signal(sem("rope_products"), 2 * NT)
        turned_made = Signal(sem("rope_made"), 2 * NT)
        stack_staged = Signal(sem("stack_staged"), 2 * NT)
        nmax_chain = Signal(sem("nmax_chain"), 3 * PAIRS)
        nmax_split = Signal(sem("nmax_split"), PAIRS)
        plo_made = Signal(sem("plo_made"), 3 * PAIRS, 2)
        av_made = Signal(sem("av_made"), PAIRS, 2)
        av_summed = Signal(sem("av_summed"), PAIRS)
        av_read = Signal(sem("av_read"), PAIRS, 2)
        ctx_made = Signal(sem("ctx_made"), PAIRS)
        chi_made = Signal(sem("chi_made"), NT)

        items = [(kind, t) for t in range(NT) for kind in "qkv"]
        staging = {("q", t): (2 * t) % 4 for t in range(NT)} | {("k", t): (2 * t + 1) % 4 for t in range(NT)}

        def source(psum, kind):
            if kind == "q":
                return psum[:, 0:D]
            if split_v:
                return psum[:, D:2 * D] if kind == "k" else psum[:, 0:D]
            return psum[:, D:D + KVD] if kind == "k" else psum[:, D + KVD:D + 2 * KVD]

        def use_of(kind, t):
            return f"V{t}" if kind == "v" and split_v else f"QK{t}"

        def frees(kind):
            return kind == "v" or (kind == "k" and split_v)

        def heads_of(kind):
            return HEADS if kind == "q" else kv_heads

        def part(kind, t, which):
            if kind == "v":
                return v[:, t, :, which * HD:(which + 1) * HD]
            slot = (0, 1, 5)[which] if kind == "q" else (0, 2, 4)[which]
            return staged[:, staging[kind, t], 0:heads_of(kind), slot, :]

        def split_cols(ap):
            return ap.rearrange("p (h d) -> p h d", d=HD)

        def stack_use(use):
            dst = qs if use[1] == "Q" else ks
            h0 = 16 * int(use[2])
            return dst, h0, min(16, dst.shape[1] - h0)

        ORDER = list(stacks)
        ACT_COPIES = [s for s in ORDER if s.endswith("0")]
        DVE_COPIES = [s for s in ORDER if s.endswith("1")]

        block = ctx.enter_context(nc.Block())

        @block.sync
        def _(sp):
            norm.credits(sp)
            for f in range(KD):
                if f >= 2:
                    sp.wait_ge(w_lo_made, f - 1)
                sp.dma_start(wraw[:, f % 2, :], w_dram[:, f, :]).then_inc(w_loaded[f % 2], 16)
            if rope:
                sp.dma_start(trig[:].rearrange("p t a d -> p (t a d)"), rope_dram).then_inc(extra_loaded, 16)
            if biased:
                sp.wait_ge(bias_cleared, 1)
                sp.dma_start(biasraw[0:8, :], bias_dram).then_inc(extra_loaded, 16)
                sp.dma_start(selraw, biassel_dram).then_inc(extra_loaded, 16)
            with sp.Fori(0, BATCH) as b:
                for t in range(NT):
                    norm.load(sp, b, t)
                for t in range(NT):
                    norm.store(sp, b, t, y_dram, f"O{t}")
            for t in range(NT):
                sp.wait_ge(norm.stored[t].sem, norm.stored[t].at(BATCH, 0))

        @block.gpsimd
        def _(pool):
            ones_rows = slice(MAXROW, ROWS)
            pool.memset(ks[ones_rows, :, :], 1.0).then_inc(rows_set, 1)
            pool.wait_ge(rows_set, 1)
            pool.memset(qs[ones_rows, :, :], SHIFT).then_inc(rows_set, 1)
            pool.wait_ge(rows_set, 2)
            pool.memset(v[:, :, :, 3 * HD:3 * HD + 1], 1.0).then_inc(rows_set, 1)
            pool.wait_ge(rows_set, 3)
            with pool.Fori(0, BATCH) as b:
                for t in range(NT):
                    norm.root(pool, b, t)
                for s in range(PAIRS):
                    for u in range(3):
                        n = 3 * s + u
                        o, c = (0, 1024, 2048)[u], (1024, 1024, 512)[u]
                        ring.emptied(pool, b, f"E{u}_{s}")
                        pool.tensor_tensor(pl[:, s % 2, o:o + c], pf[:, n % 2, 0:c], ph[:, s % 2, o:o + c],
                                           ALU.subtract).then_inc(plo_made.sem, 1)

        @block.scalar
        def _(act):
            ring.give_credits(act)
            act.sem_inc(plo_made.sem, 2)
            act.sem_inc(part_lo.sem, 2)
            act.sem_inc(av_made.sem, 2)
            act.sem_inc(av_read.sem, 2)
            for f in range(KD):
                act.wait_ge(w_loaded[f % 2], 16 * (f // 2 + 1))
                act.copy(w[:, 0, f, :], wraw[:, f % 2, :]).then_inc(w_hi_made, 1)
            if biased:
                act.wait_ge(extra_loaded, 32)
                act.copy(biashi.bitcast(F32R), biasraw)
                act.copy(sel[:], selraw[:, 0:NT * P]).then_inc(extra_hi, 1)
            act.wait_ge(w_lo_made, KD)

            def hi(b, i):
                kind, t = items[i]
                if kind != "v":
                    j = 2 * t + "qk".index(kind)
                    if j >= 4:
                        last = [u for u in stacks if u[1] == kind.upper()][-1]
                        ring.read(act, b, f"{last}_{t - 2}")
                    elif t == 0 and kind == "q":
                        act.wait_ge(av_made.sem, av_made.at(b, 0))
                if rope and kind != "v":
                    act.wait_ge(turned_made.sem, turned_made.at(b, 2 * t + "qk".index(kind) + 1))
                    src = rest[:, i % 2, 0:heads_of(kind) * HD]
                else:
                    src = source(ring.read(act, b, use_of(kind, t)), kind)
                act.copy(part(kind, t, 0), split_cols(src)).then_inc(part_hi.sem, 1)

            def mid(b, i):
                kind, t = items[i]
                if frees(kind):
                    ring.emptied(act, b, use_of(kind, t))
                else:
                    n = t + 1 if split_v else 2 * t + 1 + (kind == "k")
                    act.wait_ge(part_rest.sem, part_rest.at(b, n))
                act.copy(part(kind, t, 1), split_cols(rest[:, i % 2, 0:heads_of(kind) * HD]))\
                   .then_inc(part_mid.sem, 1)

            def stacks_out(b, t):
                for u in ACT_COPIES:
                    dst, h0, n = stack_use(u)
                    src = ring.read(act, b, f"{u}_{t}").bitcast(BF16)[0:STK, 0:n * P]
                    act.copy(dst[0:STK, h0:h0 + n, t * P:(t + 1) * P],
                             src.rearrange("p (h t) -> p h t", t=P)).then_inc(ring.is_free(f"{u}_{t}"), 1)

            with act.Fori(0, BATCH) as b:
                for t in range(NT):
                    norm.split_hi(act, b, t)
                for t in range(NT):
                    for k in range(3):
                        i = 3 * t + k
                        hi(b, i)
                        if i >= 1:
                            mid(b, i - 1)
                    if t >= 1:
                        stacks_out(b, t - 1)
                mid(b, NITEM - 1)
                stacks_out(b, NT - 1)
                for s in range(PAIRS):
                    for u in range(3):
                        n = 3 * s + u
                        o, c = (0, 1024, 2048)[u], (1024, 1024, 512)[u]
                        act.wait_ge(plo_made.sem, plo_made.at(b, n - 1))
                        src = ring.read(act, b, f"E{u}_{s}")[:, 0:c]
                        act.activation(pf[:, n % 2, 0:c], src, ACT.Exp, scale=0.25)
                        if u == 0:
                            act.wait_ge(av_made.sem, av_made.at(b, s - 1))
                        act.activation(ph[:, s % 2, o:o + c], src, ACT.Exp, scale=0.25)\
                           .then_inc(ring.is_free(f"E{u}_{s}"), 1)
                for t in range(NT):
                    norm.split_hi(act, b, t, "C", chi_made)

        @block.vector
        def _(dve):
            norm.setup(dve)
            if biased:
                dve.memset(biasraw, 0.0).then_inc(bias_cleared, 1)
            for f in range(KD):
                dve.wait_ge(w_hi_made, f + 1)
                dve.tensor_tensor(w[:, 1, f, :], wraw[:, f % 2, :], w[:, 0, f, :].bitcast(F32),
                                  ALU.subtract).then_inc(w_lo_made, 1)
            if biased:
                dve.wait_ge(extra_hi, 1)
                dve.scalar_tensor_tensor(out=bias[:], in0=biashi,
                                         scalar=selraw[:, NT * P:NT * P + 1], in1=biasraw,
                                         op0=ALU.mult, op1=ALU.add).then_inc(extra_made, 1)
            if rope:
                dve.wait_ge(extra_loaded, 16)

            def rotate(b, i):
                kind, t = items[i]
                n, j = heads_of(kind), 2 * t + "qk".index(kind)
                x = source(ring.read(dve, b, use_of(kind, t)), kind)
                x = x.rearrange("p (h a d) -> p h a d", a=2, d=HD // 2)
                shape = [P, n, HD // 2]
                dve.wait_ge(part_lo.sem, part_lo.at(b, i - 1))
                ta = turned[:, i % 2, 0, 0:n * HD].rearrange("p (h a d) -> p h a d", a=2, d=HD // 2)
                tb = turned[:, i % 2, 1, 0:n * HD].rearrange("p (h a d) -> p h a d", a=2, d=HD // 2)
                for a in range(2):
                    half = slice(a * HD // 2, (a + 1) * HD // 2)
                    dve.tensor_tensor(ta[:, :, a, :], x[:, :, a, :],
                                      trig[:, t, 0:1, half].broadcast_to(shape), ALU.mult)
                    last = dve.tensor_tensor(tb[:, :, a, :], x[:, :, 1 - a, :],
                                             trig[:, t, 1:2, half].broadcast_to(shape), ALU.mult)
                last.then_inc(turn_a.sem, 1)
                dve.wait_ge(turn_a.sem, turn_a.at(b, j + 1))
                dve.tensor_tensor(rest[:, i % 2, 0:n * HD], turned[:, i % 2, 0, 0:n * HD],
                                  turned[:, i % 2, 1, 0:n * HD], ALU.add).then_inc(turned_made.sem, 1)

            def remainder(b, i):
                kind, t = items[i]
                n = heads_of(kind) * HD
                dst = rest[:, i % 2, 0:n]
                if rope and kind != "v":
                    src = dst
                else:
                    src = source(ring.read(dve, b, use_of(kind, t)), kind)
                if not (rope and kind != "v"):
                    dve.wait_ge(part_lo.sem, part_lo.at(b, i - 1))
                dve.wait_ge(part_hi.sem, part_hi.at(b, i + 1))
                last = dve.tensor_tensor(split_cols(dst), split_cols(src), part(kind, t, 0), ALU.subtract)
                last.then_inc(ring.is_free(use_of(kind, t)) if frees(kind) else part_rest.sem, 1)

            def low(b, i):
                kind, t = items[i]
                dve.wait_ge(part_mid.sem, part_mid.at(b, i + 1))
                last = dve.tensor_tensor(part(kind, t, 2), split_cols(rest[:, i % 2, 0:heads_of(kind) * HD]),
                                         part(kind, t, 1), ALU.subtract)
                last.then_inc(part_lo.sem, 1)
                if kind == "v":
                    return
                st = staged[:, staging[kind, t], 0:heads_of(kind)]
                if kind == "q":
                    dve.tensor_copy(st[:, :, 2:4, :], st[:, :, 0:2, :])
                    dve.tensor_copy(st[:, :, 4, :], st[:, :, 0, :]).then_inc(stack_staged.sem, 1)
                else:
                    dve.tensor_copy(st[:, :, 1:4:2, :], st[:, :, 0:3:2, :])
                    dve.tensor_copy(st[:, :, 5, :], st[:, :, 0, :]).then_inc(stack_staged.sem, 1)

            def stacks_out(b, t):
                for u in DVE_COPIES:
                    dst, h0, n = stack_use(u)
                    src = ring.read(dve, b, f"{u}_{t}").bitcast(BF16)[0:STK, 0:n * P]
                    dve.tensor_copy(dst[0:STK, h0:h0 + n, t * P:(t + 1) * P],
                                    src.rearrange("p (h t) -> p h t", t=P))\
                       .then_inc(ring.is_free(f"{u}_{t}"), 1)

            def row_max(b, s):
                nm = nmax[:, s % 2]
                u0 = ring.read(dve, b, f"M0_{s}")
                dve.tensor_reduce(nm[:, 0, :], u0[:, 0:256].rearrange("p (h k) -> p h k", h=2), AX_X,
                                  ALU.max, negate=True)
                dve.tensor_reduce(nm[:, 1, :], u0[:, 256:768].rearrange("p (h k) -> p h k", h=2), AX_X,
                                  ALU.max, negate=True).then_inc(ring.is_free(f"M0_{s}"), 1)
                for u, wide in ((1, 384), (2, 512)):
                    src = ring.read(dve, b, f"M{u}_{s}").rearrange("p (h k) -> p h k", h=2)[:, :, 0:wide]
                    last = dve.tensor_reduce(nm[:, u + 1, :], src, AX_X, ALU.max, negate=True)
                    last.then_inc(ring.is_free(f"M{u}_{s}"), 1)
                nr, np_ = nrest[:, s % 2], nparts[:, s % 2]
                ring.emptied(dve, b, f"M2_{s}")
                dve.tensor_copy(np_[:, :, :, 0], nm).then_inc(nmax_chain.sem, 1)
                dve.wait_ge(nmax_chain.sem, nmax_chain.at(b, 3 * s + 1))
                dve.tensor_tensor(nr, nm, np_[:, :, :, 0], ALU.subtract).then_inc(nmax_chain.sem, 1)
                dve.wait_ge(nmax_chain.sem, nmax_chain.at(b, 3 * s + 2))
                dve.tensor_copy(np_[:, :, :, 1], nr).then_inc(nmax_chain.sem, 1)
                dve.wait_ge(nmax_chain.sem, nmax_chain.at(b, 3 * s + 3))
                dve.tensor_tensor(np_[:, :, :, 2], nr, np_[:, :, :, 1], ALU.subtract)\
                   .then_inc(nmax_split.sem, 1)

            def max_rows(b, s):
                src = ring.read(dve, b, f"N{s}").bitcast(BF16)[MAXROW:MAXROW + 3, 0:2 * T]
                dve.tensor_copy(qs[MAXROW:MAXROW + 3, 2 * s:2 * s + 2, :],
                                src.rearrange("p (h t) -> p h t", t=T))\
                   .then_inc(ring.is_free(f"N{s}"), 1)

            def finish(b, s):
                dve.wait_ge(av_made.sem, av_made.at(b, s + 1))
                a = av[:, s % 2, 0:8 * VW].rearrange("p (g c) -> p g c", c=VW)
                dve.tensor_reduce(osum[:, s % 2], a[:, :, 0:3 * HD].rearrange("p g (s d) -> p g d s", s=3),
                                  AX_X, ALU.add)
                dve.reciprocal(rden[:, s % 2, :], a[:, :, 3 * HD]).then_inc(av_read.sem, 1)
                dve.wait_ge(av_read.sem, av_read.at(b, s + 1))
                dst = cx[:, :, 2 * s * HD:(2 * s + 2) * HD].rearrange("p t (h d) -> p t h d", d=HD)
                src = osum[:, s % 2].rearrange("p (t h) d -> p t h d", h=2)
                rd = rden[:, s % 2, :].rearrange("p (t h) -> p t h", h=2).unsqueeze(3)\
                    .broadcast_to([P, NT, 2, HD])
                dve.tensor_tensor(dst, src, rd, ALU.mult).then_inc(ctx_made.sem, 1)

            with dve.Fori(0, BATCH) as b:
                for t in range(NT + 1):
                    if t < NT:
                        norm.statistics(dve, b, t)
                    if t >= 1:
                        norm.normalise(dve, b, t - 1)
                        if t >= 2:
                            norm.split_lo(dve, b, t - 2)
                norm.split_lo(dve, b, NT - 1)
                for i in range(NITEM + 2):
                    t, k = divmod(i, 3)
                    if 1 <= i <= NITEM:
                        remainder(b, i - 1)
                    if k == 0 and t >= 2:
                        stacks_out(b, t - 2)
                    if i >= 2:
                        low(b, i - 2)
                    if rope and i < NITEM and k < 2:
                        rotate(b, i)
                stacks_out(b, NT - 1)
                row_max(b, 0)
                max_rows(b, 0)
                row_max(b, 1)
                for s in range(PAIRS):
                    if s + 1 < PAIRS:
                        max_rows(b, s + 1)
                    if s + 2 < PAIRS:
                        row_max(b, s + 2)
                    if s >= 1:
                        finish(b, s - 1)
                finish(b, PAIRS - 1)
                for t in range(NT):
                    norm.split_lo(dve, b, t, "C", chi_made)
                for t in range(NT):
                    y = ring.read(dve, b, f"O{t}")[:, 0:D]
                    dve.tensor_tensor(norm.x[:, t, :], y, norm.x[:, t, :], ALU.add)\
                       .then_inc(ring.is_free(f"O{t}"), 1)

        @block.tensor
        def _(pe):
            HI, LO = 0, 1
            THREE = ((HI, HI), (LO, HI), (HI, LO))
            pe.wait_ge(rows_set, 3)

            def project(out, src, t, c0, n, bias_row):
                tok = slice(t * P, (t + 1) * P)
                pairs = [(src[:, a, f, tok], w[:, c, f, c0:c0 + n]) for f in range(KD) for a, c in THREE]
                if biased:
                    pairs.append((sel[:, bias_row * P:(bias_row + 1) * P], bias[:, 0:n]))
                return passes(pe, out, pairs)

            def stack_transposes(b, t):
                for u in stacks:
                    kind = u[1].lower()
                    _, h0, n = stack_use(u)
                    out = ring.take(pe, b, f"{u}_{t}").bitcast(BF16)
                    if u.endswith("0"):
                        j = 2 * t + "qk".index(kind)
                        pe.wait_ge(stack_staged.sem, stack_staged.at(b, j + 1))
                        i = 3 * t + "qk".index(kind)
                        pe.wait_ge(part_lo.sem, part_lo.at(b, i + 1))
                    for h in range(n):
                        src = staged[:, staging[kind, t], h0 + h].rearrange("p s d -> p (s d)")
                        mm = pe.transpose(out[0:STK, h * P:(h + 1) * P], src, identb[:])
                    mm.then_inc(ring.is_filled(f"{u}_{t}"), 1)

            def block_scores(out, lhs, rhs, mask, diag):
                pe.matmul(out, lhs, rhs, start=True, stop=False, skip_group_check=True)
                return pe.matmul(out[:, diag:diag + P], identb[:], mask[:], start=False, stop=True,
                                 skip_group_check=True)

            def max_scores(b, s, u):
                out = ring.take(pe, b, f"M{u}_{s}")
                for qt in ((0, 1), (2,), (3,))[u]:
                    n = (qt + 1) * P
                    for i in range(2):
                        h = 2 * s + i
                        at = (i * P, 2 * P + i * 2 * P, i * 512, i * 512)[qt]
                        mm = block_scores(out[:, at:at + n], qs[0:STK, h, qt * P:(qt + 1) * P],
                                          ks[0:STK, h // rep, 0:n], mask_qk, qt * P)
                mm.then_inc(ring.is_filled(f"M{u}_{s}"), 1)

            def max_transposes(b, s):
                out = ring.take(pe, b, f"N{s}").bitcast(BF16)
                pe.wait_ge(nmax_split.sem, nmax_split.at(b, s + 1))
                for i in range(2):
                    for qt in range(NT):
                        c = i * T + qt * P
                        mm = pe.transpose(out[MAXROW:MAXROW + 3, c:c + P], nparts[:, s % 2, qt, i, 0:3],
                                          identb[:])
                mm.then_inc(ring.is_filled(f"N{s}"), 1)

            def exp_scores(b, s, u):
                out = ring.take(pe, b, f"E{u}_{s}")
                if u == 0:
                    ring.emptied(pe, b, f"N{s}")
                for kb in ((0,), (1, 3), (2,))[u]:
                    n = T - kb * P
                    for i in range(2):
                        h = 2 * s + i
                        at = (i * 512, i * 512, i * 256, i * 512 + 384)[kb]
                        mm = block_scores(out[:, at:at + n], ks[:, h // rep, kb * P:(kb + 1) * P],
                                          qs[:, h, kb * P:T], mask_kq, 0)
                mm.then_inc(ring.is_filled(f"E{u}_{s}"), 1)

            def values(b, s):
                pe.wait_ge(plo_made.sem, plo_made.at(b, 3 * s + 3))
                pe.wait_ge(av_read.sem, av_read.at(b, s - 1))
                for qt in range(NT):
                    for i in range(2):
                        c = (2 * qt + i) * VW
                        pairs = []
                        for kb in range(qt + 1):
                            at = (i * 512 + qt * P, 1024 + i * 512 + (qt - 1) * P,
                                  2048 + i * 256 + (qt - 2) * P, 1024 + i * 512 + 384)[kb]
                            vh = v[:, kb, (2 * s + i) // rep, 0:3 * HD + 1]
                            pairs += [(ph[:, s % 2, at:at + P], vh), (pl[:, s % 2, at:at + P], vh)]
                        mm = passes(pe, av[:, s % 2, c:c + 3 * HD + 1], pairs)
                mm.then_inc(av_made.sem, 1)

            with pe.Fori(0, BATCH) as b:
                for t in range(NT):
                    norm.transpose(pe, b, t)
                pe.wait_ge(w_lo_made, KD)
                if biased:
                    pe.wait_ge(extra_made, 1)
                for t in range(NT + 1):
                    if t < NT:
                        out = ring.take(pe, b, f"QK{t}")
                        ring.emptied(pe, b, f"X{t}")
                        project(out[:, 0:D], xt, t, OQ, D, 0)
                        if split_v:
                            mm = project(out[:, D:2 * D], xt, t, OK, D, 1)
                        else:
                            mm = project(out[:, D:D + 2 * KVD], xt, t, OK, 2 * KVD, 1)
                        mm.then_inc(ring.is_filled(f"QK{t}"), 1)
                        if split_v:
                            out = ring.take(pe, b, f"V{t}")
                            project(out[:, 0:D], xt, t, OV, D, 2).then_inc(ring.is_filled(f"V{t}"), 1)
                    if t >= 1:
                        stack_transposes(b, t - 1)
                for u in stacks:
                    ring.emptied(pe, b, f"{u}_{NT - 1}")
                for u in range(3):
                    max_scores(b, 0, u)
                max_transposes(b, 0)
                for u in range(3):
                    max_scores(b, 1, u)
                for s in range(PAIRS):
                    if s + 1 < PAIRS:
                        max_transposes(b, s + 1)
                    for u in range(3):
                        exp_scores(b, s, u)
                        if s + 2 < PAIRS:
                            max_scores(b, s + 2, u)
                    if s == 1:
                        pe.wait_ge(part_lo.sem, part_lo.at(b, NITEM))
                    if s >= 1:
                        values(b, s - 1)
                values(b, PAIRS - 1)
                for t in range(NT):
                    out = ring.take(pe, b, f"C{t}")
                    pe.wait_ge(ctx_made.sem, ctx_made.at(b, PAIRS))
                    for f in range(KD):
                        mm = pe.transpose(out[:, f * P:(f + 1) * P], cx[:, t, f * P:(f + 1) * P], identf[:])
                    mm.then_inc(ring.is_filled(f"C{t}"), 1)
                for t in range(NT):
                    out = ring.take(pe, b, f"O{t}")
                    ring.emptied(pe, b, f"C{t}")
                    project(out[:, 0:D], xt, t, OO, D, 3).then_inc(ring.is_filled(f"O{t}"), 1)


def ffn(nc, phase, name, consts, x_dram, y_dram, gate_dram, up_dram, down_dram, scales_dram, dscale_dram, xa_dram,
        gb_dram, ub_dram, da_dram, db_dram):
    identf = consts[0]
    uses = [f"X{t}" for t in range(NT)] + ["A"]
    for n in range(NI):
        uses += [f"G{n}", f"U{n}"]
    uses += ["Y0", "DA"] + [f"Y{t}" for t in range(1, NT)]
    HI, LO = 0, 1

    with ExitStack() as ctx:
        sb = lambda n, s, d: ctx.enter_context(nc.sbuf_tensor(f"{name}_{n}", s, d))
        sem = lambda n: phase.semaphore(f"{name}_{n}")
        ring = Ring(ctx, phase, nc, name, uses)
        norm = Norm(ctx, phase, nc, name, ring, identf, x_dram)
        xt = norm.xt
        codes = sb("codes", [P, 2, KD, INTER], F32R)
        dcodes = sb("dcodes", [P, NI, D], F32R)
        raw = sb("raw", [P, 2, INTER], I32)
        scales = sb("scales", [P, 2, NI], F32)
        dscale = sb("dscale", [P, D], F32)
        xa_raw = sb("xa_raw", [P, KD * 2 * RANK], F32)
        xa = sb("xa", [P, 2, KD, 2 * RANK], F32R)
        da_raw = sb("da_raw", [P, NI * RANK], F32)
        da = sb("da", [P, 2, NI, RANK], F32R)
        lr_b = [sb(f"{k}_b", [3 * RANK, c], F32R) for k, c in (("gate", INTER), ("up", INTER), ("down", D))]
        lr_x = [sb(f"{k}_x", [3 * RANK, T], F32R) for k in ("gate", "up", "down")]
        ht = sb("ht", [P, 2, NI, T], F32R)
        work = sb("work", [P, 11 * T], F32)
        gate = work[:, 0:T]
        scaled, sig, upv, hid, ysum = (
            work[:, (2 * i + 1) * T:(2 * i + 3) * T].rearrange("p (a t) -> p a t", a=2) for i in range(5))

        raw_loaded = [sem(f"raw{i}_loaded") for i in range(2)]
        raw_used = sem("raw_used")
        small_loaded = sem("small_loaded")
        b_loaded = sem("b_loaded")
        small_hi = sem("small_hi")
        small_made = sem("small_made")
        b_scaled, b_hi, b_made = sem("b_scaled"), sem("b_hi"), sem("b_made")
        cleared = sem("cleared")
        lrx_hi = Signal(sem("lowrank_hi"), 2)
        p1_scaled = Signal(sem("scaled"), 2 * NI)
        silu_made = Signal(sem("silu_made"), NI)
        hid_made = Signal(sem("hid_made"), NI)
        hid_hi = Signal(sem("hid_hi"), NI)
        hid_lo = Signal(sem("hid_lo"), NI, 2)
        y_part = Signal(sem("y_part"), 2 * NT)

        def rows(n):
            return P if n < NI - 1 else LAST

        def lr_raw(j):
            return work[0:3 * RANK, (0, INTER, 2 * INTER)[j]:(INTER, 2 * INTER, 2 * INTER + D)[j]]

        chunks = [(s, codes[:, j, f, :], s[:, f, :], INTER) for f in range(KD)
                  for j, s in ((0, gate_dram), (1, up_dram))]
        for n in range(0, NI, 2):
            k = min(2, NI - n)
            chunks.append((down_dram, dcodes[:, n:n + k, :].rearrange("p n d -> p (n d)"),
                           down_dram[:, n * D:(n + k) * D], k * D))

        X_LO = (1, 2, 1)
        B_LO = (2, 1, 2)

        block = ctx.enter_context(nc.Block())

        @block.sync
        def _(sp):
            norm.credits(sp)
            for i, (_, _, src, c) in enumerate(chunks):
                if i >= 2:
                    sp.wait_ge(raw_used, i - 1)
                sp.dma_start(raw[:, i % 2, 0:c], src).then_inc(raw_loaded[i % 2], 16)
                if i == 1:
                    sp.dma_start(scales[:].rearrange("p a n -> p (a n)"), scales_dram)\
                      .then_inc(small_loaded, 16)
                    sp.dma_start(dscale[:], dscale_dram.broadcast_to([P, D])).then_inc(small_loaded, 16)
                    sp.dma_start(xa_raw[:], xa_dram).then_inc(small_loaded, 16)
                    sp.dma_start(da_raw[:], da_dram).then_inc(small_loaded, 16)
                    for r in range(3):
                        q = slice(r * RANK, (r + 1) * RANK)
                        for j, (d, c2) in enumerate(((gb_dram, INTER), (ub_dram, INTER), (db_dram, D))):
                            sp.dma_start(lr_raw(j)[q, 0:c2], d).then_inc(b_loaded, 16)
            with sp.Fori(0, BATCH) as b:
                for t in range(NT):
                    norm.load(sp, b, t)
                for t in range(NT):
                    norm.store(sp, b, t, y_dram, f"Y{t}")
            for t in range(NT):
                sp.wait_ge(norm.stored[t].sem, norm.stored[t].at(BATCH, 0))

        @block.gpsimd
        def _(pool):
            with pool.Fori(0, BATCH) as b:
                for t in range(NT):
                    norm.root(pool, b, t)
                for n in range(NI):
                    r = rows(n)
                    pool.wait_ge(hid_hi.sem, hid_hi.at(b, n + 1))
                    pool.tensor_tensor(ht[0:r, LO, n, :], hid[0:r, n % 2, :], ht[0:r, HI, n, :].bitcast(F32),
                                       ALU.subtract).then_inc(hid_lo.sem, 1)

        @block.scalar
        def _(act):
            ring.give_credits(act)
            act.sem_inc(hid_lo.sem, 2)
            act.wait_ge(small_loaded, 64)
            act.copy(xa[:, HI].rearrange("p f r -> p (f r)"), xa_raw[:])
            act.copy(da[:, HI].rearrange("p f r -> p (f r)"), da_raw[:]).then_inc(small_hi, 1)
            act.wait_ge(b_scaled, 3)
            for j in range(3):
                c = lr_b[j].shape[1]
                act.copy(lr_b[j][:], lr_raw(j)[:, 0:c]).then_inc(b_hi, 1)
            with act.Fori(0, BATCH) as b:
                for t in range(NT):
                    norm.split_hi(act, b, t)

                def lowrank_hi(use, j, q):
                    src = ring.read(act, b, use)[q * RANK:(q + 1) * RANK, 0:T]
                    for r in range(3):
                        if r != X_LO[j]:
                            last = act.copy(lr_x[j][r * RANK:(r + 1) * RANK, :], src)
                    return last

                lowrank_hi("A", 0, 0)
                lowrank_hi("A", 1, 1).then_inc(lrx_hi.sem, 1)

                def scale(n, j):
                    r = rows(n)
                    src = ring.read(act, b, f"{'GU'[j]}{n}")[0:r, 0:T]
                    if n >= 1:
                        ring.emptied(act, b, f"{'GU'[j]}{n - 1}")
                    act.activation(scaled[0:r, j, :], src, ACT.Identity, scale=scales[0:r, j, n:n + 1])\
                       .then_inc(p1_scaled.sem, 1)

                def silu(n):
                    r = rows(n)
                    ring.emptied(act, b, f"G{n}")
                    act.activation(sig[0:r, n % 2, :], gate[0:r, :], ACT.Silu).then_inc(silu_made.sem, 1)

                def hidden_hi(n):
                    r = rows(n)
                    act.wait_ge(hid_made.sem, hid_made.at(b, n + 1))
                    act.copy(ht[0:r, HI, n, :], hid[0:r, n % 2, :]).then_inc(hid_hi.sem, 1)

                for n in range(NI + 1):
                    if n < NI:
                        scale(n, 0)
                        scale(n, 1)
                        silu(n)
                    if n >= 1:
                        hidden_hi(n - 1)
                lowrank_hi("DA", 2, 0).then_inc(lrx_hi.sem, 1)

        @block.vector
        def _(dve):
            norm.setup(dve)
            dve.wait_ge(b_loaded, 9 * 16)
            for j in range(3):
                c = lr_b[j].shape[1]
                dve.tensor_scalar(lr_raw(j)[:, 0:c], lr_raw(j)[:, 0:c], LR_SCALE, None, ALU.mult)\
                   .then_inc(b_scaled, 1)
            dve.wait_ge(small_hi, 1)
            dve.tensor_tensor(xa[:, LO].rearrange("p f r -> p (f r)"), xa_raw[:],
                              xa[:, HI].rearrange("p f r -> p (f r)").bitcast(F32), ALU.subtract)
            dve.tensor_tensor(da[:, LO].rearrange("p f r -> p (f r)"), da_raw[:],
                              da[:, HI].rearrange("p f r -> p (f r)").bitcast(F32), ALU.subtract)
            dve.tensor_scalar(scales[:], scales[:], Q_STEP, None, ALU.mult)
            dve.tensor_scalar(dscale[:], dscale[:], Q_STEP, None, ALU.mult).then_inc(small_made, 1)
            for j in range(3):
                c = lr_b[j].shape[1]
                q = slice(B_LO[j] * RANK, (B_LO[j] + 1) * RANK)
                dve.wait_ge(b_hi, j + 1)
                dve.tensor_tensor(lr_b[j][q, :], lr_raw(j)[q, 0:c], lr_b[j][q, :].bitcast(F32),
                                  ALU.subtract).then_inc(b_made, 1)
            for i, (_, dst, _, c) in enumerate(chunks):
                dve.wait_ge(raw_loaded[i % 2], 16 * (i // 2 + 1))
                dve.tensor_scalar(dst, raw[:, i % 2, 0:c], -Q_ZERO, None, ALU.add).then_inc(raw_used, 1)
            with dve.Fori(0, BATCH) as b:
                for t in range(NT + 1):
                    if t < NT:
                        norm.statistics(dve, b, t)
                    if t >= 1:
                        norm.normalise(dve, b, t - 1)
                        if t >= 2:
                            norm.split_lo(dve, b, t - 2)
                norm.split_lo(dve, b, NT - 1)

                def lowrank_lo(use, j, q):
                    src = ring.read(dve, b, use)[q * RANK:(q + 1) * RANK, 0:T]
                    hi = q * RANK
                    return dve.tensor_tensor(lr_x[j][X_LO[j] * RANK:(X_LO[j] + 1) * RANK, :], src,
                                             lr_x[j][hi:hi + RANK, :].bitcast(F32), ALU.subtract)

                dve.wait_ge(lrx_hi.sem, lrx_hi.at(b, 1))
                lowrank_lo("A", 0, 0)
                lowrank_lo("A", 1, 1).then_inc(ring.is_free("A"), 1)

                def add_lowrank(n, j):
                    r = rows(n)
                    src = ring.read(dve, b, f"{'GU'[j]}{n}")[0:r, T:2 * T]
                    dve.wait_ge(p1_scaled.sem, p1_scaled.at(b, 2 * n + j + 1))
                    if j == 0 and n >= 1:
                        dve.wait_ge(silu_made.sem, silu_made.at(b, n))
                    dst = gate[0:r, :] if j == 0 else upv[0:r, n % 2, :]
                    dve.tensor_tensor(dst, src, scaled[0:r, j, :], ALU.add)\
                       .then_inc(ring.is_free(f"{'GU'[j]}{n}"), 1)

                def hidden(n):
                    r = rows(n)
                    dve.wait_ge(silu_made.sem, silu_made.at(b, n + 1))
                    ring.emptied(dve, b, f"U{n}")
                    dve.wait_ge(hid_lo.sem, hid_lo.at(b, n - 1))
                    dve.tensor_tensor(hid[0:r, n % 2, :], sig[0:r, n % 2, :], upv[0:r, n % 2, :], ALU.mult)\
                       .then_inc(hid_made.sem, 1)

                for n in range(NI + 1):
                    if n < NI:
                        add_lowrank(n, 0)
                        add_lowrank(n, 1)
                    if n >= 1:
                        hidden(n - 1)
                dve.wait_ge(lrx_hi.sem, lrx_hi.at(b, 2))
                lowrank_lo("DA", 2, 0).then_inc(ring.is_free("DA"), 1)
                for t in range(NT):
                    y = ring.read(dve, b, f"Y{t}")
                    dve.tensor_tensor(ysum[:, t % 2, :], y[:, 0:D], dscale[:], ALU.mult)\
                       .then_inc(y_part.sem, 1)
                    dve.wait_ge(y_part.sem, y_part.at(b, 2 * t + 1))
                    dve.tensor_tensor(norm.x[:, t, :], ysum[:, t % 2, :], norm.x[:, t, :], ALU.add)\
                       .then_inc(y_part.sem, 1)
                    dve.wait_ge(y_part.sem, y_part.at(b, 2 * t + 2))
                    dve.tensor_tensor(norm.x[:, t, :], y[:, D:2 * D], norm.x[:, t, :], ALU.add)\
                       .then_inc(ring.is_free(f"Y{t}"), 1)

        @block.tensor
        def _(pe):
            THREE = ((HI, HI), (LO, HI), (HI, LO))
            with pe.Fori(0, BATCH) as b:
                for t in range(NT):
                    norm.transpose(pe, b, t)
                pe.wait_ge(small_made, 1)
                out = ring.take(pe, b, "A")
                for t in range(NT):
                    ring.emptied(pe, b, f"X{t}")
                passes(pe, out[0:2 * RANK, 0:T], [(xa[:, a, f, :], xt[:, c, f, :])
                                                  for f in range(KD) for a, c in THREE])\
                    .then_inc(ring.is_filled("A"), 1)
                pe.wait_ge(raw_used, len(chunks))
                pe.wait_ge(b_made, 3)
                for n in range(NI):
                    r = rows(n)
                    cols = slice(n * P, n * P + r)
                    for j in range(2):
                        out = ring.take(pe, b, f"{'GU'[j]}{n}")
                        passes(pe, out[0:r, 0:T], [(codes[:, j, f, cols], xt[:, c, f, :])
                                                   for f in range(KD) for c in (HI, LO)])
                        if n == 0 and j == 0:
                            ring.emptied(pe, b, "A")
                        passes(pe, out[0:r, T:2 * T], [(lr_b[j][:, cols], lr_x[j][:])])\
                            .then_inc(ring.is_filled(f"{'GU'[j]}{n}"), 1)

                def down(out, t, ks):
                    tok = slice(t * P, (t + 1) * P)
                    for n in ks:
                        if t == 0:
                            pe.wait_ge(hid_lo.sem, hid_lo.at(b, n + 1))
                        r = rows(n)
                        passes(pe, out[:, 0:D], [(ht[0:r, c, n, tok], dcodes[0:r, n, :]) for c in (HI, LO)],
                               start=n == 0, stop=n == NI - 1)

                def down_lowrank(out, t):
                    passes(pe, out[:, D:2 * D], [(lr_x[2][:, t * P:(t + 1) * P], lr_b[2][:])])\
                        .then_inc(ring.is_filled(f"Y{t}"), 1)

                y0 = ring.take(pe, b, "Y0")
                down(y0, 0, range(NI))
                out = ring.take(pe, b, "DA")
                passes(pe, out[0:RANK, 0:T], [(da[0:rows(n), a, n, :], ht[0:rows(n), c, n, :])
                                              for n in range(NI) for a, c in THREE])\
                    .then_inc(ring.is_filled("DA"), 1)
                y1 = ring.take(pe, b, "Y1")
                down(y1, 1, range(NI))
                ring.emptied(pe, b, "DA")
                down_lowrank(y0, 0)
                down_lowrank(y1, 1)
                for t in range(2, NT):
                    out = ring.take(pe, b, f"Y{t}")
                    down(out, t, range(NI))
                    down_lowrank(out, t)


def program(nc, d):
    with ExitStack() as ctx:
        mid = [nc.dram_tensor(f"mid{i}", (BATCH, NT, P, D), F32, kind="Internal").ap() for i in range(3)]
        consts = constants(ctx, nc)
        feed = [d[n] for n in ("gate_q", "up_q", "down_q", "scales", "dscale", "xa", "gb", "ub", "da", "db")]
        with Phase(nc) as phase:
            attention(nc, phase, "aa", consts, d["x"], mid[0], d["wa"], KV_GQA, rope_dram=d["trig"])
        with Phase(nc) as phase:
            ffn(nc, phase, "f1", consts, mid[0], mid[1], *feed)
        with Phase(nc) as phase:
            attention(nc, phase, "ab", consts, mid[1], mid[2], d["wb"], HEADS, bias_dram=d["bias"],
                      biassel_dram=d["biassel"])
        with Phase(nc) as phase:
            ffn(nc, phase, "f2", consts, mid[2], d["y"], *feed)


def kernel(**inputs):
    import concourse.bacc as bacc
    from concourse.bass_utils import run_bass_kernel_spmd

    a = {k.removeprefix("L0_"): np.asarray(v) for k, v in inputs.items()}

    def by_feature(w):
        n = -(-w.shape[0] // P)
        w = np.pad(w, ((0, n * P - w.shape[0]), (0, 0)))
        return np.ascontiguousarray(w.reshape(n, P, -1).transpose(1, 0, 2))

    inv = (1.0 / np.float32(ROPE_BASE) ** (np.arange(0, HD, 2, dtype=np.float32) / np.float32(HD)))
    freqs = np.arange(T, dtype=np.float32)[:, None] * inv.astype(np.float32)[None]
    cos, sin = np.cos(freqs).astype(np.float32), np.sin(freqs).astype(np.float32)
    trig = np.stack([np.concatenate([cos, cos], 1), np.concatenate([-sin, sin], 1)], 1)
    trig = trig.reshape(NT, P, 2 * HD).transpose(1, 0, 2).reshape(P, -1)
    biassel = np.zeros((P, NT * P + 1), np.float32)
    for j in range(4):
        biassel[2 * j:2 * j + 2, j * P:(j + 1) * P] = 1.0
    biassel[1:8:2, -1] = -1.0

    qkvo = [a[f"attn_b_W{k}"].T for k in "qkvo"]
    arrays = {
        "x": a["attn_a_x"].reshape(BATCH, NT, P, D),
        "wa": by_feature(np.concatenate([a[f"attn_a_W{k}"] for k in "qkvo"], 1)),
        "wb": by_feature(np.concatenate(qkvo, 1)),
        "trig": trig,
        "bias": np.repeat(np.stack([a[f"attn_b_b{k}"] for k in "qkvo"]), 2, axis=0),
        "biassel": biassel,
        "gate_q": by_feature(a["ffn_gate_q"].T),
        "up_q": by_feature(a["ffn_up_q"].T),
        "down_q": by_feature(a["ffn_down_q"].T).reshape(P, -1),
        "scales": np.concatenate([by_feature(a[f"ffn_{k}_scale"][:, None])[:, :, 0]
                                  for k in ("gate", "up")], 1),
        "dscale": a["ffn_down_scale"].reshape(1, D),
        "xa": by_feature(np.concatenate([a["ffn_gate_A"], a["ffn_up_A"]], 1)).reshape(P, -1),
        "gb": a["ffn_gate_B"],
        "ub": a["ffn_up_B"],
        "da": by_feature(a["ffn_down_A"]).reshape(P, -1),
        "db": a["ffn_down_B"],
    }
    nc = bacc.Bacc("TRN2", target_bir_lowering=False, num_devices=1)
    feed, d = {}, {}
    for key, v in arrays.items():
        v = np.ascontiguousarray(v)
        feed[f"in_{key}"] = v
        d[key] = nc.dram_tensor(f"in_{key}", v.shape, mybir.dt.from_np(v.dtype), kind="ExternalInput").ap()
    d["y"] = nc.dram_tensor("out_y", (BATCH, NT, P, D), F32, kind="ExternalOutput").ap()
    program(nc, d)
    r = run_bass_kernel_spmd(nc, [feed], core_ids=[0])
    return r.results[0]["out_y"].reshape(BATCH, T, D)
```

```python
from contextlib import ExitStack

import numpy as np

import concourse.bass as bass
from concourse import mybir

F32 = mybir.dt.float32
F32R = mybir.dt.float32r
BF16 = mybir.dt.bfloat16
F16 = mybir.dt.float16
I32 = mybir.dt.int32
ALU = mybir.AluOpType
ACT = mybir.ActivationFunctionType
AX_X = mybir.AxisListType.X

P = 128
BATCH, T, D = 4, 512, 512
NT = T // P
KD = D // P
HEADS, HD = 32, 16
KV_GQA = 8
ROPE_BASE = 500000.0
INTER, RANK = 1376, 32
NI = -(-INTER // P)
LAST = INTER - (NI - 1) * P
Q_ZERO, Q_STEP, LR_SCALE = 7.5, 0.005, 0.02
EPS = 1e-5

PARTS = 6
STK = PARTS * HD
MAXROW = STK
ROWS = STK + 4
SHIFT = 36.0
VW = 50
MASKED = -1.0e30
PAIRS = HEADS // 2
PCOLS = 2 * (512 + 384 + 256 + 128)



class Signal:

    def __init__(self, sem, per_batch, credit=0):
        self.sem, self.per_batch, self.credit = sem, per_batch, credit

    def at(self, b, k):
        return b * self.per_batch + (k + self.credit)


class Phase:

    def __init__(self, nc):
        self.nc, self.held, self.stack = nc, [], ExitStack()

    def semaphore(self, name):
        self.held.append(self.stack.enter_context(self.nc.semaphore(name)))
        return self.held[-1]

    def __enter__(self):
        return self

    def __exit__(self, *failed):
        if failed[0] is None:
            with self.nc.Block() as block:

                @block.sync
                def _(sp):
                    for s in self.held:
                        sp.sem_clear(s)

        self.stack.close()


class Ring:

    SLOTS = 3

    def __init__(self, ctx, phase, nc, name, uses):
        self.psum = ctx.enter_context(nc.psum_tensor(f"{name}_ring", [P, self.SLOTS, 1024], F32))
        self.place = {u: (i % self.SLOTS, i // self.SLOTS) for i, u in enumerate(uses)}
        count = [len(range(s, len(uses), self.SLOTS)) for s in range(self.SLOTS)]
        self.filled = [Signal(phase.semaphore(f"{name}_psum{s}_filled"), count[s])
                       for s in range(self.SLOTS)]
        self.freed = [Signal(phase.semaphore(f"{name}_psum{s}_freed"), count[s], 1)
                      for s in range(self.SLOTS)]

    def give_credits(self, eng):
        for s in range(self.SLOTS):
            eng.sem_inc(self.freed[s].sem, 1)

    def take(self, pe, b, use):
        s, n = self.place[use]
        pe.wait_ge(self.freed[s].sem, self.freed[s].at(b, n))
        return self.psum[:, s, :]

    def read(self, eng, b, use):
        s, n = self.place[use]
        eng.wait_ge(self.filled[s].sem, self.filled[s].at(b, n + 1))
        return self.psum[:, s, :]

    def emptied(self, eng, b, use):
        s, n = self.place[use]
        eng.wait_ge(self.freed[s].sem, self.freed[s].at(b, n + 1))

    def is_filled(self, use):
        return self.filled[self.place[use][0]].sem

    def is_free(self, use):
        return self.freed[self.place[use][0]].sem


def constants(ctx, nc):
    identf = ctx.enter_context(nc.sbuf_tensor("identf", [P, P], F32))
    identb = ctx.enter_context(nc.sbuf_tensor("identb", [P, P], BF16))
    mask_qk = ctx.enter_context(nc.sbuf_tensor("mask_qk", [P, P], BF16))
    mask_kq = ctx.enter_context(nc.sbuf_tensor("mask_kq", [P, P], BF16))
    made = ctx.enter_context(nc.semaphore("constants_cleared"))
    with nc.Block() as block:

        @block.gpsimd
        def _(pool):
            pool.memset(identf[:], 0.0)
            pool.memset(identb[:], 0.0)
            pool.memset(mask_qk[:], 0.0)
            pool.memset(mask_kq[:], 0.0).then_inc(made, 1)
            pool.wait_ge(made, 1)
            for m in (identf, identb):
                pool.affine_select(out=m[:], in_=m[:], compare_op=ALU.not_equal, fill=1.0, base=0,
                                   pattern=[[-1, P]], channel_multiplier=1)
            pool.affine_select(out=mask_qk[:], in_=mask_qk[:], compare_op=ALU.is_ge, fill=MASKED, base=0,
                               pattern=[[-1, P]], channel_multiplier=1)
            pool.affine_select(out=mask_kq[:], in_=mask_kq[:], compare_op=ALU.is_ge, fill=MASKED, base=0,
                               pattern=[[1, P]], channel_multiplier=-1)

    return identf, identb, mask_qk, mask_kq


class Norm:

    def __init__(self, ctx, phase, nc, name, ring, identf, x_dram, xn=None):
        sb = lambda n, s, d: ctx.enter_context(nc.sbuf_tensor(f"{name}_{n}", s, d))
        sem = lambda n: phase.semaphore(f"{name}_{n}")
        self.ring, self.identf, self.x_dram, self.nc = ring, identf, x_dram, nc
        self.x = sb("x", [P, NT, D], F32)
        self.xn = sb("xn", [P, 2, D], F32) if xn is None else xn
        self.xt = sb("xt", [P, 2, KD, T], F32R)
        self.stats = sb("stats", [P, NT, 6], F32)
        self.mv = sb("mv", [P, NT, 2], F32)
        self.rstd = sb("rstd", [P, NT], F32)
        self.var = sb("var", [P, NT], F32)
        self.power = sb("power", [P, 1], F32)
        self.loaded = [Signal(sem(f"x{t}_loaded"), 16) for t in range(NT)]
        self.stats_made = Signal(sem("stats_made"), NT)
        self.stats_seen = sem("stats_seen")
        self.aggregated = Signal(sem("aggregated"), NT)
        self.var_made = Signal(sem("var_made"), NT)
        self.rstd_made = Signal(sem("rstd_made"), NT)
        self.normed = Signal(sem("normed"), NT)
        self.hi_made = Signal(sem("hi_made"), NT)
        self.stored = [Signal(sem(f"y{t}_stored"), 16, 16) for t in range(NT)]

    def credits(self, sp):
        for t in range(NT):
            sp.sem_inc(self.stored[t].sem, 16)

    def load(self, sp, b, t):
        sp.wait_ge(self.stored[t].sem, self.stored[t].at(b, 0))
        sp.dma_start(self.x[:, t, :], self.x_dram[b, t]).then_inc(self.loaded[t].sem, 16)

    def store(self, sp, b, t, y_dram, use):
        self.ring.emptied(sp, b, use)
        sp.dma_start(y_dram[b, t], self.x[:, t, :]).then_inc(self.stored[t].sem, 16)

    def setup(self, dve):
        dve.memset(self.power[:], -0.5)

    def statistics(self, dve, b, t):
        dve.wait_ge(self.loaded[t].sem, self.loaded[t].at(b, 16))
        dve.bn_stats(self.stats[:, t, :], self.x[:, t, :]).then_inc(self.stats_made.sem, 1)
        dve.wait_ge(self.stats_made.sem, self.stats_made.at(b, t + 1))
        dve.sem_inc(self.stats_seen, 1)
        dve.bn_aggr(self.mv[:, t, :], self.stats[:, t, :]).then_inc(self.aggregated.sem, 1)
        dve.wait_ge(self.aggregated.sem, self.aggregated.at(b, t + 1))
        dve.tensor_scalar(self.var[:, t:t + 1], self.mv[:, t, 1:2], EPS, None, ALU.add)\
           .then_inc(self.var_made.sem, 1)

    def root(self, pool, b, t):
        pool.wait_ge(self.var_made.sem, self.var_made.at(b, t + 1))
        pool.tensor_tensor(self.rstd[:, t:t + 1], self.var[:, t:t + 1], self.power[:], ALU.pow)\
            .then_inc(self.rstd_made.sem, 1)

    def normalise(self, dve, b, t):
        dve.wait_ge(self.rstd_made.sem, self.rstd_made.at(b, t + 1))
        if t >= 2:
            self.ring.read(dve, b, f"X{t - 2}")
        dve.tensor_scalar(self.xn[:, t % 2, :], self.x[:, t, :], self.mv[:, t, 0:1],
                          self.rstd[:, t:t + 1], ALU.subtract, ALU.mult).then_inc(self.normed.sem, 1)

    def transpose(self, pe, b, t):
        out = self.ring.take(pe, b, f"X{t}")
        pe.wait_ge(self.normed.sem, self.normed.at(b, t + 1))
        for f in range(KD):
            mm = pe.transpose(out[:, f * P:(f + 1) * P], self.xn[:, t % 2, f * P:(f + 1) * P],
                              self.identf[:])
        mm.then_inc(self.ring.is_filled(f"X{t}"), 1)

    def split_hi(self, act, b, t, use="X", done=None):
        dst, done = self.xt, done or self.hi_made
        src = self.ring.read(act, b, f"{use}{t}")[:, 0:D].rearrange("p (f t) -> p f t", f=KD)
        act.copy(dst[:, 0, :, t * P:(t + 1) * P], src).then_inc(done.sem, 1)

    def split_lo(self, dve, b, t, use="X", hi=None):
        hi = hi or self.hi_made
        src = self.ring.read(dve, b, f"{use}{t}")[:, 0:D].rearrange("p (f t) -> p f t", f=KD)
        dve.wait_ge(hi.sem, hi.at(b, t + 1))
        tok = slice(t * P, (t + 1) * P)
        dve.tensor_tensor(self.xt[:, 1, :, tok], src, self.xt[:, 0, :, tok].bitcast(F32), ALU.subtract)\
           .then_inc(self.ring.is_free(f"{use}{t}"), 1)


def passes(pe, out, pairs, start=True, stop=True):
    for i, (w, x) in enumerate(pairs):
        mm = pe.matmul(out, w, x, start=start and i == 0, stop=stop and i == len(pairs) - 1)
    return mm


class Timetable:

    SUB = 5

    def __init__(self, units, plan, head, n_parts):
        self.units, self.n_parts = units, n_parts
        self.cut = self.SUB * (PAIRS // units)
        end = self.SUB * PAIRS
        line = lambda b, lo, hi: [(b, j // self.SUB, j % self.SUB) for j in range(lo, hi)]
        self.plan = plan
        pure = max(head) + 3
        self.head = ([None] * pure + line(0, 0, self.cut), dict(head))
        self.head[1].update({pure + j: [(k, bb, u, t) for k, bb, u, t in plan.get(j, []) if bb == 0]
                             for j in range(self.cut)})
        body = line(0, self.cut, end) + line(1, 0, self.cut)
        tasks = {}
        for pos, (b, s, i) in enumerate(body):
            tasks[pos] = [(k, b + bb, u, t) for k, bb, u, t in plan.get(s * self.SUB + i, [])]
        self.body = (body, tasks)
        n = end - self.cut
        last = {p: [x for x in tasks[p] if x[1] == 0] for p in range(n)}
        for q, x in enumerate(("C0", "C1", "C2", "C3", "O0", "O1", "O2", "O3")):
            last[n + 1 + q] = [(x[0], 0, 0, int(x[1]))]
        self.tail = (body[:n] + [None] * 10, last)

    def names(self, region):
        out = []
        for pos in range(len(region[0])):
            for kind, bb, u, t in region[1].get(pos, []):
                out += [(kind, u, t, p) for p in range(self.n_parts if kind == "T" else 1)]
        return out

    @staticmethod
    def started(region, pos, lag, *kinds):
        return [x for x in region[1].get(pos - lag, []) if x[0] in kinds]


class Banks:

    def __init__(self, phase, name, psum, n, table):
        self.psum, self.n, self.filled, self.freed, self.places, self.base = psum, n, [], [], {}, {}
        self.filled = [phase.semaphore(f"{name}_task_bank{i}_filled") for i in range(n)]
        self.freed = [phase.semaphore(f"{name}_task_bank{i}_freed") for i in range(n)]
        before = [0] * n
        for key, region, times in (("head", table.head, 1), ("body", table.body, BATCH - 1),
                                   ("tail", table.tail, 1)):
            names = table.names(region)
            per = [len(range(i, len(names), n)) for i in range(n)]
            self.base[key] = (list(before), per)
            self.places[key] = {u: (i % n, i // n) for i, u in enumerate(names)}
            before = [x + times * p for x, p in zip(before, per)]

    def _at(self, where, use):
        key, b = where
        bank, nth = self.places[key][use]
        base, per = self.base[key]
        return bank, b * per[bank] + (base[bank] + nth)

    def take(self, pe, where, use):
        bank, n = self._at(where, use)
        pe.wait_ge(self.freed[bank], n + 1)
        return self.psum[:, bank, :]

    def read(self, eng, where, use):
        bank, n = self._at(where, use)
        eng.wait_ge(self.filled[bank], n + 1)
        return self.psum[:, bank, :]

    def emptied(self, eng, where, use):
        bank, n = self._at(where, use)
        eng.wait_ge(self.freed[bank], n + 2)

    def all_emptied(self, eng, where, uses, take=None):
        skip = None if take is None else self.places[where[0]][take][0]
        last = {self.places[where[0]][u][0]: u for u in sorted(uses, key=lambda u: self.places[where[0]][u][1])}
        for bank, use in last.items():
            if bank != skip:
                self.emptied(eng, where, use)

    def is_filled(self, where, use):
        return self.filled[self._at(where, use)[0]]

    def is_free(self, where, use):
        return self.freed[self._at(where, use)[0]]


def attention(nc, phase, name, consts, x_dram, y_dram, w_dram, kv_heads, units, plan, head,
              rope_dram=None, bias_dram=None, biassel_dram=None):
    identf, identb, mask_qk, mask_kq = consts
    rope, biased = rope_dram is not None, bias_dram is not None
    rep = HEADS // kv_heads
    HU, KU = HEADS // units, kv_heads // units
    NQ, NKV = HU * HD, KU * HD
    NU = NQ + 2 * NKV
    OO = units * NU
    WN = OO + D
    NST = HU + KU
    TPARTS = -(-NST // 8)
    STEPS = PAIRS // units
    SUB = Timetable.SUB
    EW = 512
    table = Timetable(units, plan, head, TPARTS)
    HI, LO = 0, 1
    SLOT_HI, SLOT_MID, Q_LO, K_LO = 2, 3, 5, 1

    with ExitStack() as ctx:
        sb = lambda n, s, d: ctx.enter_context(nc.sbuf_tensor(f"{name}_{n}", s, d))
        sem = lambda n: phase.semaphore(f"{name}_{n}")
        scores = ctx.enter_context(nc.psum_tensor(f"{name}_scores", [P, 3, EW], F32))
        maxima = ctx.enter_context(nc.psum_tensor(f"{name}_maxima", [P, 2, EW], F32))
        av = ctx.enter_context(nc.psum_tensor(f"{name}_av", [P, EW], F32))
        banks = Banks(phase, name, ctx.enter_context(nc.psum_tensor(f"{name}_tasks", [P, 2, 512], F32)),
                      2, table)
        x = sb("x", [P, NT, D], F32)
        res = sb("res", [P, 2, D], F32)
        xt = sb("xt", [P, 2, KD, T], F32R)
        ct = sb("ct", [P, 2, KD, T], F32R)
        cx = sb("ctx", [P, NT, D], F32)
        w = sb("w", [P, 2, KD, WN], F32R)
        stacks = sb("stacks", [ROWS, 2, NST, T], BF16)
        v = sb("v", [P, 2, NT, KU, VW], BF16)
        staged = sb("staged", [P, NT, NST, PARTS, HD], BF16)
        rest = sb("rest", [P, 2, NU], F32)
        stats = sb("stats", [P, NT, 6], F32)
        mv = sb("mv", [P, NT, 2], F32)
        var = sb("var", [P, NT], F32)
        rstd = sb("rstd", [P, NT], F32)
        power = sb("power", [P, 1], F32)
        nmax = sb("nmax", [P, 2, NT, 2], F32)
        nrest = sb("nrest", [P, 2, NT, 2], F32)
        nparts = sb("nparts", [P, 2, NT, 2, 4], BF16)
        osum = sb("osum", [P, 2, 8, HD], F32)
        rden = sb("rden", [P, 2, 8], F32)
        region = sb("region", [P, 4 * EW + 2 * PCOLS], F32)
        pf = region[:, 0:4 * EW].rearrange("p (i n) -> p i n", i=4)
        ph = region[:, 4 * EW:4 * EW + PCOLS].bitcast(F16).rearrange("p (i n) -> p i n", i=2)
        pl = region[:, 4 * EW + PCOLS:].bitcast(F16).rearrange("p (i n) -> p i n", i=2)
        wraw = region[:, 0:2 * WN].rearrange("p (i n) -> p i n", i=2)
        if rope:
            trig = sb("trig", [P, NT, 2, HD], F32)
            turned = sb("turned", [P, 2, NQ + NKV], F32)
        if biased:
            biasraw, biashi = region[:, 2 * WN:2 * WN + D], region[:, 2 * WN + D:2 * WN + 2 * D]
            selraw = region[:, 2 * WN + 2 * D:2 * WN + 2 * D + (units + 1) * P + 1]
            bias = sb("bias", [P, D], F32R)
            sel = sb("sel", [P, units + 1, P], F32R)

        w_loaded = [sem(f"w{i}_loaded") for i in range(2)]
        w_hi_made, w_lo_made = sem("w_hi_made"), sem("w_lo_made")
        extra_loaded, extra_hi, extra_made = sem("extra_loaded"), sem("extra_hi"), sem("extra_made")
        ones_set, shift_set, bias_cleared = sem("ones_set"), sem("shift_set"), sem("bias_cleared")
        UT = units * NT
        x_loaded = [Signal(sem(f"x{t}_loaded"), 16) for t in range(NT)]
        res_loaded = [Signal(sem(f"res{i}_loaded"), 32) for i in range(2)]
        stored = [Signal(sem(f"y{i}_stored"), 32, 16) for i in range(2)]
        stats_made = Signal(sem("stats_made"), NT)
        stats_seen = sem("stats_seen")
        aggregated = Signal(sem("aggregated"), NT)
        var_made = Signal(sem("var_made"), NT)
        rstd_made = Signal(sem("rstd_made"), NT)
        normed = Signal(sem("normed"), NT)
        xhi_made = Signal(sem("xhi_made"), NT)
        chi_made = Signal(sem("chi_made"), NT)
        rope_products = Signal(sem("rope_products"), UT)
        roped = Signal(sem("roped"), UT)
        qk_hi = Signal(sem("qk_hi"), UT)
        v_hi = Signal(sem("v_hi"), UT)
        qk_rest = Signal(sem("qk_rest"), UT)
        mid_made = Signal(sem("mid_made"), UT)
        low_made = Signal(sem("low_made"), UT, 2)
        replicated = Signal(sem("replicated"), UT)
        nmax_chain = Signal(sem("nmax_chain"), 3 * PAIRS)
        nmax_split = Signal(sem("nmax_split"), PAIRS)
        SB = [2, 2, 1]
        scores_filled = [Signal(sem(f"scores{i}_filled"), SB[i] * PAIRS) for i in range(3)]
        scores_freed = [Signal(sem(f"scores{i}_freed"), SB[i] * PAIRS, 1) for i in range(3)]
        MB = [3, 3]
        maxima_filled = [Signal(sem(f"maxima{i}_filled"), MB[i] * PAIRS) for i in range(2)]
        maxima_freed = [Signal(sem(f"maxima{i}_freed"), MB[i] * PAIRS, 1) for i in range(2)]
        plo_made = Signal(sem("plo_made"), SUB * PAIRS, 4)
        av_made = Signal(sem("av_made"), PAIRS, 2)
        av_read = Signal(sem("av_read"), PAIRS, 3)
        rows_filled = Signal(sem("rows_filled"), PAIRS)
        rows_made = Signal(sem("rows_made"), PAIRS)
        ctx_made = Signal(sem("ctx_made"), PAIRS)

        def split_cols(ap):
            return ap.rearrange("p (h d) -> p h d", d=HD)

        def unit(s):
            return s // STEPS

        def heads(s, i):
            h = 2 * (s % STEPS) + i
            return h, HU + h // rep, h // rep

        ACT_PARTS = [tuple(p for p in range(TPARTS) if p % 2 == 1) for t in range(NT)]
        DVE_PARTS = [tuple(p for p in range(TPARTS) if p % 2 == 0) for t in range(NT)]

        def stack_out(copy, eng, where, u, t, p):
            n = min(8, NST - 8 * p)
            src = banks.read(eng, where, ("T", u, t, p)).bitcast(BF16)[0:STK, 0:n * P]
            copy(stacks[0:STK, u % 2, 8 * p:8 * p + n, t * P:(t + 1) * P],
                 src.rearrange("p (h t) -> p h t", t=P)).then_inc(banks.is_free(where, ("T", u, t, p)), 1)

        MAXIMA_AT = ((1, (5,)), (1, ()), (2, (0, 1)), (2, (2, 3)), (2, (4,)))
        TRANSPOSE_AT, ROWS_AT, VALUES_AT, FINISH_AT = 1, 2, 3, 4

        def following(region, b, s, ahead):
            if s + ahead < PAIRS:
                return b, s + ahead
            return (b + 1, s + ahead - PAIRS) if region is table.body else None

        def preceding(region, b, s):
            if s >= 1:
                return b, s - 1
            return (b - 1, PAIRS - 1) if region is table.body else None

        block = ctx.enter_context(nc.Block())

        def whole(eng, part):
            part(table.head, ("head", 0), 0)
            with eng.Fori(0, BATCH - 1) as b:
                part(table.body, ("body", b), b)
            part(table.tail, ("tail", 0), BATCH - 1)

        @block.sync
        def _(sp):
            for i in range(2):
                sp.sem_inc(stored[i].sem, 16)
            for t in range(NT):
                sp.dma_start(x[:, t, :], x_dram[0, t]).then_inc(x_loaded[t].sem, 16)
            for f in range(KD):
                if f >= 2:
                    sp.wait_ge(w_lo_made, f - 1)
                sp.dma_start(wraw[:, f % 2, :], w_dram[:, f, :]).then_inc(w_loaded[f % 2], 16)
            if rope:
                sp.dma_start(trig[:].rearrange("p t a d -> p (t a d)"), rope_dram).then_inc(extra_loaded, 16)
            if biased:
                sp.wait_ge(bias_cleared, 1)
                sp.dma_start(biasraw[0:2 * (units + 1), :], bias_dram).then_inc(extra_loaded, 16)
                sp.dma_start(selraw, biassel_dram).then_inc(extra_loaded, 16)

            def next_tokens(b):
                for t in range(NT):
                    sp.wait_ge(xhi_made.sem, xhi_made.at(b, t + 1))
                    sp.dma_start(x[:, t, :], x_dram[b + 1, t]).then_inc(x_loaded[t].sem, 16)

            def residual(where, b):
                def load(t):
                    sp.wait_ge(stored[t % 2].sem, stored[t % 2].at(b, 16 * (t // 2)))
                    sp.dma_start(res[:, t % 2, :], x_dram[b, t]).then_inc(res_loaded[t % 2].sem, 16)

                load(0)
                load(1)
                for t in range(NT):
                    banks.emptied(sp, where, ("O", 0, t, 0))
                    sp.dma_start(y_dram[b, t], res[:, t % 2, :]).then_inc(stored[t % 2].sem, 16)
                    if t + 2 < NT:
                        load(t + 2)

            with sp.Fori(0, BATCH - 1) as b:
                next_tokens(b)
                residual(("body", b), b)
            residual(("tail", 0), BATCH - 1)
            for i in range(2):
                sp.wait_ge(stored[i].sem, stored[i].at(BATCH, 0))

        @block.gpsimd
        def _(pool):
            ones_rows = slice(MAXROW, ROWS)
            pool.memset(stacks[ones_rows, :, HU:NST, :], 1.0).then_inc(ones_set, 1)
            pool.wait_ge(ones_set, 1)
            pool.memset(v[:, :, :, :, 3 * HD:3 * HD + 1], 1.0).then_inc(ones_set, 1)
            pool.wait_ge(ones_set, 2)

            def part(region, where, b0):
                for pos, step in enumerate(region[0]):
                    for _, bb, _, t in table.started(region, pos + 2, 0, "X"):
                        pool.wait_ge(var_made.sem, var_made.at(b0 + bb, t + 1))
                        pool.tensor_tensor(rstd[:, t:t + 1], var[:, t:t + 1], power[:], ALU.pow)\
                            .then_inc(rstd_made.sem, 1)
                    for _, bb, u, t in table.started(region, pos, 4 if rope else 3, "P"):
                        k = u * NT + t
                        r = rest[:, k % 2, :]
                        pool.wait_ge(mid_made.sem, mid_made.at(b0 + bb, k + 1))
                        pool.tensor_tensor(staged[:, t, 0:HU, Q_LO, :], split_cols(r[:, 0:NQ]),
                                           staged[:, t, 0:HU, SLOT_MID, :], ALU.subtract)
                        pool.tensor_tensor(staged[:, t, HU:NST, K_LO, :], split_cols(r[:, NQ:NQ + NKV]),
                                           staged[:, t, HU:NST, SLOT_MID, :], ALU.subtract)
                        pool.tensor_tensor(v[:, u % 2, t, :, 2 * HD:3 * HD], split_cols(r[:, NQ + NKV:NU]),
                                           v[:, u % 2, t, :, HD:2 * HD], ALU.subtract)\
                            .then_inc(low_made.sem, 1)
                    if step is not None:
                        bs, s, i = step
                        b = b0 + bs
                        n = SUB * s + i
                        cols = slice(i * EW, (i + 1) * EW)
                        sbk, nth = i % 3, SB[i % 3] * s + i // 3
                        pool.wait_ge(scores_freed[sbk].sem, scores_freed[sbk].at(b, nth + 1))
                        pool.tensor_tensor(pl[:, s % 2, cols], pf[:, n % 4, :], ph[:, s % 2, cols],
                                           ALU.subtract).then_inc(plo_made.sem, 1)

            whole(pool, part)

        @block.scalar
        def _(act):
            for sems in (banks.freed, [f.sem for f in scores_freed + maxima_freed]):
                for one in sems:
                    act.sem_inc(one, 1)
            act.sem_inc(av_read.sem, 3)
            act.sem_inc(low_made.sem, 2)
            act.sem_inc(plo_made.sem, 4)
            act.sem_inc(av_made.sem, 2)
            for f in range(KD):
                act.wait_ge(w_loaded[f % 2], 16 * (f // 2 + 1))
                act.copy(w[:, HI, f, :], wraw[:, f % 2, :]).then_inc(w_hi_made, 1)
            if biased:
                act.wait_ge(extra_loaded, 32)
                act.copy(biashi.bitcast(F32R), biasraw)
                act.copy(sel[:].rearrange("p a n -> p (a n)"), selraw[:, 0:(units + 1) * P])\
                   .then_inc(extra_hi, 1)
                act.wait_ge(extra_made, 1)
            act.wait_ge(w_lo_made, KD)

            def part(region, where, b0):
                for pos, step in enumerate(region[0]):
                    for kind, bb, _, t in table.started(region, pos, 1, "X", "C"):
                        src = banks.read(act, where, (kind, 0, t, 0)).rearrange("p (f t) -> p f t", f=KD)
                        dst, made = (xt, xhi_made) if kind == "X" else (ct, chi_made)
                        act.copy(dst[:, HI, :, t * P:(t + 1) * P], src).then_inc(made.sem, 1)
                    for _, bb, u, t in table.started(region, pos, 1, "P"):
                        psum = banks.read(act, where, ("P", u, t, 0))
                        if not rope:
                            act.copy(staged[:, t, :, SLOT_HI, :], split_cols(psum[:, 0:NQ + NKV]))\
                               .then_inc(qk_hi.sem, 1)
                        act.copy(v[:, u % 2, t, :, 0:HD], split_cols(psum[:, NQ + NKV:NU]))\
                           .then_inc(v_hi.sem, 1)
                    if rope:
                        for _, bb, u, t in table.started(region, pos, 2, "P"):
                            k = u * NT + t
                            act.wait_ge(roped.sem, roped.at(b0 + bb, k + 1))
                            act.copy(staged[:, t, :, SLOT_HI, :], split_cols(rest[:, k % 2, 0:NQ + NKV]))\
                               .then_inc(qk_hi.sem, 1)
                    for _, bb, u, t in table.started(region, pos, 3 if rope else 2, "P"):
                        k = u * NT + t
                        act.wait_ge(qk_rest.sem, qk_rest.at(b0 + bb, k + 1))
                        act.copy(staged[:, t, :, SLOT_MID, :], split_cols(rest[:, k % 2, 0:NQ + NKV]))
                        banks.emptied(act, where, ("P", u, t, 0))
                        act.copy(v[:, u % 2, t, :, HD:2 * HD], split_cols(rest[:, k % 2, NQ + NKV:NU]))\
                           .then_inc(mid_made.sem, 1)
                    for _, bb, u, t in table.started(region, pos, 1, "T"):
                        for p in ACT_PARTS[t]:
                            stack_out(act.copy, act, where, u, t, p)
                    if step is not None:
                        bs, s, i = step
                        b = b0 + bs
                        n = SUB * s + i
                        sbk, nth = i % 3, SB[i % 3] * s + i // 3
                        cols = slice(i * EW, (i + 1) * EW)
                        act.wait_ge(plo_made.sem, plo_made.at(b, n - 3))
                        act.wait_ge(scores_filled[sbk].sem, scores_filled[sbk].at(b, nth + 1))
                        act.activation(pf[:, n % 4, :], scores[:, sbk, :], ACT.Exp, scale=0.25)
                        if i == 0:
                            act.wait_ge(av_made.sem, av_made.at(b, s - 1))
                        act.activation(ph[:, s % 2, cols], scores[:, sbk, :], ACT.Exp, scale=0.25)\
                           .then_inc(scores_freed[sbk].sem, 1)

            whole(act, part)

        @block.vector
        def _(dve):
            dve.memset(power[:], -0.5)
            if biased:
                dve.memset(biasraw, 0.0).then_inc(bias_cleared, 1)
            dve.memset(stacks[MAXROW:ROWS, :, 0:HU, :], SHIFT).then_inc(shift_set, 1)
            for f in range(KD):
                dve.wait_ge(w_hi_made, f + 1)
                dve.tensor_tensor(w[:, LO, f, :], wraw[:, f % 2, :], w[:, HI, f, :].bitcast(F32),
                                  ALU.subtract).then_inc(w_lo_made, 1)
            if biased:
                dve.wait_ge(extra_hi, 1)
                dve.scalar_tensor_tensor(out=bias[:], in0=biashi, scalar=selraw[:, (units + 1) * P:],
                                         in1=biasraw, op0=ALU.mult, op1=ALU.add).then_inc(extra_made, 1)
            if rope:
                dve.wait_ge(extra_loaded, 16)

            def statistics(b, t):
                dve.wait_ge(x_loaded[t].sem, x_loaded[t].at(b, 16))
                dve.bn_stats(stats[:, t, :], x[:, t, :]).then_inc(stats_made.sem, 1)
                dve.wait_ge(stats_made.sem, stats_made.at(b, t + 1))
                dve.sem_inc(stats_seen, 1)
                dve.bn_aggr(mv[:, t, :], stats[:, t, :]).then_inc(aggregated.sem, 1)
                dve.wait_ge(aggregated.sem, aggregated.at(b, t + 1))
                dve.tensor_scalar(var[:, t:t + 1], mv[:, t, 1:2], EPS, None, ALU.add)\
                   .then_inc(var_made.sem, 1)

            def normalise(b, t):
                dve.wait_ge(rstd_made.sem, rstd_made.at(b, t + 1))
                dve.tensor_scalar(x[:, t, :], x[:, t, :], mv[:, t, 0:1], rstd[:, t:t + 1],
                                  ALU.subtract, ALU.mult).then_inc(normed.sem, 1)

            def rotate(where, b, u, t):
                k, n = u * NT + t, NST
                q = banks.read(dve, where, ("P", u, t, 0))[:, 0:NQ + NKV]
                q = q.rearrange("p (h a d) -> p h a d", a=2, d=HD // 2)
                shape = [P, n, HD // 2]
                ta = turned[:, 0, :].rearrange("p (h a d) -> p h a d", a=2, d=HD // 2)
                tb = turned[:, 1, :].rearrange("p (h a d) -> p h a d", a=2, d=HD // 2)
                dve.wait_ge(low_made.sem, low_made.at(b, k - 1))
                for a in range(2):
                    half = slice(a * HD // 2, (a + 1) * HD // 2)
                    dve.tensor_tensor(ta[:, :, a, :], q[:, :, a, :],
                                      trig[:, t, 0:1, half].broadcast_to(shape), ALU.mult)
                    last = dve.tensor_tensor(tb[:, :, a, :], q[:, :, 1 - a, :],
                                             trig[:, t, 1:2, half].broadcast_to(shape), ALU.mult)
                last.then_inc(rope_products.sem, 1)
                dve.wait_ge(rope_products.sem, rope_products.at(b, k + 1))
                dve.tensor_tensor(rest[:, k % 2, 0:NQ + NKV], turned[:, 0, :], turned[:, 1, :],
                                  ALU.add).then_inc(roped.sem, 1)

            def remainder(where, b, u, t):
                k = u * NT + t
                dst = rest[:, k % 2, 0:NQ + NKV]
                if rope:
                    src = dst
                else:
                    src = banks.read(dve, where, ("P", u, t, 0))[:, 0:NQ + NKV]
                    dve.wait_ge(low_made.sem, low_made.at(b, k - 1))
                dve.wait_ge(qk_hi.sem, qk_hi.at(b, k + 1))
                dve.tensor_tensor(split_cols(dst), split_cols(src), staged[:, t, :, SLOT_HI, :],
                                  ALU.subtract).then_inc(qk_rest.sem, 1)

            def value_remainder(where, b, u, t):
                k = u * NT + t
                src = banks.read(dve, where, ("P", u, t, 0))[:, NQ + NKV:NU]
                dve.tensor_tensor(split_cols(rest[:, k % 2, NQ + NKV:NU]), split_cols(src),
                                  v[:, u % 2, t, :, 0:HD], ALU.subtract)\
                   .then_inc(banks.is_free(where, ("P", u, t, 0)), 1)

            def replicate(b, u, t):
                k = u * NT + t
                dve.wait_ge(mid_made.sem, mid_made.at(b, k + 1))
                st = staged[:, t]
                hi, mid = st[:, :, SLOT_HI:SLOT_HI + 1, :], st[:, :, SLOT_MID, :]
                dve.tensor_copy(st[:, 0:HU, 0:2, :], hi[:, 0:HU].broadcast_to([P, HU, 2, HD]))
                dve.tensor_copy(st[:, 0:HU, 4, :], mid[:, 0:HU])
                dve.tensor_copy(st[:, HU:NST, 4:6, :], hi[:, HU:NST].broadcast_to([P, KU, 2, HD]))
                dve.tensor_copy(st[:, HU:NST, 0, :], mid[:, HU:NST]).then_inc(replicated.sem, 1)

            def reduce_max(b, s, k):
                mb, nth = k % 2, MB[k % 2] * s + k // 2
                dve.wait_ge(maxima_filled[mb].sem, maxima_filled[mb].at(b, nth + 1))
                nm, h, src = nmax[:, s % 2], k % 2, maxima[:, mb, :]
                if k < 2:
                    dve.tensor_reduce(nm[:, 0, h:h + 1], src[:, 0:P], AX_X, ALU.max, negate=True)
                    last = dve.tensor_reduce(nm[:, 1, h:h + 1], src[:, P:3 * P], AX_X, ALU.max, negate=True)
                else:
                    qt = 1 + k // 2
                    last = dve.tensor_reduce(nm[:, qt, h:h + 1], src[:, 0:(qt + 1) * P], AX_X, ALU.max,
                                             negate=True)
                last.then_inc(maxima_freed[mb].sem, 1)

            def split_max(b, s):
                nm, nr, np_ = nmax[:, s % 2], nrest[:, s % 2], nparts[:, s % 2]
                dve.wait_ge(maxima_freed[1].sem, maxima_freed[1].at(b, MB[1] * (s + 1)))
                dve.tensor_copy(np_[:, :, :, 0], nm).then_inc(nmax_chain.sem, 1)
                dve.wait_ge(nmax_chain.sem, nmax_chain.at(b, 3 * s + 1))
                dve.tensor_tensor(nr, nm, np_[:, :, :, 0], ALU.subtract).then_inc(nmax_chain.sem, 1)
                dve.wait_ge(nmax_chain.sem, nmax_chain.at(b, 3 * s + 2))
                dve.tensor_copy(np_[:, :, :, 1], nr).then_inc(nmax_chain.sem, 1)
                dve.wait_ge(nmax_chain.sem, nmax_chain.at(b, 3 * s + 3))
                dve.tensor_tensor(np_[:, :, :, 2], nr, np_[:, :, :, 1], ALU.subtract)\
                   .then_inc(nmax_split.sem, 1)

            def max_rows(b, s):
                dve.wait_ge(rows_filled.sem, rows_filled.at(b, s + 1))
                src = av[MAXROW:MAXROW + 3, :].bitcast(BF16)
                h, _, _ = heads(s, 0)
                dve.tensor_copy(stacks[MAXROW:MAXROW + 3, unit(s) % 2, h:h + 2, :],
                                src.rearrange("p (h t) -> p h t", t=T)).then_inc(rows_made.sem, 1)

            def finish(b, s):
                dve.wait_ge(av_made.sem, av_made.at(b, s + 1))
                a = av[:, 0:8 * VW].rearrange("p (g c) -> p g c", c=VW)
                dve.tensor_reduce(osum[:, s % 2], a[:, :, 0:3 * HD].rearrange("p g (s d) -> p g d s", s=3),
                                  AX_X, ALU.add)
                dve.reciprocal(rden[:, s % 2, :], a[:, :, 3 * HD]).then_inc(av_read.sem, 1)
                dve.wait_ge(av_read.sem, av_read.at(b, s + 1))
                dst = cx[:, :, 2 * s * HD:(2 * s + 2) * HD].rearrange("p t (h d) -> p t h d", d=HD)
                src = osum[:, s % 2].rearrange("p (t h) d -> p t h d", h=2)
                rd = rden[:, s % 2, :].rearrange("p (t h) -> p t h", h=2).unsqueeze(3)\
                    .broadcast_to([P, NT, 2, HD])
                dve.tensor_tensor(dst, src, rd, ALU.mult).then_inc(ctx_made.sem, 1)

            def part(region, where, b0):
                for pos, step in enumerate(region[0]):
                    for _, bb, _, t in table.started(region, pos + 3, 0, "X"):
                        statistics(b0 + bb, t)
                    for _, bb, _, t in table.started(region, pos + 1, 0, "X"):
                        normalise(b0 + bb, t)
                    for kind, bb, _, t in table.started(region, pos, 1, "X", "C"):
                        src = banks.read(dve, where, (kind, 0, t, 0)).rearrange("p (f t) -> p f t", f=KD)
                        dst, made = (xt, xhi_made) if kind == "X" else (ct, chi_made)
                        dve.wait_ge(made.sem, made.at(b0 + bb, t + 1))
                        tok = slice(t * P, (t + 1) * P)
                        dve.tensor_tensor(dst[:, LO, :, tok], src, dst[:, HI, :, tok].bitcast(F32),
                                          ALU.subtract).then_inc(banks.is_free(where, (kind, 0, t, 0)), 1)
                    for _, bb, _, t in table.started(region, pos, 1, "O"):
                        y = banks.read(dve, where, ("O", 0, t, 0))
                        dve.wait_ge(res_loaded[t % 2].sem, res_loaded[t % 2].at(b0 + bb, 16 * (t // 2 + 1)))
                        dve.tensor_tensor(res[:, t % 2, :], y, res[:, t % 2, :], ALU.add)\
                           .then_inc(banks.is_free(where, ("O", 0, t, 0)), 1)
                    for _, bb, u, t in table.started(region, pos, 1, "P"):
                        dve.wait_ge(v_hi.sem, v_hi.at(b0 + bb, u * NT + t + 1))
                        if rope:
                            rotate(where, b0 + bb, u, t)
                        else:
                            remainder(where, b0 + bb, u, t)
                        value_remainder(where, b0 + bb, u, t)
                    if rope:
                        for _, bb, u, t in table.started(region, pos, 2, "P"):
                            remainder(where, b0 + bb, u, t)
                    for _, bb, u, t in table.started(region, pos, 4 if rope else 3, "P"):
                        replicate(b0 + bb, u, t)
                    for _, bb, u, t in table.started(region, pos, 1, "T"):
                        for p in DVE_PARTS[t]:
                            stack_out(dve.tensor_copy, dve, where, u, t, p)
                    if step is None:
                        if region is table.head and region[0][pos + 1] is not None:
                            for k in range(6):
                                reduce_max(0, 0, k)
                            split_max(0, 0)
                            max_rows(0, 0)
                            for k in range(5):
                                reduce_max(0, 1, k)
                        if region is table.tail and region[0][pos - 1] is not None:
                            finish(b0, PAIRS - 1)
                        continue
                    bs, s, i = step
                    b = b0 + bs
                    if i == ROWS_AT and (after := following(region, b, s, 1)) is not None:
                        max_rows(*after)
                    ahead, ks = MAXIMA_AT[i]
                    if (after := following(region, b, s, ahead)) is not None:
                        for k in ks:
                            reduce_max(*after, k)
                            if k == 5:
                                split_max(*after)
                    if i == FINISH_AT and (before := preceding(region, b, s)) is not None:
                        finish(*before)

            whole(dve, part)

        @block.tensor
        def _(pe):
            THREE = ((HI, HI), (LO, HI), (HI, LO))
            pe.wait_ge(ones_set, 2)
            pe.wait_ge(shift_set, 1)

            def project(out, src, t, c0, n, bias_row):
                tok = slice(t * P, (t + 1) * P)
                pairs = [(src[:, a, f, tok], w[:, c, f, c0:c0 + n]) for f in range(KD) for a, c in THREE]
                if biased:
                    pairs.append((sel[:, bias_row, :], bias[:, 0:n]))
                return passes(pe, out, pairs)

            def block_scores(out, lhs, rhs, mask, diag):
                pe.matmul(out, lhs, rhs, start=True, stop=False, skip_group_check=True)
                return pe.matmul(out[:, diag:diag + P], identb[:], mask[:], start=False, stop=True,
                                 skip_group_check=True)

            def max_scores(b, s, k):
                mb, nth = k % 2, MB[k % 2] * s + k // 2
                pe.wait_ge(maxima_freed[mb].sem, maxima_freed[mb].at(b, nth))
                st, (h, hk, _) = stacks[:, unit(s) % 2], heads(s, k % 2)
                for qt in ((0, 1) if k < 2 else (1 + k // 2,)):
                    n, at = (qt + 1) * P, P if qt == 1 else 0
                    mm = block_scores(maxima[:, mb, at:at + n], st[0:STK, h, qt * P:(qt + 1) * P],
                                      st[0:STK, hk, 0:n], mask_qk, qt * P)
                mm.then_inc(maxima_filled[mb].sem, 1)

            def max_transposes(b, s):
                pe.wait_ge(av_read.sem, av_read.at(b, s - 2))
                pe.wait_ge(nmax_split.sem, nmax_split.at(b, s + 1))
                out = av[MAXROW:MAXROW + 3, :].bitcast(BF16)
                for i in range(2):
                    for qt in range(NT):
                        c = i * T + qt * P
                        mm = pe.transpose(out[:, c:c + P], nparts[:, s % 2, qt, i, 0:3], identb[:])
                mm.then_inc(rows_filled.sem, 1)

            def exp_scores(b, s, i):
                sbk, nth = i % 3, SB[i % 3] * s + i // 3
                pe.wait_ge(scores_freed[sbk].sem, scores_freed[sbk].at(b, nth))
                if i == 0:
                    pe.wait_ge(rows_made.sem, rows_made.at(b, s + 1))
                st = stacks[:, unit(s) % 2]
                for kb, hh, at in (((0, 0, 0),), ((0, 1, 0),), ((1, 0, 0), (3, 0, 384)),
                                   ((1, 1, 0), (3, 1, 384)), ((2, 0, 0), (2, 1, 256)))[i]:
                    h, hk, _ = heads(s, hh)
                    n = T - kb * P
                    mm = block_scores(scores[:, sbk, at:at + n], st[:, hk, kb * P:(kb + 1) * P],
                                      st[:, h, kb * P:T], mask_kq, 0)
                mm.then_inc(scores_filled[sbk].sem, 1)

            def values(b, s, rows_out):
                if rows_out:
                    pe.wait_ge(rows_made.sem, rows_made.at(b, s + 3))
                pe.wait_ge(plo_made.sem, plo_made.at(b, SUB * (s + 1)))
                pe.wait_ge(av_read.sem, av_read.at(b, s))
                for qt in range(NT):
                    for i in range(2):
                        c = (2 * qt + i) * VW
                        pairs = []
                        for kb in range(qt + 1):
                            at = (i * 512 + qt * P, 1024 + i * 512 + (qt - 1) * P,
                                  2048 + i * 256 + (qt - 2) * P, 1024 + i * 512 + 384)[kb]
                            vh = v[:, unit(s) % 2, kb, heads(s, i)[2], 0:3 * HD + 1]
                            pairs += [(ph[:, s % 2, at:at + P], vh), (pl[:, s % 2, at:at + P], vh)]
                        mm = passes(pe, av[:, c:c + 3 * HD + 1], pairs)
                mm.then_inc(av_made.sem, 1)

            def transposes(where, b, kind, t):
                out = banks.take(pe, where, (kind, 0, t, 0))
                if kind == "X":
                    pe.wait_ge(normed.sem, normed.at(b, t + 1))
                else:
                    pe.wait_ge(ctx_made.sem, ctx_made.at(b, PAIRS))
                src = x if kind == "X" else cx
                for f in range(KD):
                    mm = pe.transpose(out[:, f * P:(f + 1) * P], src[:, t, f * P:(f + 1) * P], identf[:])
                mm.then_inc(banks.is_filled(where, (kind, 0, t, 0)), 1)

            def part(region, where, b0):
                for pos, step in enumerate(region[0]):
                    if step is not None:
                        bs, s, i = step
                        b = b0 + bs
                        exp_scores(b, s, i)
                        if i == TRANSPOSE_AT and (after := following(region, b, s, 1)) is not None:
                            max_transposes(*after)
                        ahead, ks = MAXIMA_AT[i]
                        if (after := following(region, b, s, ahead)) is not None:
                            if 0 in ks and after[1] % STEPS == 0:
                                banks.all_emptied(pe, where, [("T", unit(after[1]), t, p)
                                                              for t in range(NT) for p in range(TPARTS)])
                            for k in ks:
                                max_scores(*after, k)
                        if i == VALUES_AT and (before := preceding(region, b, s)) is not None:
                            values(*before, following(region, b, s, 1) is not None)
                    for kind, bb, u, t in table.started(region, pos, 0, "X", "C", "P", "O", "T"):
                        bt = b0 + bb
                        if kind in "XC":
                            transposes(where, bt, kind, t)
                        elif kind == "P":
                            out = banks.take(pe, where, ("P", u, t, 0))
                            if u == 0:
                                if region is table.head and t == 0:
                                    pe.wait_ge(w_lo_made, KD)
                                    if biased:
                                        pe.wait_ge(extra_made, 1)
                                banks.all_emptied(pe, where, [("X", 0, t, 0)], take=("P", u, t, 0))
                            project(out[:, 0:NU], xt, t, u * NU, NU, u)\
                                .then_inc(banks.is_filled(where, ("P", u, t, 0)), 1)
                        elif kind == "O":
                            out = banks.take(pe, where, ("O", 0, t, 0))
                            banks.all_emptied(pe, where, [("C", 0, t, 0)], take=("O", 0, t, 0))
                            project(out, ct, t, OO, D, units)\
                                .then_inc(banks.is_filled(where, ("O", 0, t, 0)), 1)
                        else:
                            k = u * NT + t
                            pe.wait_ge(replicated.sem, replicated.at(bt, k + 1))
                            pe.wait_ge(low_made.sem, low_made.at(bt, k + 1))
                            for p in range(TPARTS):
                                out = banks.take(pe, where, ("T", u, t, p)).bitcast(BF16)
                                for h in range(min(8, NST - 8 * p)):
                                    src = staged[:, t, 8 * p + h].rearrange("p s d -> p (s d)")
                                    mm = pe.transpose(out[0:STK, h * P:(h + 1) * P], src, identb[:])
                                mm.then_inc(banks.is_filled(where, ("T", u, t, p)), 1)
                    if step is None:
                        if region is table.head and region[0][pos + 1] is not None:
                            banks.all_emptied(pe, where, [("T", 0, t, p)
                                                          for t in range(NT) for p in range(TPARTS)])
                            for k in range(6):
                                max_scores(0, 0, k)
                            max_transposes(0, 0)
                            for k in range(5):
                                max_scores(0, 1, k)
                        if region is table.tail and region[0][pos - 1] is not None:
                            values(b0, PAIRS - 1, False)

            whole(pe, part)


def ffn(nc, phase, name, consts, x_dram, y_dram, gate_dram, up_dram, down_dram, scales_dram, dscale_dram, xa_dram,
        gb_dram, ub_dram, da_dram, db_dram):
    identf = consts[0]
    uses = [f"X{t}" for t in range(NT)] + ["A"]
    for n in range(NI):
        uses += [f"G{n}", f"U{n}"]
    uses += ["Y0", "DA"] + [f"Y{t}" for t in range(1, NT)]
    HI, LO = 0, 1

    with ExitStack() as ctx:
        sb = lambda n, s, d: ctx.enter_context(nc.sbuf_tensor(f"{name}_{n}", s, d))
        sem = lambda n: phase.semaphore(f"{name}_{n}")
        ring = Ring(ctx, phase, nc, name, uses)
        norm = Norm(ctx, phase, nc, name, ring, identf, x_dram)
        xt = norm.xt
        codes = sb("codes", [P, 2, KD, INTER], F32R)
        dcodes = sb("dcodes", [P, NI, D], F32R)
        raw = sb("raw", [P, 2, INTER], I32)
        scales = sb("scales", [P, 2, NI], F32)
        dscale = sb("dscale", [P, D], F32)
        xa_raw = sb("xa_raw", [P, KD * 2 * RANK], F32)
        xa = sb("xa", [P, 2, KD, 2 * RANK], F32R)
        da_raw = sb("da_raw", [P, NI * RANK], F32)
        da = sb("da", [P, 2, NI, RANK], F32R)
        lr_b = [sb(f"{k}_b", [3 * RANK, c], F32R) for k, c in (("gate", INTER), ("up", INTER), ("down", D))]
        lr_x = [sb(f"{k}_x", [3 * RANK, T], F32R) for k in ("gate", "up", "down")]
        ht = sb("ht", [P, 2, NI, T], F32R)
        work = sb("work", [P, 11 * T], F32)
        gate = work[:, 0:T]
        scaled, sig, upv, hid, ysum = (
            work[:, (2 * i + 1) * T:(2 * i + 3) * T].rearrange("p (a t) -> p a t", a=2) for i in range(5))

        raw_loaded = [sem(f"raw{i}_loaded") for i in range(2)]
        raw_used = sem("raw_used")
        small_loaded = sem("small_loaded")
        b_loaded = sem("b_loaded")
        small_hi = sem("small_hi")
        small_made = sem("small_made")
        b_scaled, b_hi, b_made = sem("b_scaled"), sem("b_hi"), sem("b_made")
        cleared = sem("cleared")
        lrx_hi = Signal(sem("lowrank_hi"), 2)
        p1_scaled = Signal(sem("scaled"), 2 * NI)
        silu_made = Signal(sem("silu_made"), NI)
        hid_made = Signal(sem("hid_made"), NI)
        hid_hi = Signal(sem("hid_hi"), NI)
        hid_lo = Signal(sem("hid_lo"), NI, 2)
        y_part = Signal(sem("y_part"), 2 * NT)

        def rows(n):
            return P if n < NI - 1 else LAST

        def lr_raw(j):
            return work[0:3 * RANK, (0, INTER, 2 * INTER)[j]:(INTER, 2 * INTER, 2 * INTER + D)[j]]

        chunks = [(s, codes[:, j, f, :], s[:, f, :], INTER) for f in range(KD)
                  for j, s in ((0, gate_dram), (1, up_dram))]
        for n in range(0, NI, 2):
            k = min(2, NI - n)
            chunks.append((down_dram, dcodes[:, n:n + k, :].rearrange("p n d -> p (n d)"),
                           down_dram[:, n * D:(n + k) * D], k * D))

        X_LO = (1, 2, 1)
        B_LO = (2, 1, 2)

        block = ctx.enter_context(nc.Block())

        @block.sync
        def _(sp):
            norm.credits(sp)
            for i, (_, _, src, c) in enumerate(chunks):
                if i >= 2:
                    sp.wait_ge(raw_used, i - 1)
                sp.dma_start(raw[:, i % 2, 0:c], src).then_inc(raw_loaded[i % 2], 16)
                if i == 1:
                    sp.dma_start(scales[:].rearrange("p a n -> p (a n)"), scales_dram)\
                      .then_inc(small_loaded, 16)
                    sp.dma_start(dscale[:], dscale_dram.broadcast_to([P, D])).then_inc(small_loaded, 16)
                    sp.dma_start(xa_raw[:], xa_dram).then_inc(small_loaded, 16)
                    sp.dma_start(da_raw[:], da_dram).then_inc(small_loaded, 16)
                    for r in range(3):
                        q = slice(r * RANK, (r + 1) * RANK)
                        for j, (d, c2) in enumerate(((gb_dram, INTER), (ub_dram, INTER), (db_dram, D))):
                            sp.dma_start(lr_raw(j)[q, 0:c2], d).then_inc(b_loaded, 16)
            with sp.Fori(0, BATCH) as b:
                for t in range(NT):
                    norm.load(sp, b, t)
                for t in range(NT):
                    norm.store(sp, b, t, y_dram, f"Y{t}")
            for t in range(NT):
                sp.wait_ge(norm.stored[t].sem, norm.stored[t].at(BATCH, 0))

        @block.gpsimd
        def _(pool):
            with pool.Fori(0, BATCH) as b:
                for t in range(NT):
                    norm.root(pool, b, t)
                for n in range(NI):
                    r = rows(n)
                    pool.wait_ge(hid_hi.sem, hid_hi.at(b, n + 1))
                    pool.tensor_tensor(ht[0:r, LO, n, :], hid[0:r, n % 2, :], ht[0:r, HI, n, :].bitcast(F32),
                                       ALU.subtract).then_inc(hid_lo.sem, 1)

        @block.scalar
        def _(act):
            ring.give_credits(act)
            act.sem_inc(hid_lo.sem, 2)
            act.wait_ge(small_loaded, 64)
            act.copy(xa[:, HI].rearrange("p f r -> p (f r)"), xa_raw[:])
            act.copy(da[:, HI].rearrange("p f r -> p (f r)"), da_raw[:]).then_inc(small_hi, 1)
            act.wait_ge(b_scaled, 3)
            for j in range(3):
                c = lr_b[j].shape[1]
                act.copy(lr_b[j][:], lr_raw(j)[:, 0:c]).then_inc(b_hi, 1)
            with act.Fori(0, BATCH) as b:
                for t in range(NT):
                    norm.split_hi(act, b, t)

                def lowrank_hi(use, j, q):
                    src = ring.read(act, b, use)[q * RANK:(q + 1) * RANK, 0:T]
                    for r in range(3):
                        if r != X_LO[j]:
                            last = act.copy(lr_x[j][r * RANK:(r + 1) * RANK, :], src)
                    return last

                lowrank_hi("A", 0, 0)
                lowrank_hi("A", 1, 1).then_inc(lrx_hi.sem, 1)

                def scale(n, j):
                    r = rows(n)
                    src = ring.read(act, b, f"{'GU'[j]}{n}")[0:r, 0:T]
                    if n >= 1:
                        ring.emptied(act, b, f"{'GU'[j]}{n - 1}")
                    act.activation(scaled[0:r, j, :], src, ACT.Identity, scale=scales[0:r, j, n:n + 1])\
                       .then_inc(p1_scaled.sem, 1)

                def silu(n):
                    r = rows(n)
                    ring.emptied(act, b, f"G{n}")
                    act.activation(sig[0:r, n % 2, :], gate[0:r, :], ACT.Silu).then_inc(silu_made.sem, 1)

                def hidden_hi(n):
                    r = rows(n)
                    act.wait_ge(hid_made.sem, hid_made.at(b, n + 1))
                    act.copy(ht[0:r, HI, n, :], hid[0:r, n % 2, :]).then_inc(hid_hi.sem, 1)

                for n in range(NI + 1):
                    if n < NI:
                        scale(n, 0)
                        scale(n, 1)
                        silu(n)
                    if n >= 1:
                        hidden_hi(n - 1)
                lowrank_hi("DA", 2, 0).then_inc(lrx_hi.sem, 1)

        @block.vector
        def _(dve):
            norm.setup(dve)
            dve.wait_ge(b_loaded, 9 * 16)
            for j in range(3):
                c = lr_b[j].shape[1]
                dve.tensor_scalar(lr_raw(j)[:, 0:c], lr_raw(j)[:, 0:c], LR_SCALE, None, ALU.mult)\
                   .then_inc(b_scaled, 1)
            dve.wait_ge(small_hi, 1)
            dve.tensor_tensor(xa[:, LO].rearrange("p f r -> p (f r)"), xa_raw[:],
                              xa[:, HI].rearrange("p f r -> p (f r)").bitcast(F32), ALU.subtract)
            dve.tensor_tensor(da[:, LO].rearrange("p f r -> p (f r)"), da_raw[:],
                              da[:, HI].rearrange("p f r -> p (f r)").bitcast(F32), ALU.subtract)
            dve.tensor_scalar(scales[:], scales[:], Q_STEP, None, ALU.mult)
            dve.tensor_scalar(dscale[:], dscale[:], Q_STEP, None, ALU.mult).then_inc(small_made, 1)
            for j in range(3):
                c = lr_b[j].shape[1]
                q = slice(B_LO[j] * RANK, (B_LO[j] + 1) * RANK)
                dve.wait_ge(b_hi, j + 1)
                dve.tensor_tensor(lr_b[j][q, :], lr_raw(j)[q, 0:c], lr_b[j][q, :].bitcast(F32),
                                  ALU.subtract).then_inc(b_made, 1)
            for i, (_, dst, _, c) in enumerate(chunks):
                dve.wait_ge(raw_loaded[i % 2], 16 * (i // 2 + 1))
                dve.tensor_scalar(dst, raw[:, i % 2, 0:c], -Q_ZERO, None, ALU.add).then_inc(raw_used, 1)
            with dve.Fori(0, BATCH) as b:
                for t in range(NT + 1):
                    if t < NT:
                        norm.statistics(dve, b, t)
                    if t >= 1:
                        norm.normalise(dve, b, t - 1)
                        if t >= 2:
                            norm.split_lo(dve, b, t - 2)
                norm.split_lo(dve, b, NT - 1)

                def lowrank_lo(use, j, q):
                    src = ring.read(dve, b, use)[q * RANK:(q + 1) * RANK, 0:T]
                    hi = q * RANK
                    return dve.tensor_tensor(lr_x[j][X_LO[j] * RANK:(X_LO[j] + 1) * RANK, :], src,
                                             lr_x[j][hi:hi + RANK, :].bitcast(F32), ALU.subtract)

                dve.wait_ge(lrx_hi.sem, lrx_hi.at(b, 1))
                lowrank_lo("A", 0, 0)
                lowrank_lo("A", 1, 1).then_inc(ring.is_free("A"), 1)

                def add_lowrank(n, j):
                    r = rows(n)
                    src = ring.read(dve, b, f"{'GU'[j]}{n}")[0:r, T:2 * T]
                    dve.wait_ge(p1_scaled.sem, p1_scaled.at(b, 2 * n + j + 1))
                    if j == 0 and n >= 1:
                        dve.wait_ge(silu_made.sem, silu_made.at(b, n))
                    dst = gate[0:r, :] if j == 0 else upv[0:r, n % 2, :]
                    dve.tensor_tensor(dst, src, scaled[0:r, j, :], ALU.add)\
                       .then_inc(ring.is_free(f"{'GU'[j]}{n}"), 1)

                def hidden(n):
                    r = rows(n)
                    dve.wait_ge(silu_made.sem, silu_made.at(b, n + 1))
                    ring.emptied(dve, b, f"U{n}")
                    dve.wait_ge(hid_lo.sem, hid_lo.at(b, n - 1))
                    dve.tensor_tensor(hid[0:r, n % 2, :], sig[0:r, n % 2, :], upv[0:r, n % 2, :], ALU.mult)\
                       .then_inc(hid_made.sem, 1)

                for n in range(NI + 1):
                    if n < NI:
                        add_lowrank(n, 0)
                        add_lowrank(n, 1)
                    if n >= 1:
                        hidden(n - 1)
                dve.wait_ge(lrx_hi.sem, lrx_hi.at(b, 2))
                lowrank_lo("DA", 2, 0).then_inc(ring.is_free("DA"), 1)
                for t in range(NT):
                    y = ring.read(dve, b, f"Y{t}")
                    dve.tensor_tensor(ysum[:, t % 2, :], y[:, 0:D], dscale[:], ALU.mult)\
                       .then_inc(y_part.sem, 1)
                    dve.wait_ge(y_part.sem, y_part.at(b, 2 * t + 1))
                    dve.tensor_tensor(norm.x[:, t, :], ysum[:, t % 2, :], norm.x[:, t, :], ALU.add)\
                       .then_inc(y_part.sem, 1)
                    dve.wait_ge(y_part.sem, y_part.at(b, 2 * t + 2))
                    dve.tensor_tensor(norm.x[:, t, :], y[:, D:2 * D], norm.x[:, t, :], ALU.add)\
                       .then_inc(ring.is_free(f"Y{t}"), 1)

        @block.tensor
        def _(pe):
            THREE = ((HI, HI), (LO, HI), (HI, LO))
            with pe.Fori(0, BATCH) as b:
                for t in range(NT):
                    norm.transpose(pe, b, t)
                pe.wait_ge(small_made, 1)
                out = ring.take(pe, b, "A")
                for t in range(NT):
                    ring.emptied(pe, b, f"X{t}")
                passes(pe, out[0:2 * RANK, 0:T], [(xa[:, a, f, :], xt[:, c, f, :])
                                                  for f in range(KD) for a, c in THREE])\
                    .then_inc(ring.is_filled("A"), 1)
                pe.wait_ge(raw_used, len(chunks))
                pe.wait_ge(b_made, 3)
                for n in range(NI):
                    r = rows(n)
                    cols = slice(n * P, n * P + r)
                    for j in range(2):
                        out = ring.take(pe, b, f"{'GU'[j]}{n}")
                        passes(pe, out[0:r, 0:T], [(codes[:, j, f, cols], xt[:, c, f, :])
                                                   for f in range(KD) for c in (HI, LO)])
                        if n == 0 and j == 0:
                            ring.emptied(pe, b, "A")
                        passes(pe, out[0:r, T:2 * T], [(lr_b[j][:, cols], lr_x[j][:])])\
                            .then_inc(ring.is_filled(f"{'GU'[j]}{n}"), 1)

                def down(out, t, ks):
                    tok = slice(t * P, (t + 1) * P)
                    for n in ks:
                        if t == 0:
                            pe.wait_ge(hid_lo.sem, hid_lo.at(b, n + 1))
                        r = rows(n)
                        passes(pe, out[:, 0:D], [(ht[0:r, c, n, tok], dcodes[0:r, n, :]) for c in (HI, LO)],
                               start=n == 0, stop=n == NI - 1)

                def down_lowrank(out, t):
                    passes(pe, out[:, D:2 * D], [(lr_x[2][:, t * P:(t + 1) * P], lr_b[2][:])])\
                        .then_inc(ring.is_filled(f"Y{t}"), 1)

                y0 = ring.take(pe, b, "Y0")
                down(y0, 0, range(NI))
                out = ring.take(pe, b, "DA")
                passes(pe, out[0:RANK, 0:T], [(da[0:rows(n), a, n, :], ht[0:rows(n), c, n, :])
                                              for n in range(NI) for a, c in THREE])\
                    .then_inc(ring.is_filled("DA"), 1)
                y1 = ring.take(pe, b, "Y1")
                down(y1, 1, range(NI))
                ring.emptied(pe, b, "DA")
                down_lowrank(y0, 0)
                down_lowrank(y1, 1)
                for t in range(2, NT):
                    out = ring.take(pe, b, f"Y{t}")
                    down(out, t, range(NI))
                    down_lowrank(out, t)


def program(nc, d):
    with ExitStack() as ctx:
        mid = [nc.dram_tensor(f"mid{i}", (BATCH, NT, P, D), F32, kind="Internal").ap() for i in range(3)]
        consts = constants(ctx, nc)
        feed = [d[n] for n in ("gate_q", "up_q", "down_q", "scales", "dscale", "xa", "gb", "ub", "da", "db")]
        with Phase(nc) as phase:
            attention(nc, phase, "aa", consts, d["x"], mid[0], d["wa"], KV_GQA, UNITS_A, PLAN_A, HEAD_A,
                      rope_dram=d["trig"])
        with Phase(nc) as phase:
            ffn(nc, phase, "f1", consts, mid[0], mid[1], *feed)
        with Phase(nc) as phase:
            attention(nc, phase, "ab", consts, mid[1], mid[2], d["wb"], HEADS, UNITS_B, PLAN_B, HEAD_B,
                      bias_dram=d["bias"], biassel_dram=d["biassel"])
        with Phase(nc) as phase:
            ffn(nc, phase, "f2", consts, mid[2], d["y"], *feed)


def timed(*tasks):
    plan = {}
    for j, kind, bb, u, t in tasks:
        plan.setdefault(j, []).append((kind, bb, u, t))
    return plan


UNITS_A, UNITS_B = 2, 4
OUTPUT = [(j, "C", -1, 0, t) for t, j in enumerate((5, 6, 7, 8))]
PLAN_A = timed(
    *[(j, "P", 0, 1, t) for t, j in enumerate((3, 10, 15, 21))], *OUTPUT,
    *[(j, "T", 0, 1, t) for t, j in enumerate((8, 16, 22, 28))],
    *[(j, "O", -1, 0, t) for t, j in enumerate((12, 13, 18, 19))],
    *[(j, "X", 1, 0, t) for t, j in enumerate((43, 44, 45, 46))],
    *[(j, "P", 1, 0, t) for t, j in enumerate((48, 53, 58, 62))],
    *[(j, "T", 1, 0, t) for t, j in enumerate((54, 59, 64, 68))],
)
PLAN_B = timed(
    *[(20 * (u - 1) + j, "P", 0, u, t) for u in range(1, 4) for t, j in enumerate((3, 4, 5, 6))],
    *OUTPUT,
    *[(20 * (u - 1) + j, "T", 0, u, t) for u in range(1, 4) for t, j in enumerate((7, 8, 9, 10))],
    *[(j, "O", -1, 0, t) for t, j in enumerate((15, 16, 17, 18))],
    *[(j, "X", 1, 0, t) for t, j in enumerate((55, 56, 57, 58))],
    *[(60 + j, "P", 1, 0, t) for t, j in enumerate((3, 4, 5, 6))],
    *[(60 + j, "T", 1, 0, t) for t, j in enumerate((7, 8, 9, 10))],
)
HEAD_A = HEAD_B = timed(
    *[(3 + t, "X", 0, 0, t) for t in range(NT)],
    *[(7 + 2 * t, "P", 0, 0, t) for t in range(NT)],
    *[(14 + 2 * t, "T", 0, 0, t) for t in range(NT)],
)


def kernel(**inputs):
    import concourse.bacc as bacc
    from concourse.bass_utils import run_bass_kernel_spmd

    a = {k.removeprefix("L0_"): np.asarray(v) for k, v in inputs.items()}

    def by_feature(w):
        n = -(-w.shape[0] // P)
        w = np.pad(w, ((0, n * P - w.shape[0]), (0, 0)))
        return np.ascontiguousarray(w.reshape(n, P, -1).transpose(1, 0, 2))

    inv = (1.0 / np.float32(ROPE_BASE) ** (np.arange(0, HD, 2, dtype=np.float32) / np.float32(HD)))
    freqs = np.arange(T, dtype=np.float32)[:, None] * inv.astype(np.float32)[None]
    cos, sin = np.cos(freqs).astype(np.float32), np.sin(freqs).astype(np.float32)
    trig = np.stack([np.concatenate([cos, cos], 1), np.concatenate([-sin, sin], 1)], 1)
    trig = trig.reshape(NT, P, 2 * HD).transpose(1, 0, 2).reshape(P, -1)
    n_rows = UNITS_B + 1
    biassel = np.zeros((P, n_rows * P + 1), np.float32)
    for j in range(n_rows):
        biassel[2 * j:2 * j + 2, j * P:(j + 1) * P] = 1.0
    biassel[1:2 * n_rows:2, -1] = -1.0

    def by_unit(q, k, v, units):
        parts = [np.split(m, units, axis=-1) for m in (q, k, v)]
        return [m[u] for u in range(units) for m in parts]

    wa = [a[f"attn_a_W{k}"] for k in "qkvo"]
    wb = [a[f"attn_b_W{k}"].T for k in "qkvo"]
    bias = by_unit(*[a[f"attn_b_b{k}"] for k in "qkv"], UNITS_B)
    bias = [np.pad(np.concatenate(bias[3 * u:3 * u + 3]), (0, D - 3 * D // UNITS_B)) for u in range(UNITS_B)]
    arrays = {
        "x": a["attn_a_x"].reshape(BATCH, NT, P, D),
        "wa": by_feature(np.concatenate(by_unit(*wa[:3], UNITS_A) + [wa[3]], 1)),
        "wb": by_feature(np.concatenate(by_unit(*wb[:3], UNITS_B) + [wb[3]], 1)),
        "trig": trig,
        "bias": np.repeat(np.stack(bias + [a["attn_b_bo"]]), 2, axis=0),
        "biassel": biassel,
        "gate_q": by_feature(a["ffn_gate_q"].T),
        "up_q": by_feature(a["ffn_up_q"].T),
        "down_q": by_feature(a["ffn_down_q"].T).reshape(P, -1),
        "scales": np.concatenate([by_feature(a[f"ffn_{k}_scale"][:, None])[:, :, 0]
                                  for k in ("gate", "up")], 1),
        "dscale": a["ffn_down_scale"].reshape(1, D),
        "xa": by_feature(np.concatenate([a["ffn_gate_A"], a["ffn_up_A"]], 1)).reshape(P, -1),
        "gb": a["ffn_gate_B"],
        "ub": a["ffn_up_B"],
        "da": by_feature(a["ffn_down_A"]).reshape(P, -1),
        "db": a["ffn_down_B"],
    }
    nc = bacc.Bacc("TRN2", target_bir_lowering=False, num_devices=1)
    feed, d = {}, {}
    for key, v in arrays.items():
        v = np.ascontiguousarray(v)
        feed[f"in_{key}"] = v
        d[key] = nc.dram_tensor(f"in_{key}", v.shape, mybir.dt.from_np(v.dtype), kind="ExternalInput").ap()
    d["y"] = nc.dram_tensor("out_y", (BATCH, NT, P, D), F32, kind="ExternalOutput").ap()
    program(nc, d)
    r = run_bass_kernel_spmd(nc, [feed], core_ids=[0])
    return r.results[0]["out_y"].reshape(BATCH, T, D)
```

```python
from contextlib import ExitStack

import numpy as np

import concourse.bass as bass
from concourse import mybir

F32 = mybir.dt.float32
F32R = mybir.dt.float32r
BF16 = mybir.dt.bfloat16
F16 = mybir.dt.float16
I32 = mybir.dt.int32
ALU = mybir.AluOpType
ACT = mybir.ActivationFunctionType
AX_X = mybir.AxisListType.X

P = 128
BATCH, T, D = 4, 512, 512
NT = T // P
KD = D // P
HEADS, HD = 32, 16
KV_GQA = 8
ROPE_BASE = 500000.0
INTER, RANK = 1376, 32
NI = -(-INTER // P)
LAST = INTER - (NI - 1) * P
Q_ZERO, Q_STEP, LR_SCALE = 7.5, 0.005, 0.02
EPS = 1e-5

PARTS = 6
STK = PARTS * HD
MAXROW = STK
ROWS = STK + 4
SHIFT = 36.0
VW = 50
MASKED = -1.0e30
PAIRS = HEADS // 2
PCOLS = 2 * (512 + 384 + 256 + 128)



class Signal:

    def __init__(self, sem, per_batch, credit=0):
        self.sem, self.per_batch, self.credit = sem, per_batch, credit

    def at(self, b, k):
        return b * self.per_batch + (k + self.credit)


class Phase:

    def __init__(self, nc):
        self.nc, self.held, self.stack = nc, [], ExitStack()

    def semaphore(self, name):
        self.held.append(self.stack.enter_context(self.nc.semaphore(name)))
        return self.held[-1]

    def __enter__(self):
        return self

    def __exit__(self, *failed):
        if failed[0] is None:
            with self.nc.Block() as block:

                @block.sync
                def _(sp):
                    for s in self.held:
                        sp.sem_clear(s)

        self.stack.close()


class Ring:

    def __init__(self, ctx, phase, nc, name, uses, slots, columns):
        self.slots = slots
        self.psum = ctx.enter_context(nc.psum_tensor(f"{name}_ring", [P, slots, columns], F32))
        self.place = {u: (i % slots, i // slots) for i, u in enumerate(uses)}
        count = [len(range(s, len(uses), slots)) for s in range(slots)]
        self.filled = [Signal(phase.semaphore(f"{name}_psum{s}_filled"), count[s])
                       for s in range(self.slots)]
        self.freed = [Signal(phase.semaphore(f"{name}_psum{s}_freed"), count[s], 1)
                      for s in range(self.slots)]

    def give_credits(self, eng):
        for s in range(self.slots):
            eng.sem_inc(self.freed[s].sem, 1)

    def take(self, pe, b, use):
        s, n = self.place[use]
        pe.wait_ge(self.freed[s].sem, self.freed[s].at(b, n))
        return self.psum[:, s, :]

    def read(self, eng, b, use):
        s, n = self.place[use]
        eng.wait_ge(self.filled[s].sem, self.filled[s].at(b, n + 1))
        return self.psum[:, s, :]

    def emptied(self, eng, b, use):
        s, n = self.place[use]
        eng.wait_ge(self.freed[s].sem, self.freed[s].at(b, n + 1))

    def is_filled(self, use):
        return self.filled[self.place[use][0]].sem

    def is_free(self, use):
        return self.freed[self.place[use][0]].sem


def constants(ctx, nc):
    identf = ctx.enter_context(nc.sbuf_tensor("identf", [P, P], F32))
    identb = ctx.enter_context(nc.sbuf_tensor("identb", [P, P], BF16))
    mask_qk = ctx.enter_context(nc.sbuf_tensor("mask_qk", [P, P], BF16))
    mask_kq = ctx.enter_context(nc.sbuf_tensor("mask_kq", [P, P], BF16))
    made = ctx.enter_context(nc.semaphore("constants_cleared"))
    with nc.Block() as block:

        @block.gpsimd
        def _(pool):
            pool.memset(identf[:], 0.0)
            pool.memset(identb[:], 0.0)
            pool.memset(mask_qk[:], 0.0)
            pool.memset(mask_kq[:], 0.0).then_inc(made, 1)
            pool.wait_ge(made, 1)
            for m in (identf, identb):
                pool.affine_select(out=m[:], in_=m[:], compare_op=ALU.not_equal, fill=1.0, base=0,
                                   pattern=[[-1, P]], channel_multiplier=1)
            pool.affine_select(out=mask_qk[:], in_=mask_qk[:], compare_op=ALU.is_ge, fill=MASKED, base=0,
                               pattern=[[-1, P]], channel_multiplier=1)
            pool.affine_select(out=mask_kq[:], in_=mask_kq[:], compare_op=ALU.is_ge, fill=MASKED, base=0,
                               pattern=[[1, P]], channel_multiplier=-1)

    return identf, identb, mask_qk, mask_kq


class Norm:

    def __init__(self, ctx, phase, nc, name, identf, x_dram):
        sb = lambda n, s, d: ctx.enter_context(nc.sbuf_tensor(f"{name}_{n}", s, d))
        sem = lambda n: phase.semaphore(f"{name}_{n}")
        self.ring = Ring(ctx, phase, nc, f"{name}_norm", [f"X{t}" for t in range(NT)], 2, D)
        self.identf, self.x_dram = identf, x_dram
        self.x = sb("x", [P, NT, D], F32)
        self.xn = sb("xn", [P, 2, D], F32)
        self.xt = sb("xt", [P, 2, KD, T], F32R)
        self.stats = sb("stats", [P, NT, 6], F32)
        self.mv = sb("mv", [P, NT, 2], F32)
        self.rstd = sb("rstd", [P, NT], F32)
        self.var = sb("var", [P, NT], F32)
        self.power = sb("power", [P, 1], F32)
        self.loaded = [Signal(sem(f"x{t}_loaded"), 16) for t in range(NT)]
        self.stats_made = Signal(sem("stats_made"), NT)
        self.stats_seen = sem("stats_seen")
        self.aggregated = Signal(sem("aggregated"), NT)
        self.var_made = Signal(sem("var_made"), NT)
        self.rstd_made = Signal(sem("rstd_made"), NT)
        self.normed = Signal(sem("normed"), NT)
        self.hi_made = Signal(sem("hi_made"), NT)

    def load(self, sp, b, t, first=False):
        if not first:
            sp.wait_ge(self.normed.sem, self.normed.at(b, t + 1 - NT))
        sp.dma_start(self.x[:, t, :], self.x_dram[b, t]).then_inc(self.loaded[t].sem, 16)

    def setup(self, dve):
        dve.memset(self.power[:], -0.5)

    def statistics(self, dve, b, t):
        dve.wait_ge(self.loaded[t].sem, self.loaded[t].at(b, 16))
        dve.bn_stats(self.stats[:, t, :], self.x[:, t, :]).then_inc(self.stats_made.sem, 1)
        dve.wait_ge(self.stats_made.sem, self.stats_made.at(b, t + 1))
        dve.sem_inc(self.stats_seen, 1)
        dve.bn_aggr(self.mv[:, t, :], self.stats[:, t, :]).then_inc(self.aggregated.sem, 1)
        dve.wait_ge(self.aggregated.sem, self.aggregated.at(b, t + 1))
        dve.tensor_scalar(self.var[:, t:t + 1], self.mv[:, t, 1:2], EPS, None, ALU.add)\
           .then_inc(self.var_made.sem, 1)

    def root(self, pool, b, t):
        pool.wait_ge(self.var_made.sem, self.var_made.at(b, t + 1))
        pool.tensor_tensor(self.rstd[:, t:t + 1], self.var[:, t:t + 1], self.power[:], ALU.pow)\
            .then_inc(self.rstd_made.sem, 1)

    def normalise(self, dve, b, t):
        dve.wait_ge(self.rstd_made.sem, self.rstd_made.at(b, t + 1))
        if t >= 2:
            self.ring.read(dve, b, f"X{t - 2}")
        dve.tensor_scalar(self.xn[:, t % 2, :], self.x[:, t, :], self.mv[:, t, 0:1],
                          self.rstd[:, t:t + 1], ALU.subtract, ALU.mult).then_inc(self.normed.sem, 1)

    def transpose(self, pe, b, t):
        out = self.ring.take(pe, b, f"X{t}")
        pe.wait_ge(self.normed.sem, self.normed.at(b, t + 1))
        for f in range(KD):
            mm = pe.transpose(out[:, f * P:(f + 1) * P], self.xn[:, t % 2, f * P:(f + 1) * P],
                              self.identf[:])
        mm.then_inc(self.ring.is_filled(f"X{t}"), 1)

    def split_hi(self, act, b, t):
        src = self.ring.read(act, b, f"X{t}").rearrange("p (f t) -> p f t", f=KD)
        act.copy(self.xt[:, 0, :, t * P:(t + 1) * P], src).then_inc(self.hi_made.sem, 1)

    def split_lo(self, dve, b, t):
        src = self.ring.read(dve, b, f"X{t}").rearrange("p (f t) -> p f t", f=KD)
        dve.wait_ge(self.hi_made.sem, self.hi_made.at(b, t + 1))
        tok = slice(t * P, (t + 1) * P)
        dve.tensor_tensor(self.xt[:, 1, :, tok], src, self.xt[:, 0, :, tok].bitcast(F32), ALU.subtract)\
           .then_inc(self.ring.is_free(f"X{t}"), 1)


def passes(pe, out, pairs, start=True, stop=True):
    for i, (w, x) in enumerate(pairs):
        mm = pe.matmul(out, w, x, start=start and i == 0, stop=stop and i == len(pairs) - 1)
    return mm


class Timetable:

    SUB = 5

    def __init__(self, units, plan, head, n_parts):
        self.units, self.n_parts = units, n_parts
        self.cut = self.SUB * (PAIRS // units)
        end = self.SUB * PAIRS
        line = lambda b, lo, hi: [(b, j // self.SUB, j % self.SUB) for j in range(lo, hi)]
        self.plan = plan
        pure = max(head) + n_parts + 2
        self.head = ([None] * pure + line(0, 0, self.cut), dict(head))
        self.head[1].update({pure + j: [(k, bb, u, t) for k, bb, u, t in plan.get(j, []) if bb == 0]
                             for j in range(self.cut)})
        body = line(0, self.cut, end) + line(1, 0, self.cut)
        tasks = {}
        for pos, (b, s, i) in enumerate(body):
            tasks[pos] = [(k, b + bb, u, t) for k, bb, u, t in plan.get(s * self.SUB + i, [])]
        self.body = (body, tasks)
        n = end - self.cut
        last = {p: [x for x in tasks[p] if x[1] == 0] for p in range(n)}
        for q, x in enumerate(("C0", "C1", "C2", "C3", "O0", "O1", "O2", "O3")):
            last[n + 1 + q] = [(x[0], 0, 0, int(x[1]))]
        self.tail = (body[:n] + [None] * 10, last)

    def names(self, region):
        out = []
        for pos in range(len(region[0])):
            out += [(kind, u, t, 0) for kind, _, u, t in region[1].get(pos, []) if kind != "T"]
            out += [("T", u, t, p) for _, u, t, p in self.turned(region, pos)]
        return out

    def turned(self, region, pos, lag=0):
        return [(bb, u, t, p) for p in range(self.n_parts)
                for _, bb, u, t in self.started(region, pos, lag + p, "T")]

    @staticmethod
    def started(region, pos, lag, *kinds):
        return [x for x in region[1].get(pos - lag, []) if x[0] in kinds]


class Banks:

    def __init__(self, phase, name, psum, n, table):
        self.psum, self.n, self.filled, self.freed, self.places, self.base = psum, n, [], [], {}, {}
        self.filled = [phase.semaphore(f"{name}_task_bank{i}_filled") for i in range(n)]
        self.freed = [phase.semaphore(f"{name}_task_bank{i}_freed") for i in range(n)]
        before = [0] * n
        for key, region, times in (("head", table.head, 1), ("body", table.body, BATCH - 1),
                                   ("tail", table.tail, 1)):
            names = table.names(region)
            per = [len(range(i, len(names), n)) for i in range(n)]
            self.base[key] = (list(before), per)
            self.places[key] = {u: (i % n, i // n) for i, u in enumerate(names)}
            before = [x + times * p for x, p in zip(before, per)]

    def _at(self, where, use):
        key, b = where
        bank, nth = self.places[key][use]
        base, per = self.base[key]
        return bank, b * per[bank] + (base[bank] + nth)

    def take(self, pe, where, use):
        bank, n = self._at(where, use)
        pe.wait_ge(self.freed[bank], n + 1)
        return self.psum[:, bank, :]

    def read(self, eng, where, use):
        bank, n = self._at(where, use)
        eng.wait_ge(self.filled[bank], n + 1)
        return self.psum[:, bank, :]

    def emptied(self, eng, where, use):
        bank, n = self._at(where, use)
        eng.wait_ge(self.freed[bank], n + 2)

    def all_emptied(self, eng, where, uses, take=None):
        skip = None if take is None else self.places[where[0]][take][0]
        last = {self.places[where[0]][u][0]: u for u in sorted(uses, key=lambda u: self.places[where[0]][u][1])}
        for bank, use in last.items():
            if bank != skip:
                self.emptied(eng, where, use)

    def is_filled(self, where, use):
        return self.filled[self._at(where, use)[0]]

    def is_free(self, where, use):
        return self.freed[self._at(where, use)[0]]


def attention(nc, phase, name, consts, x_dram, y_dram, w_dram, kv_heads, units, plan, head,
              rope_dram=None, bias_dram=None, biassel_dram=None):
    identf, identb, mask_qk, mask_kq = consts
    rope, biased = rope_dram is not None, bias_dram is not None
    rep = HEADS // kv_heads
    HU, KU = HEADS // units, kv_heads // units
    NQ, NKV = HU * HD, KU * HD
    NU = NQ + 2 * NKV
    OO = units * NU
    WN = OO + D
    NST = HU + KU
    TPARTS = -(-NST // 8)
    STEPS = PAIRS // units
    SUB = Timetable.SUB
    EW = 512
    NPF = 5
    table = Timetable(units, plan, head, TPARTS)
    HI, LO = 0, 1
    SLOT_HI, SLOT_MID, Q_LO, K_LO = 2, 3, 5, 1

    with ExitStack() as ctx:
        sb = lambda n, s, d: ctx.enter_context(nc.sbuf_tensor(f"{name}_{n}", s, d))
        sem = lambda n: phase.semaphore(f"{name}_{n}")
        scores = ctx.enter_context(nc.psum_tensor(f"{name}_scores", [P, 3, EW], F32))
        maxima = ctx.enter_context(nc.psum_tensor(f"{name}_maxima", [P, 2, EW], F32))
        av = ctx.enter_context(nc.psum_tensor(f"{name}_av", [P, EW], F32))
        banks = Banks(phase, name, ctx.enter_context(nc.psum_tensor(f"{name}_tasks", [P, 2, 512], F32)),
                      2, table)
        x = sb("x", [P, NT, D], F32)
        res = sb("res", [P, 2, D], F32)
        xt = sb("xt", [P, 2, KD, T], F32R)
        ct = sb("ct", [P, 2, KD, T], F32R)
        cx = sb("ctx", [P, NT, D], F32)
        w = sb("w", [P, 2, KD, WN], F32R)
        stacks = sb("stacks", [ROWS, 2, NST, T], BF16)
        v = sb("v", [P, 2, NT, KU, VW], BF16)
        staged = sb("staged", [P, NT, NST, PARTS, HD], BF16)
        rest = sb("rest", [P, 2, NU], F32)
        stats = sb("stats", [P, NT, 6], F32)
        mv = sb("mv", [P, NT, 2], F32)
        var = sb("var", [P, NT], F32)
        rstd = sb("rstd", [P, NT], F32)
        power = sb("power", [P, 1], F32)
        nmax = sb("nmax", [P, 2, NT, 2], F32)
        nrest = sb("nrest", [P, 2, NT, 2], F32)
        nparts = sb("nparts", [P, 2, NT, 2, 4], BF16)
        osum = sb("osum", [P, 8, HD], F32)
        rden = sb("rden", [P, 2, 8], F32)
        region = sb("region", [P, NPF * EW + 2 * PCOLS], F32)
        pf = region[:, 0:NPF * EW].rearrange("p (i n) -> p i n", i=NPF)
        ph = region[:, NPF * EW:NPF * EW + PCOLS].bitcast(F16).rearrange("p (i n) -> p i n", i=2)
        pl = region[:, NPF * EW + PCOLS:].bitcast(F16).rearrange("p (i n) -> p i n", i=2)
        wraw = region[:, 0:2 * WN].rearrange("p (i n) -> p i n", i=2)
        if rope:
            trig = sb("trig", [P, NT, 2, HD], F32)
            turned = sb("turned", [P, 2, NQ + NKV], F32)
        if biased:
            biasraw, biashi = region[:, 2 * WN:2 * WN + D], region[:, 2 * WN + D:2 * WN + 2 * D]
            selraw = region[:, 2 * WN + 2 * D:2 * WN + 2 * D + (units + 1) * P + 1]
            bias = sb("bias", [P, D], F32R)
            sel = sb("sel", [P, units + 1, P], F32R)

        w_loaded = [sem(f"w{i}_loaded") for i in range(2)]
        w_hi_made, w_lo_made = sem("w_hi_made"), sem("w_lo_made")
        extra_loaded, extra_hi, extra_made = sem("extra_loaded"), sem("extra_hi"), sem("extra_made")
        ones_set, shift_set, bias_cleared = sem("ones_set"), sem("shift_set"), sem("bias_cleared")
        UT = units * NT
        x_loaded = [Signal(sem(f"x{t}_loaded"), 16) for t in range(NT)]
        res_loaded = [Signal(sem(f"res{i}_loaded"), 32) for i in range(2)]
        stored = [Signal(sem(f"y{i}_stored"), 32, 16) for i in range(2)]
        stats_made = Signal(sem("stats_made"), NT)
        stats_seen = sem("stats_seen")
        aggregated = Signal(sem("aggregated"), NT)
        var_made = Signal(sem("var_made"), NT)
        rstd_made = Signal(sem("rstd_made"), NT)
        normed = Signal(sem("normed"), NT)
        xhi_made = Signal(sem("xhi_made"), NT)
        chi_made = Signal(sem("chi_made"), NT)
        rope_products = Signal(sem("rope_products"), UT)
        roped = Signal(sem("roped"), UT)
        qk_hi = Signal(sem("qk_hi"), UT)
        v_hi = Signal(sem("v_hi"), UT)
        qk_rest = Signal(sem("qk_rest"), UT)
        mid_made = Signal(sem("mid_made"), UT)
        low_made = Signal(sem("low_made"), UT, 2)
        replicated = Signal(sem("replicated"), UT)
        nmax_chain = Signal(sem("nmax_chain"), 3 * PAIRS)
        nmax_split = Signal(sem("nmax_split"), PAIRS)
        SB = [2, 2, 1]
        scores_filled = [Signal(sem(f"scores{i}_filled"), SB[i] * PAIRS) for i in range(3)]
        scores_freed = [Signal(sem(f"scores{i}_freed"), SB[i] * PAIRS, 1) for i in range(3)]
        MB = [3, 3]
        maxima_filled = [Signal(sem(f"maxima{i}_filled"), MB[i] * PAIRS) for i in range(2)]
        maxima_freed = [Signal(sem(f"maxima{i}_freed"), MB[i] * PAIRS, 1) for i in range(2)]
        plo_made = Signal(sem("plo_made"), SUB * PAIRS, NPF)
        av_made = Signal(sem("av_made"), PAIRS, 2)
        av_read = Signal(sem("av_read"), PAIRS, 3)
        rows_filled = Signal(sem("rows_filled"), PAIRS)
        rows_made = Signal(sem("rows_made"), PAIRS)
        ctx_made = Signal(sem("ctx_made"), PAIRS, 1)

        def split_cols(ap):
            return ap.rearrange("p (h d) -> p h d", d=HD)

        def unit(s):
            return s // STEPS

        def heads(s, i):
            h = 2 * (s % STEPS) + i
            return h, HU + h // rep, h // rep

        def stack_out(copy, eng, where, u, t, p):
            n = min(8, NST - 8 * p)
            src = banks.read(eng, where, ("T", u, t, p)).bitcast(BF16)[0:STK, 0:n * P]
            copy(stacks[0:STK, u % 2, 8 * p:8 * p + n, t * P:(t + 1) * P],
                 src.rearrange("p (h t) -> p h t", t=P)).then_inc(banks.is_free(where, ("T", u, t, p)), 1)

        if rope:
            MAXIMA_AT = ((1, ()), (1, ()), (2, (0, 1)), (2, (2, 3)), (2, (4, 5)))
        else:
            MAXIMA_AT = ((1, (4, 5)), (1, ()), (2, ()), (2, (0, 1)), (2, (2, 3)))
        FIRST = sum(len(ks) for ahead, ks in MAXIMA_AT if ahead == 2)
        TRANSPOSE_AT, ROWS_AT, VALUES_AT, FINISH_AT = 2, 3, 4, 0

        def following(region, b, s, ahead):
            if s + ahead < PAIRS:
                return b, s + ahead
            return (b + 1, s + ahead - PAIRS) if region is table.body else None

        def preceding(region, b, s, back):
            if s >= back:
                return b, s - back
            return (b - 1, s - back + PAIRS) if region is table.body else None

        block = ctx.enter_context(nc.Block())

        def whole(eng, part):
            part(table.head, ("head", 0), 0)
            with eng.Fori(0, BATCH - 1) as b:
                part(table.body, ("body", b), b)
            part(table.tail, ("tail", 0), BATCH - 1)

        @block.sync
        def _(sp):
            for i in range(2):
                sp.sem_inc(stored[i].sem, 16)
            for t in range(NT):
                sp.dma_start(x[:, t, :], x_dram[0, t]).then_inc(x_loaded[t].sem, 16)
            for f in range(KD):
                if f >= 2:
                    sp.wait_ge(w_lo_made, f - 1)
                sp.dma_start(wraw[:, f % 2, :], w_dram[:, f, :]).then_inc(w_loaded[f % 2], 16)
            if rope:
                sp.dma_start(trig[:].rearrange("p t a d -> p (t a d)"), rope_dram).then_inc(extra_loaded, 16)
            if biased:
                sp.wait_ge(bias_cleared, 1)
                sp.dma_start(biasraw[0:2 * (units + 1), :], bias_dram).then_inc(extra_loaded, 16)
                sp.dma_start(selraw, biassel_dram).then_inc(extra_loaded, 16)

            def next_tokens(b):
                for t in range(NT):
                    sp.wait_ge(xhi_made.sem, xhi_made.at(b, t + 1))
                    sp.dma_start(x[:, t, :], x_dram[b + 1, t]).then_inc(x_loaded[t].sem, 16)

            def residual(where, b):
                def load(t):
                    sp.wait_ge(stored[t % 2].sem, stored[t % 2].at(b, 16 * (t // 2)))
                    sp.dma_start(res[:, t % 2, :], x_dram[b, t]).then_inc(res_loaded[t % 2].sem, 16)

                load(0)
                load(1)
                for t in range(NT):
                    banks.emptied(sp, where, ("O", 0, t, 0))
                    sp.dma_start(y_dram[b, t], res[:, t % 2, :]).then_inc(stored[t % 2].sem, 16)
                    if t + 2 < NT:
                        load(t + 2)

            with sp.Fori(0, BATCH - 1) as b:
                next_tokens(b)
                residual(("body", b), b)
            residual(("tail", 0), BATCH - 1)
            for i in range(2):
                sp.wait_ge(stored[i].sem, stored[i].at(BATCH, 0))

        @block.gpsimd
        def _(pool):
            ones_rows = slice(MAXROW, ROWS)
            pool.memset(stacks[ones_rows, :, HU:NST, :], 1.0).then_inc(ones_set, 1)
            pool.wait_ge(ones_set, 1)
            pool.memset(v[:, :, :, :, 3 * HD:3 * HD + 1], 1.0).then_inc(ones_set, 1)
            pool.wait_ge(ones_set, 2)
            pool.memset(stacks[ones_rows, :, 0:HU, :], SHIFT).then_inc(shift_set, 1)
            pool.wait_ge(shift_set, 1)

            def part(region, where, b0):
                for pos, step in enumerate(region[0]):
                    for _, bb, _, t in table.started(region, pos + 2, 0, "X"):
                        pool.wait_ge(var_made.sem, var_made.at(b0 + bb, t + 1))
                        pool.tensor_tensor(rstd[:, t:t + 1], var[:, t:t + 1], power[:], ALU.pow)\
                            .then_inc(rstd_made.sem, 1)
                    for _, bb, u, t in table.started(region, pos, 3 if rope else 2, "P"):
                        k = u * NT + t
                        r = rest[:, k % 2, :]
                        pool.wait_ge(mid_made.sem, mid_made.at(b0 + bb, k + 1))
                        pool.tensor_tensor(staged[:, t, 0:HU, Q_LO, :], split_cols(r[:, 0:NQ]),
                                           staged[:, t, 0:HU, SLOT_MID, :], ALU.subtract)
                        pool.tensor_tensor(staged[:, t, HU:NST, K_LO, :], split_cols(r[:, NQ:NQ + NKV]),
                                           staged[:, t, HU:NST, SLOT_MID, :], ALU.subtract)
                        pool.tensor_tensor(v[:, u % 2, t, :, 2 * HD:3 * HD], split_cols(r[:, NQ + NKV:NU]),
                                           v[:, u % 2, t, :, HD:2 * HD], ALU.subtract)\
                            .then_inc(low_made.sem, 1)
                    if step is not None:
                        bs, s, i = step
                        b = b0 + bs
                        n = SUB * s + i
                        cols = slice(i * EW, (i + 1) * EW)
                        sbk, nth = i % 3, SB[i % 3] * s + i // 3
                        pool.wait_ge(scores_freed[sbk].sem, scores_freed[sbk].at(b, nth + 1))
                        pool.tensor_tensor(pl[:, s % 2, cols], pf[:, n % NPF, :], ph[:, s % 2, cols],
                                           ALU.subtract).then_inc(plo_made.sem, 1)

            whole(pool, part)

        @block.scalar
        def _(act):
            for sems in (banks.freed, [f.sem for f in scores_freed + maxima_freed]):
                for one in sems:
                    act.sem_inc(one, 1)
            act.sem_inc(av_read.sem, 3)
            act.sem_inc(ctx_made.sem, 1)
            act.sem_inc(low_made.sem, 2)
            act.sem_inc(plo_made.sem, NPF)
            act.sem_inc(av_made.sem, 2)
            for f in range(KD):
                act.wait_ge(w_loaded[f % 2], 16 * (f // 2 + 1))
                act.copy(w[:, HI, f, :], wraw[:, f % 2, :]).then_inc(w_hi_made, 1)
            if biased:
                act.wait_ge(extra_loaded, 32)
                act.copy(biashi.bitcast(F32R), biasraw)
                act.copy(sel[:].rearrange("p a n -> p (a n)"), selraw[:, 0:(units + 1) * P])\
                   .then_inc(extra_hi, 1)
                act.wait_ge(extra_made, 1)
            act.wait_ge(w_lo_made, KD)

            def part(region, where, b0):
                for pos, step in enumerate(region[0]):
                    for _, u, t, p in table.turned(region, pos, 1):
                        if p % 2 == 1:
                            stack_out(act.copy, act, where, u, t, p)
                    for kind, bb, _, t in table.started(region, pos, 1, "X", "C"):
                        src = banks.read(act, where, (kind, 0, t, 0)).rearrange("p (f t) -> p f t", f=KD)
                        dst, made = (xt, xhi_made) if kind == "X" else (ct, chi_made)
                        act.copy(dst[:, HI, :, t * P:(t + 1) * P], src).then_inc(made.sem, 1)
                    for _, bb, u, t in table.started(region, pos, 1, "P"):
                        psum = banks.read(act, where, ("P", u, t, 0))
                        if not rope:
                            act.copy(staged[:, t, :, SLOT_HI, :], split_cols(psum[:, 0:NQ + NKV]))\
                               .then_inc(qk_hi.sem, 1)
                        act.copy(v[:, u % 2, t, :, 0:HD], split_cols(psum[:, NQ + NKV:NU]))\
                           .then_inc(v_hi.sem, 1)
                    if rope:
                        for _, bb, u, t in table.started(region, pos, 2, "P"):
                            k = u * NT + t
                            act.wait_ge(roped.sem, roped.at(b0 + bb, k + 1))
                            act.copy(staged[:, t, :, SLOT_HI, :], split_cols(rest[:, k % 2, 0:NQ + NKV]))\
                               .then_inc(qk_hi.sem, 1)
                    for _, bb, u, t in table.started(region, pos, 3 if rope else 2, "P"):
                        k = u * NT + t
                        act.wait_ge(qk_rest.sem, qk_rest.at(b0 + bb, k + 1))
                        act.copy(staged[:, t, :, SLOT_MID, :], split_cols(rest[:, k % 2, 0:NQ + NKV]))
                        banks.emptied(act, where, ("P", u, t, 0))
                        act.copy(v[:, u % 2, t, :, HD:2 * HD], split_cols(rest[:, k % 2, NQ + NKV:NU]))\
                           .then_inc(mid_made.sem, 1)
                    if step is not None:
                        bs, s, i = step
                        b = b0 + bs
                        n = SUB * s + i
                        sbk, nth = i % 3, SB[i % 3] * s + i // 3
                        cols = slice(i * EW, (i + 1) * EW)
                        act.wait_ge(plo_made.sem, plo_made.at(b, n + 1 - NPF))
                        act.wait_ge(scores_filled[sbk].sem, scores_filled[sbk].at(b, nth + 1))
                        act.activation(pf[:, n % NPF, :], scores[:, sbk, :], ACT.Exp, scale=0.25)
                        if i == 0:
                            act.wait_ge(av_made.sem, av_made.at(b, s - 1))
                        act.activation(ph[:, s % 2, cols], scores[:, sbk, :], ACT.Exp, scale=0.25)\
                           .then_inc(scores_freed[sbk].sem, 1)

            whole(act, part)

        @block.vector
        def _(dve):
            dve.memset(power[:], -0.5)
            if biased:
                dve.memset(biasraw, 0.0).then_inc(bias_cleared, 1)
            for f in range(KD):
                dve.wait_ge(w_hi_made, f + 1)
                dve.tensor_tensor(w[:, LO, f, :], wraw[:, f % 2, :], w[:, HI, f, :].bitcast(F32),
                                  ALU.subtract).then_inc(w_lo_made, 1)
            if biased:
                dve.wait_ge(extra_hi, 1)
                dve.scalar_tensor_tensor(out=bias[:], in0=biashi, scalar=selraw[:, (units + 1) * P:],
                                         in1=biasraw, op0=ALU.mult, op1=ALU.add).then_inc(extra_made, 1)
            if rope:
                dve.wait_ge(extra_loaded, 16)

            def statistics(b, t):
                dve.wait_ge(x_loaded[t].sem, x_loaded[t].at(b, 16))
                dve.bn_stats(stats[:, t, :], x[:, t, :]).then_inc(stats_made.sem, 1)
                dve.wait_ge(stats_made.sem, stats_made.at(b, t + 1))
                dve.sem_inc(stats_seen, 1)
                dve.bn_aggr(mv[:, t, :], stats[:, t, :]).then_inc(aggregated.sem, 1)
                dve.wait_ge(aggregated.sem, aggregated.at(b, t + 1))
                dve.tensor_scalar(var[:, t:t + 1], mv[:, t, 1:2], EPS, None, ALU.add)\
                   .then_inc(var_made.sem, 1)

            def normalise(b, t):
                dve.wait_ge(rstd_made.sem, rstd_made.at(b, t + 1))
                dve.tensor_scalar(x[:, t, :], x[:, t, :], mv[:, t, 0:1], rstd[:, t:t + 1],
                                  ALU.subtract, ALU.mult).then_inc(normed.sem, 1)

            def rotate(where, b, u, t):
                k, n = u * NT + t, NST
                q = banks.read(dve, where, ("P", u, t, 0))[:, 0:NQ + NKV]
                q = q.rearrange("p (h a d) -> p h a d", a=2, d=HD // 2)
                shape = [P, n, HD // 2]
                ta = turned[:, 0, :].rearrange("p (h a d) -> p h a d", a=2, d=HD // 2)
                tb = turned[:, 1, :].rearrange("p (h a d) -> p h a d", a=2, d=HD // 2)
                dve.wait_ge(low_made.sem, low_made.at(b, k - 1))
                for a in range(2):
                    half = slice(a * HD // 2, (a + 1) * HD // 2)
                    dve.tensor_tensor(ta[:, :, a, :], q[:, :, a, :],
                                      trig[:, t, 0:1, half].broadcast_to(shape), ALU.mult)
                    last = dve.tensor_tensor(tb[:, :, a, :], q[:, :, 1 - a, :],
                                             trig[:, t, 1:2, half].broadcast_to(shape), ALU.mult)
                last.then_inc(rope_products.sem, 1)
                dve.wait_ge(rope_products.sem, rope_products.at(b, k + 1))
                dve.tensor_tensor(rest[:, k % 2, 0:NQ + NKV], turned[:, 0, :], turned[:, 1, :],
                                  ALU.add).then_inc(roped.sem, 1)

            def remainder(where, b, u, t):
                k = u * NT + t
                dst = rest[:, k % 2, 0:NQ + NKV]
                if rope:
                    src = dst
                else:
                    src = banks.read(dve, where, ("P", u, t, 0))[:, 0:NQ + NKV]
                    dve.wait_ge(low_made.sem, low_made.at(b, k - 1))
                dve.wait_ge(qk_hi.sem, qk_hi.at(b, k + 1))
                dve.tensor_tensor(split_cols(dst), split_cols(src), staged[:, t, :, SLOT_HI, :],
                                  ALU.subtract).then_inc(qk_rest.sem, 1)

            def value_remainder(where, b, u, t):
                k = u * NT + t
                src = banks.read(dve, where, ("P", u, t, 0))[:, NQ + NKV:NU]
                dve.tensor_tensor(split_cols(rest[:, k % 2, NQ + NKV:NU]), split_cols(src),
                                  v[:, u % 2, t, :, 0:HD], ALU.subtract)\
                   .then_inc(banks.is_free(where, ("P", u, t, 0)), 1)

            def replicate(b, u, t):
                k = u * NT + t
                dve.wait_ge(mid_made.sem, mid_made.at(b, k + 1))
                st = staged[:, t]
                hi, mid = st[:, :, SLOT_HI:SLOT_HI + 1, :], st[:, :, SLOT_MID, :]
                dve.tensor_copy(st[:, 0:HU, 0:2, :], hi[:, 0:HU].broadcast_to([P, HU, 2, HD]))
                dve.tensor_copy(st[:, 0:HU, 4, :], mid[:, 0:HU])
                dve.tensor_copy(st[:, HU:NST, 4:6, :], hi[:, HU:NST].broadcast_to([P, KU, 2, HD]))
                dve.tensor_copy(st[:, HU:NST, 0, :], mid[:, HU:NST]).then_inc(replicated.sem, 1)

            def reduce_max(b, s, k):
                mb, nth = k % 2, MB[k % 2] * s + k // 2
                dve.wait_ge(maxima_filled[mb].sem, maxima_filled[mb].at(b, nth + 1))
                nm, h, src = nmax[:, s % 2], k % 2, maxima[:, mb, :]
                if k < 2:
                    dve.tensor_reduce(nm[:, 0, h:h + 1], src[:, 0:P], AX_X, ALU.max, negate=True)
                    last = dve.tensor_reduce(nm[:, 1, h:h + 1], src[:, P:3 * P], AX_X, ALU.max, negate=True)
                else:
                    qt = 1 + k // 2
                    last = dve.tensor_reduce(nm[:, qt, h:h + 1], src[:, 0:(qt + 1) * P], AX_X, ALU.max,
                                             negate=True)
                last.then_inc(maxima_freed[mb].sem, 1)

            def split_max(b, s):
                nm, nr, np_ = nmax[:, s % 2], nrest[:, s % 2], nparts[:, s % 2]
                dve.wait_ge(maxima_freed[1].sem, maxima_freed[1].at(b, MB[1] * (s + 1)))
                dve.tensor_copy(np_[:, :, :, 0], nm).then_inc(nmax_chain.sem, 1)
                dve.wait_ge(nmax_chain.sem, nmax_chain.at(b, 3 * s + 1))
                dve.tensor_tensor(nr, nm, np_[:, :, :, 0], ALU.subtract).then_inc(nmax_chain.sem, 1)
                dve.wait_ge(nmax_chain.sem, nmax_chain.at(b, 3 * s + 2))
                dve.tensor_copy(np_[:, :, :, 1], nr).then_inc(nmax_chain.sem, 1)
                dve.wait_ge(nmax_chain.sem, nmax_chain.at(b, 3 * s + 3))
                dve.tensor_tensor(np_[:, :, :, 2], nr, np_[:, :, :, 1], ALU.subtract)\
                   .then_inc(nmax_split.sem, 1)

            def max_rows(b, s):
                dve.wait_ge(rows_filled.sem, rows_filled.at(b, s + 1))
                src = av[MAXROW:MAXROW + 3, :].bitcast(BF16)
                h, _, _ = heads(s, 0)
                dve.tensor_copy(stacks[MAXROW:MAXROW + 3, unit(s) % 2, h:h + 2, :],
                                src.rearrange("p (h t) -> p h t", t=T)).then_inc(rows_made.sem, 1)

            def finish(b, s):
                dve.wait_ge(av_made.sem, av_made.at(b, s + 1))
                dve.wait_ge(ctx_made.sem, ctx_made.at(b, s))
                a = av[:, 0:8 * VW].rearrange("p (g c) -> p g c", c=VW)
                dve.tensor_reduce(osum[:], a[:, :, 0:3 * HD].rearrange("p g (s d) -> p g d s", s=3),
                                  AX_X, ALU.add)
                dve.reciprocal(rden[:, s % 2, :], a[:, :, 3 * HD]).then_inc(av_read.sem, 1)
                dve.wait_ge(av_read.sem, av_read.at(b, s + 1))
                dst = cx[:, :, 2 * s * HD:(2 * s + 2) * HD].rearrange("p t (h d) -> p t h d", d=HD)
                src = osum[:].rearrange("p (t h) d -> p t h d", h=2)
                rd = rden[:, s % 2, :].rearrange("p (t h) -> p t h", h=2).unsqueeze(3)\
                    .broadcast_to([P, NT, 2, HD])
                dve.tensor_tensor(dst, src, rd, ALU.mult).then_inc(ctx_made.sem, 1)

            def part(region, where, b0):
                for pos, step in enumerate(region[0]):
                    if step is not None:
                        bs, s, i = step
                        b = b0 + bs
                        if i == ROWS_AT and (after := following(region, b, s, 1)) is not None:
                            max_rows(*after)
                        ahead, ks = MAXIMA_AT[i]
                        if (after := following(region, b, s, ahead)) is not None:
                            for k in ks:
                                reduce_max(*after, k)
                                if k == 5:
                                    split_max(*after)
                        if i == FINISH_AT and (before := preceding(region, b, s, 2)) is not None:
                            finish(*before)
                    for _, u, t, p in table.turned(region, pos, 1):
                        if p % 2 == 0:
                            stack_out(dve.tensor_copy, dve, where, u, t, p)
                    for _, bb, _, t in table.started(region, pos + 3, 0, "X"):
                        statistics(b0 + bb, t)
                    for _, bb, _, t in table.started(region, pos + 1, 0, "X"):
                        normalise(b0 + bb, t)
                    for kind, bb, _, t in table.started(region, pos, 1, "X", "C"):
                        src = banks.read(dve, where, (kind, 0, t, 0)).rearrange("p (f t) -> p f t", f=KD)
                        dst, made = (xt, xhi_made) if kind == "X" else (ct, chi_made)
                        dve.wait_ge(made.sem, made.at(b0 + bb, t + 1))
                        tok = slice(t * P, (t + 1) * P)
                        dve.tensor_tensor(dst[:, LO, :, tok], src, dst[:, HI, :, tok].bitcast(F32),
                                          ALU.subtract).then_inc(banks.is_free(where, (kind, 0, t, 0)), 1)
                    for _, bb, _, t in table.started(region, pos, 1, "O"):
                        y = banks.read(dve, where, ("O", 0, t, 0))
                        dve.wait_ge(res_loaded[t % 2].sem, res_loaded[t % 2].at(b0 + bb, 16 * (t // 2 + 1)))
                        dve.tensor_tensor(res[:, t % 2, :], y, res[:, t % 2, :], ALU.add)\
                           .then_inc(banks.is_free(where, ("O", 0, t, 0)), 1)
                    for _, bb, u, t in table.started(region, pos, 1, "P"):
                        dve.wait_ge(v_hi.sem, v_hi.at(b0 + bb, u * NT + t + 1))
                        if rope:
                            rotate(where, b0 + bb, u, t)
                        else:
                            remainder(where, b0 + bb, u, t)
                        value_remainder(where, b0 + bb, u, t)
                    if rope:
                        for _, bb, u, t in table.started(region, pos, 2, "P"):
                            remainder(where, b0 + bb, u, t)
                    for _, bb, u, t in table.started(region, pos, 3 if rope else 2, "P"):
                        replicate(b0 + bb, u, t)
                    if step is None:
                        if region is table.head and region[0][pos + 1] is not None:
                            for k in range(6):
                                reduce_max(0, 0, k)
                            split_max(0, 0)
                            max_rows(0, 0)
                            for k in range(FIRST):
                                reduce_max(0, 1, k)
                            if FIRST == 6:
                                split_max(0, 1)
                        if region is table.tail and region[0][pos - 1] is not None:
                            finish(b0, PAIRS - 2)
                            finish(b0, PAIRS - 1)

            whole(dve, part)

        @block.tensor
        def _(pe):
            THREE = ((HI, HI), (LO, HI), (HI, LO))
            pe.wait_ge(ones_set, 2)
            pe.wait_ge(shift_set, 1)

            def project(out, src, t, c0, n, bias_row):
                tok = slice(t * P, (t + 1) * P)
                pairs = [(src[:, a, f, tok], w[:, c, f, c0:c0 + n]) for f in range(KD) for a, c in THREE]
                if biased:
                    pairs.append((sel[:, bias_row, :], bias[:, 0:n]))
                return passes(pe, out, pairs)

            def block_scores(out, lhs, rhs, mask, diag):
                pe.matmul(out, lhs, rhs, start=True, stop=False, skip_group_check=True)
                return pe.matmul(out[:, diag:diag + P], identb[:], mask[:], start=False, stop=True,
                                 skip_group_check=True)

            def max_scores(b, s, k):
                mb, nth = k % 2, MB[k % 2] * s + k // 2
                pe.wait_ge(maxima_freed[mb].sem, maxima_freed[mb].at(b, nth))
                st, (h, hk, _) = stacks[:, unit(s) % 2], heads(s, k % 2)
                for qt in ((0, 1) if k < 2 else (1 + k // 2,)):
                    n, at = (qt + 1) * P, P if qt == 1 else 0
                    mm = block_scores(maxima[:, mb, at:at + n], st[0:STK, h, qt * P:(qt + 1) * P],
                                      st[0:STK, hk, 0:n], mask_qk, qt * P)
                mm.then_inc(maxima_filled[mb].sem, 1)

            def max_transposes(b, s):
                pe.wait_ge(av_read.sem, av_read.at(b, s - 2))
                pe.wait_ge(nmax_split.sem, nmax_split.at(b, s + 1))
                out = av[MAXROW:MAXROW + 3, :].bitcast(BF16)
                for i in range(2):
                    for qt in range(NT):
                        c = i * T + qt * P
                        mm = pe.transpose(out[:, c:c + P], nparts[:, s % 2, qt, i, 0:3], identb[:])
                mm.then_inc(rows_filled.sem, 1)

            def exp_scores(b, s, i):
                sbk, nth = i % 3, SB[i % 3] * s + i // 3
                pe.wait_ge(scores_freed[sbk].sem, scores_freed[sbk].at(b, nth))
                if i == 0:
                    pe.wait_ge(rows_made.sem, rows_made.at(b, s + 1))
                st = stacks[:, unit(s) % 2]
                for kb, hh, at in (((0, 0, 0),), ((0, 1, 0),), ((1, 0, 0), (3, 0, 384)),
                                   ((1, 1, 0), (3, 1, 384)), ((2, 0, 0), (2, 1, 256)))[i]:
                    h, hk, _ = heads(s, hh)
                    n = T - kb * P
                    mm = block_scores(scores[:, sbk, at:at + n], st[:, hk, kb * P:(kb + 1) * P],
                                      st[:, h, kb * P:T], mask_kq, 0)
                mm.then_inc(scores_filled[sbk].sem, 1)

            def values(b, s, rows_out):
                if rows_out:
                    pe.wait_ge(rows_made.sem, rows_made.at(b, s + 3))
                pe.wait_ge(plo_made.sem, plo_made.at(b, SUB * (s + 1)))
                pe.wait_ge(av_read.sem, av_read.at(b, s))
                for qt in range(NT):
                    for i in range(2):
                        c = (2 * qt + i) * VW
                        pairs = []
                        for kb in range(qt + 1):
                            at = (i * 512 + qt * P, 1024 + i * 512 + (qt - 1) * P,
                                  2048 + i * 256 + (qt - 2) * P, 1024 + i * 512 + 384)[kb]
                            vh = v[:, unit(s) % 2, kb, heads(s, i)[2], 0:3 * HD + 1]
                            pairs += [(ph[:, s % 2, at:at + P], vh), (pl[:, s % 2, at:at + P], vh)]
                        mm = passes(pe, av[:, c:c + 3 * HD + 1], pairs)
                mm.then_inc(av_made.sem, 1)

            def transposes(where, b, kind, t):
                out = banks.take(pe, where, (kind, 0, t, 0))
                if kind == "X":
                    pe.wait_ge(normed.sem, normed.at(b, t + 1))
                else:
                    pe.wait_ge(ctx_made.sem, ctx_made.at(b, PAIRS))
                src = x if kind == "X" else cx
                for f in range(KD):
                    mm = pe.transpose(out[:, f * P:(f + 1) * P], src[:, t, f * P:(f + 1) * P], identf[:])
                mm.then_inc(banks.is_filled(where, (kind, 0, t, 0)), 1)

            def part(region, where, b0):
                for pos, step in enumerate(region[0]):
                    if step is not None:
                        bs, s, i = step
                        b = b0 + bs
                        exp_scores(b, s, i)
                        if i == TRANSPOSE_AT and (after := following(region, b, s, 1)) is not None:
                            max_transposes(*after)
                        ahead, ks = MAXIMA_AT[i]
                        if (after := following(region, b, s, ahead)) is not None:
                            if 0 in ks and after[1] % STEPS == 0:
                                banks.all_emptied(pe, where, [("T", unit(after[1]), t, p)
                                                              for t in range(NT) for p in range(TPARTS)])
                            for k in ks:
                                max_scores(*after, k)
                        if i == VALUES_AT and (before := preceding(region, b, s, 1)) is not None:
                            values(*before, following(region, b, s, 1) is not None)
                    for kind, bb, u, t in table.started(region, pos, 0, "X", "C", "P", "O"):
                        bt = b0 + bb
                        if kind in "XC":
                            transposes(where, bt, kind, t)
                        elif kind == "P":
                            out = banks.take(pe, where, ("P", u, t, 0))
                            if u == 0:
                                if region is table.head and t == 0:
                                    pe.wait_ge(w_lo_made, KD)
                                    if biased:
                                        pe.wait_ge(extra_made, 1)
                                banks.all_emptied(pe, where, [("X", 0, t, 0)], take=("P", u, t, 0))
                            project(out[:, 0:NU], xt, t, u * NU, NU, u)\
                                .then_inc(banks.is_filled(where, ("P", u, t, 0)), 1)
                        else:
                            out = banks.take(pe, where, ("O", 0, t, 0))
                            banks.all_emptied(pe, where, [("C", 0, t, 0)], take=("O", 0, t, 0))
                            project(out, ct, t, OO, D, units)\
                                .then_inc(banks.is_filled(where, ("O", 0, t, 0)), 1)
                    for bb, u, t, p in table.turned(region, pos):
                        if p == 0:
                            k = u * NT + t
                            pe.wait_ge(replicated.sem, replicated.at(b0 + bb, k + 1))
                            pe.wait_ge(low_made.sem, low_made.at(b0 + bb, k + 1))
                        out = banks.take(pe, where, ("T", u, t, p)).bitcast(BF16)
                        for h in range(min(8, NST - 8 * p)):
                            src = staged[:, t, 8 * p + h].rearrange("p s d -> p (s d)")
                            mm = pe.transpose(out[0:STK, h * P:(h + 1) * P], src, identb[:])
                        mm.then_inc(banks.is_filled(where, ("T", u, t, p)), 1)
                    if step is None:
                        if region is table.head and region[0][pos + 1] is not None:
                            banks.all_emptied(pe, where, [("T", 0, t, p)
                                                          for t in range(NT) for p in range(TPARTS)])
                            for k in range(6):
                                max_scores(0, 0, k)
                            max_transposes(0, 0)
                            for k in range(FIRST):
                                max_scores(0, 1, k)
                        if region is table.tail and region[0][pos - 1] is not None:
                            values(b0, PAIRS - 1, False)

            whole(pe, part)


def ffn(nc, phase, name, consts, x_dram, y_dram, gate_dram, up_dram, down_dram, scales_dram, dscale_dram, xa_dram,
        gb_dram, ub_dram, da_dram, db_dram):
    identf = consts[0]
    uses = ["A"]
    for n in range(NI):
        uses += [f"G{n}", f"U{n}"]
    uses += ["Y0", "DA"] + [f"Y{t}" for t in range(1, NT)]
    HI, LO = 0, 1
    RAWS = 3

    with ExitStack() as ctx:
        sb = lambda n, s, d: ctx.enter_context(nc.sbuf_tensor(f"{name}_{n}", s, d))
        sem = lambda n: phase.semaphore(f"{name}_{n}")
        ring = Ring(ctx, phase, nc, name, uses, 3, 2 * T)
        norm = Norm(ctx, phase, nc, name, identf, x_dram)
        xt = norm.xt
        codes = sb("codes", [P, 2, KD, INTER], F32R)
        dcodes = sb("dcodes", [P, NI, D], F32R)
        raw = sb("raw", [P, RAWS, INTER], I32)
        res = raw[:].rearrange("p i n -> p (i n)").bitcast(F32)[:, 0:NT * D]
        res = res.rearrange("p (t d) -> p t d", t=NT)
        scales = sb("scales", [P, 2, NI], F32)
        dscale = sb("dscale", [P, D], F32)
        xa_raw = sb("xa_raw", [P, KD * 2 * RANK], F32)
        xa = sb("xa", [P, 2, KD, 2 * RANK], F32R)
        da_raw = sb("da_raw", [P, NI * RANK], F32)
        da = sb("da", [P, 2, NI, RANK], F32R)
        lr_b = [sb(f"{k}_b", [3 * RANK, c], F32R) for k, c in (("gate", INTER), ("up", INTER), ("down", D))]
        lr_x = [sb(f"{k}_x", [3 * RANK, T], F32R) for k in ("gate", "up", "down")]
        ht = sb("ht", [P, 2, NI, T], F32R)
        work = sb("work", [P, 11 * T], F32)
        gate = work[:, 0:T]
        scaled, sig, upv, hid, ysum = (
            work[:, (2 * i + 1) * T:(2 * i + 3) * T].rearrange("p (a t) -> p a t", a=2) for i in range(5))

        raw_loaded = [sem(f"raw{i}_loaded") for i in range(RAWS)]
        res_loaded = [Signal(sem(f"res{t}_loaded"), 16) for t in range(NT)]
        stored = [Signal(sem(f"y{t}_stored"), 16, 16) for t in range(NT)]
        raw_used = sem("raw_used")
        small_loaded = sem("small_loaded")
        b_loaded = sem("b_loaded")
        small_hi = sem("small_hi")
        small_made = sem("small_made")
        b_scaled, b_hi, b_made = sem("b_scaled"), sem("b_hi"), sem("b_made")
        cleared = sem("cleared")
        lrx_hi = Signal(sem("lowrank_hi"), 2)
        p1_scaled = Signal(sem("scaled"), 2 * NI)
        silu_made = Signal(sem("silu_made"), NI)
        hid_made = Signal(sem("hid_made"), NI)
        hid_hi = Signal(sem("hid_hi"), NI)
        hid_lo = Signal(sem("hid_lo"), NI, 2)
        y_part = Signal(sem("y_part"), 2 * NT)

        def rows(n):
            return P if n < NI - 1 else LAST

        def lr_raw(j):
            return work[0:3 * RANK, (0, INTER, 2 * INTER)[j]:(INTER, 2 * INTER, 2 * INTER + D)[j]]

        early_chunks = [(codes[:, j, f, :], src[:, f, :]) for f in range(KD)
                        for j, src in ((0, gate_dram), (1, up_dram))]
        chunks = early_chunks + [(dcodes[:, n:min(n + 2, NI), :].rearrange("p n d -> p (n d)"),
                                  down_dram[:, n * D:min(n + 2, NI) * D]) for n in range(0, NI, 2)]

        def raw_chunk(i):
            return raw[:, i % RAWS, 0:chunks[i][1].shape[1]]

        X_LO = (1, 2, 1)
        B_LO = (2, 1, 2)

        STATS_AT, NORMALISE_AT = 1, 6

        block = ctx.enter_context(nc.Block())

        @block.sync
        def _(sp):
            for t in range(NT):
                sp.sem_inc(stored[t].sem, 16)
                norm.load(sp, 0, t, first=True)
            sp.dma_start(scales[:].rearrange("p a n -> p (a n)"), scales_dram).then_inc(small_loaded, 16)
            sp.dma_start(dscale[:], dscale_dram.broadcast_to([P, D])).then_inc(small_loaded, 16)
            sp.dma_start(xa_raw[:], xa_dram).then_inc(small_loaded, 16)
            sp.dma_start(da_raw[:], da_dram).then_inc(small_loaded, 16)
            for r in range(3):
                q = slice(r * RANK, (r + 1) * RANK)
                for j, (d, c2) in enumerate(((gb_dram, INTER), (ub_dram, INTER), (db_dram, D))):
                    sp.dma_start(lr_raw(j)[q, 0:c2], d).then_inc(b_loaded, 16)
            for i, (_, src) in enumerate(chunks):
                if i >= RAWS:
                    sp.wait_ge(raw_used, i - RAWS + 1)
                sp.dma_start(raw_chunk(i), src).then_inc(raw_loaded[i % RAWS], 16)
            sp.wait_ge(raw_used, len(chunks))

            def batch(b, ahead):
                if ahead:
                    for t in range(NT):
                        norm.load(sp, b + 1, t)
                for t in range(NT):
                    sp.wait_ge(stored[t].sem, stored[t].at(b, 0))
                    sp.dma_start(res[:, t, :], x_dram[b, t]).then_inc(res_loaded[t].sem, 16)
                for t in range(NT):
                    ring.emptied(sp, b, f"Y{t}")
                    sp.dma_start(y_dram[b, t], res[:, t, :]).then_inc(stored[t].sem, 16)

            with sp.Fori(0, BATCH - 1) as b:
                batch(b, True)
            batch(BATCH - 1, False)
            for t in range(NT):
                sp.wait_ge(stored[t].sem, stored[t].at(BATCH, 0))

        @block.gpsimd
        def _(pool):
            for t in range(NT):
                norm.root(pool, 0, t)

            def batch(b, ahead):
                for n in range(NI):
                    r = rows(n)
                    pool.wait_ge(hid_hi.sem, hid_hi.at(b, n + 1))
                    pool.tensor_tensor(ht[0:r, LO, n, :], hid[0:r, n % 2, :], ht[0:r, HI, n, :].bitcast(F32),
                                       ALU.subtract).then_inc(hid_lo.sem, 1)
                    if ahead and STATS_AT <= n < STATS_AT + NT:
                        norm.root(pool, b + 1, n - STATS_AT)

            with pool.Fori(0, BATCH - 1) as b:
                batch(b, True)
            batch(BATCH - 1, False)

        @block.scalar
        def _(act):
            ring.give_credits(act)
            norm.ring.give_credits(act)
            for t in range(NT):
                norm.split_hi(act, 0, t)
            act.sem_inc(hid_lo.sem, 2)
            act.wait_ge(small_loaded, 64)
            act.copy(xa[:, HI].rearrange("p f r -> p (f r)"), xa_raw[:])
            act.copy(da[:, HI].rearrange("p f r -> p (f r)"), da_raw[:]).then_inc(small_hi, 1)
            act.wait_ge(b_scaled, 3)
            for j in range(3):
                c = lr_b[j].shape[1]
                act.copy(lr_b[j][:], lr_raw(j)[:, 0:c]).then_inc(b_hi, 1)

            def batch(b, ahead):
                def lowrank_hi(use, j, q):
                    src = ring.read(act, b, use)[q * RANK:(q + 1) * RANK, 0:T]
                    for r in range(3):
                        if r != X_LO[j]:
                            last = act.copy(lr_x[j][r * RANK:(r + 1) * RANK, :], src)
                    return last

                lowrank_hi("A", 0, 0)
                lowrank_hi("A", 1, 1).then_inc(lrx_hi.sem, 1)

                def scale(n, j):
                    r = rows(n)
                    src = ring.read(act, b, f"{'GU'[j]}{n}")[0:r, 0:T]
                    if n >= 1:
                        ring.emptied(act, b, f"{'GU'[j]}{n - 1}")
                    act.activation(scaled[0:r, j, :], src, ACT.Identity, scale=scales[0:r, j, n:n + 1])\
                       .then_inc(p1_scaled.sem, 1)

                def silu(n):
                    r = rows(n)
                    ring.emptied(act, b, f"G{n}")
                    act.activation(sig[0:r, n % 2, :], gate[0:r, :], ACT.Silu).then_inc(silu_made.sem, 1)

                def hidden_hi(n):
                    r = rows(n)
                    act.wait_ge(hid_made.sem, hid_made.at(b, n + 1))
                    act.copy(ht[0:r, HI, n, :], hid[0:r, n % 2, :]).then_inc(hid_hi.sem, 1)

                for n in range(NI + 1):
                    if n < NI:
                        scale(n, 0)
                        scale(n, 1)
                        silu(n)
                    if n >= 1:
                        hidden_hi(n - 1)
                if ahead:
                    norm.split_hi(act, b + 1, 0)
                    norm.split_hi(act, b + 1, 1)
                lowrank_hi("DA", 2, 0).then_inc(lrx_hi.sem, 1)
                if ahead:
                    norm.split_hi(act, b + 1, 2)
                    norm.split_hi(act, b + 1, 3)

            with act.Fori(0, BATCH - 1) as b:
                batch(b, True)
            batch(BATCH - 1, False)

        @block.vector
        def _(dve):
            norm.setup(dve)
            for t in range(NT + 1):
                if t < NT:
                    norm.statistics(dve, 0, t)
                if t >= 1:
                    norm.normalise(dve, 0, t - 1)
                    if t >= 2:
                        norm.split_lo(dve, 0, t - 2)
            norm.split_lo(dve, 0, NT - 1)
            dve.wait_ge(b_loaded, 9 * 16)
            for j in range(3):
                c = lr_b[j].shape[1]
                dve.tensor_scalar(lr_raw(j)[:, 0:c], lr_raw(j)[:, 0:c], LR_SCALE, None, ALU.mult)\
                   .then_inc(b_scaled, 1)
            dve.wait_ge(small_hi, 1)
            dve.tensor_tensor(xa[:, LO].rearrange("p f r -> p (f r)"), xa_raw[:],
                              xa[:, HI].rearrange("p f r -> p (f r)").bitcast(F32), ALU.subtract)
            dve.tensor_tensor(da[:, LO].rearrange("p f r -> p (f r)"), da_raw[:],
                              da[:, HI].rearrange("p f r -> p (f r)").bitcast(F32), ALU.subtract)
            dve.tensor_scalar(scales[:], scales[:], Q_STEP, None, ALU.mult)
            dve.tensor_scalar(dscale[:], dscale[:], Q_STEP, None, ALU.mult).then_inc(small_made, 1)
            for j in range(3):
                c = lr_b[j].shape[1]
                q = slice(B_LO[j] * RANK, (B_LO[j] + 1) * RANK)
                dve.wait_ge(b_hi, j + 1)
                dve.tensor_tensor(lr_b[j][q, :], lr_raw(j)[q, 0:c], lr_b[j][q, :].bitcast(F32),
                                  ALU.subtract).then_inc(b_made, 1)
            for i, (dst, _) in enumerate(chunks):
                dve.wait_ge(raw_loaded[i % RAWS], 16 * (i // RAWS + 1))
                dve.tensor_scalar(dst, raw_chunk(i), -Q_ZERO, None, ALU.add).then_inc(raw_used, 1)

            def batch(b, ahead):
                def lowrank_lo(use, j, q):
                    src = ring.read(dve, b, use)[q * RANK:(q + 1) * RANK, 0:T]
                    hi = q * RANK
                    return dve.tensor_tensor(lr_x[j][X_LO[j] * RANK:(X_LO[j] + 1) * RANK, :], src,
                                             lr_x[j][hi:hi + RANK, :].bitcast(F32), ALU.subtract)

                dve.wait_ge(lrx_hi.sem, lrx_hi.at(b, 1))
                lowrank_lo("A", 0, 0)
                lowrank_lo("A", 1, 1).then_inc(ring.is_free("A"), 1)

                def add_lowrank(n, j):
                    r = rows(n)
                    src = ring.read(dve, b, f"{'GU'[j]}{n}")[0:r, T:2 * T]
                    dve.wait_ge(p1_scaled.sem, p1_scaled.at(b, 2 * n + j + 1))
                    if j == 0 and n >= 1:
                        dve.wait_ge(silu_made.sem, silu_made.at(b, n))
                    dst = gate[0:r, :] if j == 0 else upv[0:r, n % 2, :]
                    dve.tensor_tensor(dst, src, scaled[0:r, j, :], ALU.add)\
                       .then_inc(ring.is_free(f"{'GU'[j]}{n}"), 1)

                def hidden(n):
                    r = rows(n)
                    dve.wait_ge(silu_made.sem, silu_made.at(b, n + 1))
                    ring.emptied(dve, b, f"U{n}")
                    dve.wait_ge(hid_lo.sem, hid_lo.at(b, n - 1))
                    dve.tensor_tensor(hid[0:r, n % 2, :], sig[0:r, n % 2, :], upv[0:r, n % 2, :], ALU.mult)\
                       .then_inc(hid_made.sem, 1)

                for n in range(NI + 1):
                    if n < NI:
                        add_lowrank(n, 0)
                        add_lowrank(n, 1)
                    if n >= 1:
                        hidden(n - 1)
                    if ahead and STATS_AT <= n < STATS_AT + NT:
                        norm.statistics(dve, b + 1, n - STATS_AT)
                    if ahead and NORMALISE_AT <= n < NORMALISE_AT + 2:
                        norm.normalise(dve, b + 1, n - NORMALISE_AT)
                if ahead:
                    for t in (0, 1):
                        norm.split_lo(dve, b + 1, t)
                        norm.normalise(dve, b + 1, t + 2)
                dve.wait_ge(lrx_hi.sem, lrx_hi.at(b, 2))
                lowrank_lo("DA", 2, 0).then_inc(ring.is_free("DA"), 1)
                if ahead:
                    norm.split_lo(dve, b + 1, 2)
                    norm.split_lo(dve, b + 1, 3)
                for t in range(NT):
                    y = ring.read(dve, b, f"Y{t}")
                    dve.tensor_tensor(ysum[:, t % 2, :], y[:, 0:D], dscale[:], ALU.mult)\
                       .then_inc(y_part.sem, 1)
                    dve.wait_ge(y_part.sem, y_part.at(b, 2 * t + 1))
                    dve.wait_ge(res_loaded[t].sem, res_loaded[t].at(b, 16))
                    dve.tensor_tensor(res[:, t, :], ysum[:, t % 2, :], res[:, t, :], ALU.add)\
                       .then_inc(y_part.sem, 1)
                    dve.wait_ge(y_part.sem, y_part.at(b, 2 * t + 2))
                    dve.tensor_tensor(res[:, t, :], y[:, D:2 * D], res[:, t, :], ALU.add)\
                       .then_inc(ring.is_free(f"Y{t}"), 1)

            with dve.Fori(0, BATCH - 1) as b:
                batch(b, True)
            batch(BATCH - 1, False)

        @block.tensor
        def _(pe):
            THREE = ((HI, HI), (LO, HI), (HI, LO))
            for t in range(NT):
                norm.transpose(pe, 0, t)
            pe.wait_ge(small_made, 1)

            def batch(b, ahead):
                out = ring.take(pe, b, "A")
                for t in (2, 3):
                    norm.ring.emptied(pe, b, f"X{t}")
                passes(pe, out[0:2 * RANK, 0:T], [(xa[:, a, f, :], xt[:, c, f, :])
                                                  for f in range(KD) for a, c in THREE])\
                    .then_inc(ring.is_filled("A"), 1)
                pe.wait_ge(raw_used, len(early_chunks))
                pe.wait_ge(b_made, 3)
                for n in range(NI):
                    r = rows(n)
                    cols = slice(n * P, n * P + r)
                    for j in range(2):
                        out = ring.take(pe, b, f"{'GU'[j]}{n}")
                        passes(pe, out[0:r, 0:T], [(codes[:, j, f, cols], xt[:, c, f, :])
                                                   for f in range(KD) for c in (HI, LO)])
                        if n == 0 and j == 0:
                            ring.emptied(pe, b, "A")
                        passes(pe, out[0:r, T:2 * T], [(lr_b[j][:, cols], lr_x[j][:])])\
                            .then_inc(ring.is_filled(f"{'GU'[j]}{n}"), 1)

                def down(out, t, ks):
                    tok = slice(t * P, (t + 1) * P)
                    for n in ks:
                        if t == 0:
                            pe.wait_ge(hid_lo.sem, hid_lo.at(b, n + 1))
                        r = rows(n)
                        passes(pe, out[:, 0:D], [(ht[0:r, c, n, tok], dcodes[0:r, n, :]) for c in (HI, LO)],
                               start=n == 0, stop=n == NI - 1)

                def down_lowrank(out, t):
                    passes(pe, out[:, D:2 * D], [(lr_x[2][:, t * P:(t + 1) * P], lr_b[2][:])])\
                        .then_inc(ring.is_filled(f"Y{t}"), 1)

                if ahead:
                    norm.transpose(pe, b + 1, 0)
                    norm.transpose(pe, b + 1, 1)
                pe.wait_ge(raw_used, len(chunks))
                y0 = ring.take(pe, b, "Y0")
                down(y0, 0, range(NI))
                if ahead:
                    norm.transpose(pe, b + 1, 2)
                    norm.transpose(pe, b + 1, 3)
                out = ring.take(pe, b, "DA")
                passes(pe, out[0:RANK, 0:T], [(da[0:rows(n), a, n, :], ht[0:rows(n), c, n, :])
                                              for n in range(NI) for a, c in THREE])\
                    .then_inc(ring.is_filled("DA"), 1)
                y1 = ring.take(pe, b, "Y1")
                down(y1, 1, range(NI))
                ring.emptied(pe, b, "DA")
                down_lowrank(y0, 0)
                down_lowrank(y1, 1)
                for t in range(2, NT):
                    out = ring.take(pe, b, f"Y{t}")
                    down(out, t, range(NI))
                    down_lowrank(out, t)

            with pe.Fori(0, BATCH - 1) as b:
                batch(b, True)
            batch(BATCH - 1, False)


def program(nc, d):
    with ExitStack() as ctx:
        mid = [nc.dram_tensor(f"mid{i}", (BATCH, NT, P, D), F32, kind="Internal").ap() for i in range(3)]
        consts = constants(ctx, nc)
        feed = [d[n] for n in ("gate_q", "up_q", "down_q", "scales", "dscale", "xa", "gb", "ub", "da", "db")]
        with Phase(nc) as phase:
            attention(nc, phase, "aa", consts, d["x"], mid[0], d["wa"], KV_GQA, UNITS_A, PLAN_A, HEAD_A,
                      rope_dram=d["trig"])
        with Phase(nc) as phase:
            ffn(nc, phase, "f1", consts, mid[0], mid[1], *feed)
        with Phase(nc) as phase:
            attention(nc, phase, "ab", consts, mid[1], mid[2], d["wb"], HEADS, UNITS_B, PLAN_B, HEAD_B,
                      bias_dram=d["bias"], biassel_dram=d["biassel"])
        with Phase(nc) as phase:
            ffn(nc, phase, "f2", consts, mid[2], d["y"], *feed)


def timed(*tasks):
    plan = {}
    for j, kind, bb, u, t in tasks:
        plan.setdefault(j, []).append((kind, bb, u, t))
    return plan


UNITS_A, UNITS_B = 2, 4
OUTPUT = [(j, "C", -1, 0, t) for t, j in enumerate((5, 6, 7, 8))]
PLAN_A = timed(
    *[(j, "P", 0, 1, t) for t, j in enumerate((4, 10, 15, 20))], *OUTPUT,
    *[(j, "T", 0, 1, t) for t, j in enumerate((11, 17, 22, 27))],
    *[(j, "O", -1, 0, t) for t, j in enumerate((14, 19, 24, 29))],
    *[(j, "X", 1, 0, t) for t, j in enumerate((43, 44, 45, 46))],
    *[(j, "P", 1, 0, t) for t, j in enumerate((48, 52, 56, 60))],
    *[(j, "T", 1, 0, t) for t, j in enumerate((54, 58, 62, 66))],
)
PLAN_B = timed(
    *[(20 * (u - 1) + j, "P", 0, u, t) for u in range(1, 4) for t, j in enumerate((4, 5, 6, 7))],
    *OUTPUT,
    *[(20 * (u - 1) + j, "T", 0, u, t) for u in range(1, 4) for t, j in enumerate((8, 9, 10, 11))],
    *[(j, "O", -1, 0, t) for t, j in enumerate((13, 14, 15, 16))],
    *[(j, "X", 1, 0, t) for t, j in enumerate((53, 54, 55, 56))],
    *[(60 + j, "P", 1, 0, t) for t, j in enumerate((4, 5, 6, 7))],
    *[(60 + j, "T", 1, 0, t) for t, j in enumerate((8, 9, 10, 11))],
)
HEAD_A = HEAD_B = timed(
    *[(3 + t, "X", 0, 0, t) for t in range(NT)],
    *[(7 + 2 * t, "P", 0, 0, t) for t in range(NT)],
    *[(14 + 2 * t, "T", 0, 0, t) for t in range(NT)],
)


def kernel(**inputs):
    import concourse.bacc as bacc
    from concourse.bass_utils import run_bass_kernel_spmd

    a = {k.removeprefix("L0_"): np.asarray(v) for k, v in inputs.items()}

    def by_feature(w):
        n = -(-w.shape[0] // P)
        w = np.pad(w, ((0, n * P - w.shape[0]), (0, 0)))
        return np.ascontiguousarray(w.reshape(n, P, -1).transpose(1, 0, 2))

    inv = (1.0 / np.float32(ROPE_BASE) ** (np.arange(0, HD, 2, dtype=np.float32) / np.float32(HD)))
    freqs = np.arange(T, dtype=np.float32)[:, None] * inv.astype(np.float32)[None]
    cos, sin = np.cos(freqs).astype(np.float32), np.sin(freqs).astype(np.float32)
    trig = np.stack([np.concatenate([cos, cos], 1), np.concatenate([-sin, sin], 1)], 1)
    trig = trig.reshape(NT, P, 2 * HD).transpose(1, 0, 2).reshape(P, -1)
    n_rows = UNITS_B + 1
    biassel = np.zeros((P, n_rows * P + 1), np.float32)
    for j in range(n_rows):
        biassel[2 * j:2 * j + 2, j * P:(j + 1) * P] = 1.0
    biassel[1:2 * n_rows:2, -1] = -1.0

    def by_unit(q, k, v, units):
        parts = [np.split(m, units, axis=-1) for m in (q, k, v)]
        return [m[u] for u in range(units) for m in parts]

    wa = [a[f"attn_a_W{k}"] for k in "qkvo"]
    wb = [a[f"attn_b_W{k}"].T for k in "qkvo"]
    bias = by_unit(*[a[f"attn_b_b{k}"] for k in "qkv"], UNITS_B)
    bias = [np.pad(np.concatenate(bias[3 * u:3 * u + 3]), (0, D - 3 * D // UNITS_B)) for u in range(UNITS_B)]
    arrays = {
        "x": a["attn_a_x"].reshape(BATCH, NT, P, D),
        "wa": by_feature(np.concatenate(by_unit(*wa[:3], UNITS_A) + [wa[3]], 1)),
        "wb": by_feature(np.concatenate(by_unit(*wb[:3], UNITS_B) + [wb[3]], 1)),
        "trig": trig,
        "bias": np.repeat(np.stack(bias + [a["attn_b_bo"]]), 2, axis=0),
        "biassel": biassel,
        "gate_q": by_feature(a["ffn_gate_q"].T),
        "up_q": by_feature(a["ffn_up_q"].T),
        "down_q": by_feature(a["ffn_down_q"].T).reshape(P, -1),
        "scales": np.concatenate([by_feature(a[f"ffn_{k}_scale"][:, None])[:, :, 0]
                                  for k in ("gate", "up")], 1),
        "dscale": a["ffn_down_scale"].reshape(1, D),
        "xa": by_feature(np.concatenate([a["ffn_gate_A"], a["ffn_up_A"]], 1)).reshape(P, -1),
        "gb": a["ffn_gate_B"],
        "ub": a["ffn_up_B"],
        "da": by_feature(a["ffn_down_A"]).reshape(P, -1),
        "db": a["ffn_down_B"],
    }
    nc = bacc.Bacc("TRN2", target_bir_lowering=False, num_devices=1)
    feed, d = {}, {}
    for key, v in arrays.items():
        v = np.ascontiguousarray(v)
        feed[f"in_{key}"] = v
        d[key] = nc.dram_tensor(f"in_{key}", v.shape, mybir.dt.from_np(v.dtype), kind="ExternalInput").ap()
    d["y"] = nc.dram_tensor("out_y", (BATCH, NT, P, D), F32, kind="ExternalOutput").ap()
    program(nc, d)
    r = run_bass_kernel_spmd(nc, [feed], core_ids=[0])
    return r.results[0]["out_y"].reshape(BATCH, T, D)
```
